# Optimizing a Trainium2 kernel written in Bass

```python
import numpy as np
import jax
import jax.numpy as jnp

def _softmax(x, axis=-1):
    return jax.nn.softmax(x, axis=axis)

def _gelu(x):
    return jax.nn.gelu(x, approximate=True)

def _silu(x):
    return jax.nn.silu(x)

def _sigmoid(x):
    return jax.nn.sigmoid(x)

def _layernorm(x, axis=-1, eps=1e-05):
    m = jnp.mean(x, axis=axis, keepdims=True)
    v = jnp.var(x, axis=axis, keepdims=True)
    return (x - m) / jnp.sqrt(v + eps)

def _scatter_add(tgt, idx, src, axis=0):
    return tgt.at[idx].add(src)

def _segment_sum(src, seg, n):
    return jax.ops.segment_sum(src, seg, n)
kernel_name = 'mk_early_fusion_embed_d2_tok_img768_r4_225593'

def setup_inputs(seed: int=0):
    np.random.seed(seed)
    _w = jnp.asarray

    def _rec_inputs():
        import jax
        import jax.numpy as jnp
        _rk = jax.random.key(seed)
        x = -9.30917e-05 + 1.0002 * jax.random.normal(jax.random.fold_in(_rk, 1), (32, 3, 64, 64), jnp.float32)
        x_txt = jax.random.randint(jax.random.fold_in(_rk, 51), (32, 32), 0, 127999, jnp.int32)
        return (x, x_txt)
    x, x_txt = _rec_inputs()

    def _L0_tok_setup():
        import jax, jax.numpy as jnp
        import numpy as np
        PATCH = 16
        EPS = 1e-05

        def _shift(x, dy, dx):
            H, W = (x.shape[2], x.shape[3])
            if dy > 0:
                x = jnp.pad(x, ((0, 0), (0, 0), (dy, 0), (0, 0)))[:, :, :H, :]
            elif dy < 0:
                x = jnp.pad(x, ((0, 0), (0, 0), (0, -dy), (0, 0)))[:, :, -H:, :]
            if dx > 0:
                x = jnp.pad(x, ((0, 0), (0, 0), (0, 0), (dx, 0)))[:, :, :, :W]
            elif dx < 0:
                x = jnp.pad(x, ((0, 0), (0, 0), (0, 0), (0, -dx)))[:, :, :, -W:]
            return x

        def _patchify(x, p):
            B, C, H, W = x.shape
            gh, gw = (H // p, W // p)
            x = x.reshape(B, C, gh, p, gw, p).transpose(0, 2, 4, 1, 3, 5)
            return x.reshape(B, gh * gw, C * p * p)
        key = jax.random.key(seed)
        ks = jax.random.split(key, 3)
        B, C, H, W = (32, 3, 224, 224)
        patch_dim = 5 * C * PATCH * PATCH
        embed_dim = 192
        hidden = 2 * embed_dim
        x = jax.random.normal(ks[0], (B, C, H, W), dtype=jnp.float32)
        W1 = jax.random.normal(ks[1], (patch_dim, hidden), dtype=jnp.float32) * (1.0 / np.sqrt(patch_dim))
        W2 = jax.random.normal(ks[2], (hidden, embed_dim), dtype=jnp.float32) * (1.0 / np.sqrt(hidden))
        return {'x': x, 'gamma': jnp.ones((patch_dim,), jnp.float32), 'beta': jnp.zeros((patch_dim,), jnp.float32), 'W1': W1, 'b1': jnp.zeros((hidden,), jnp.float32), 'W2': W2, 'b2': jnp.zeros((embed_dim,), jnp.float32)}
    _L0_tok_all = _L0_tok_setup()
    _L0_tok_in = {k: v for k, v in _L0_tok_all.items() if k in ('gamma', 'beta', 'W1', 'b1', 'W2', 'b2')}
    del _L0_tok_all

    def _L0_txt_setup():
        import jax, jax.numpy as jnp
        import numpy as np
        import math
        VOCAB = 32000
        BASIN_DIM = 64
        D_MODEL = 192
        EPS = 1e-08
        key = jax.random.key(seed)
        k1, k2, k3, k4 = jax.random.split(key, 4)
        token_ids = jax.random.randint(k1, (8, 1024), 0, VOCAB, dtype=jnp.int32)
        coords = jax.random.normal(k2, (VOCAB, BASIN_DIM), dtype=jnp.float32)
        coords = coords / jnp.linalg.norm(coords, axis=-1, keepdims=True)
        coords = coords * (math.sqrt(BASIN_DIM) / 5.0)
        coords = coords + jax.random.normal(k3, coords.shape, dtype=jnp.float32) * 0.01
        w = jax.random.normal(k4, (D_MODEL, BASIN_DIM), dtype=jnp.float32)
        q, _ = jnp.linalg.qr(w)
        proj_w = q * 0.1
        norm_w = jnp.ones((D_MODEL,), dtype=jnp.float32)
        return {'token_ids': token_ids, 'basin_coords': coords, 'proj_w': proj_w, 'norm_w': norm_w}
    _L0_txt_all = _L0_txt_setup()
    _L0_txt_in = {k: v for k, v in _L0_txt_all.items() if k in ('basin_coords', 'proj_w', 'norm_w')}
    del _L0_txt_all

    def _L0_attn_setup():
        import jax, jax.numpy as jnp
        import numpy as np
        B, N, C, H = (4, 256, 192, 12)
        D = C // H
        EPS_BN = 1e-05
        key = jax.random.key(seed)
        ks = jax.random.split(key, 8)
        s = np.float32(D ** (-0.5))
        return {'x': jax.random.normal(ks[0], (B, N, C), dtype=jnp.float32), 'qkv_w': jax.random.normal(ks[1], (3 * C, C), dtype=jnp.float32) * C ** (-0.5), 'qkv_b': jnp.zeros((3 * C,), dtype=jnp.float32), 'proj_w': jax.random.normal(ks[2], (C, C), dtype=jnp.float32) * C ** (-0.5), 'proj_b': jnp.zeros((C,), dtype=jnp.float32), 'scale': jnp.asarray(s), 'riem_scale': jnp.asarray(s), 'grass_scale': jnp.asarray(s), 'conv_w': jax.random.normal(ks[3], (H, 3 * H), dtype=jnp.float32) * (3 * H) ** (-0.5), 'conv_b': jnp.zeros((H,), dtype=jnp.float32), 'bn_gamma': jnp.ones((H,), dtype=jnp.float32), 'bn_beta': jnp.zeros((H,), dtype=jnp.float32), 'bn_mean': jnp.zeros((H,), dtype=jnp.float32), 'bn_var': jnp.ones((H,), dtype=jnp.float32)}
    _L0_attn_all = _L0_attn_setup()
    _L0_attn_in = {k: v for k, v in _L0_attn_all.items() if k in ('qkv_w', 'qkv_b', 'proj_w', 'proj_b', 'scale', 'riem_scale', 'grass_scale', 'conv_w', 'conv_b', 'bn_gamma', 'bn_beta', 'bn_mean', 'bn_var')}
    del _L0_attn_all

    def _L0_ffn_setup():
        import jax, jax.numpy as jnp
        import numpy as np
        B, S, D = (2, 256, 192)
        NF, NR, R, DS, K = (128, 128, 128, 64, 4)

        @jax.checkpoint
        def feature_fn(x, neurons, weights):
            all_h = jnp.einsum('bsd,ndr->bsnr', x, neurons)
            return jnp.einsum('bsnr,bsn->bsr', all_h, weights)

        @jax.checkpoint
        def restore_fn(h, neurons, weights):
            all_out = jnp.einsum('bsr,nrd->bsnd', h, neurons)
            return jnp.einsum('bsnd,bsn->bsd', all_out, weights)

        def topk_sparsify(weights, k):
            topk_vals, topk_idx = jax.lax.top_k(weights, k)
            N = weights.shape[-1]
            one_hot_mask = jax.nn.one_hot(topk_idx, N, dtype=weights.dtype)
            sparse = (one_hot_mask * topk_vals[..., jnp.newaxis]).sum(axis=-2)
            sparse = sparse / (sparse.sum(axis=-1, keepdims=True) + 1e-08)
            return (sparse, topk_idx)
        key = jax.random.key(seed)
        ks = jax.random.split(key, 8)
        x = jax.random.normal(ks[0], (B, S, D), jnp.float32)
        f_know = jax.random.normal(ks[1], (NF, D, R), jnp.float32) * 0.02
        r_know = jax.random.normal(ks[2], (NR, R, D), jnp.float32) * 0.02
        W_fk = jax.random.normal(ks[3], (D, DS), jnp.float32) * 0.02
        b_fk = jnp.zeros((DS,), jnp.float32)
        W_rk = jax.random.normal(ks[4], (D, DS), jnp.float32) * 0.02
        b_rk = jnp.zeros((DS,), jnp.float32)
        emb_fk = jax.random.normal(ks[5], (NF, DS), jnp.float32) * 0.02
        emb_rk = jax.random.normal(ks[6], (NR, DS), jnp.float32) * 0.02
        return {'x': x, 'f_know': f_know, 'r_know': r_know, 'W_fk': W_fk, 'b_fk': b_fk, 'W_rk': W_rk, 'b_rk': b_rk, 'emb_fk': emb_fk, 'emb_rk': emb_rk}
    _L0_ffn_all = _L0_ffn_setup()
    _L0_ffn_in = {k: v for k, v in _L0_ffn_all.items() if k in ('f_know', 'r_know', 'W_fk', 'b_fk', 'W_rk', 'b_rk', 'emb_fk', 'emb_rk')}
    del _L0_ffn_all

    def _L1_attn_setup():
        import jax, jax.numpy as jnp
        import numpy as np
        B, N, C = (64, 80, 192)
        NUM_HEADS = 12
        LENS_Z = 64
        SCALE = (C // NUM_HEADS) ** (-0.5)
        key = jax.random.key(seed)
        k1, k2, k3 = jax.random.split(key, 3)
        x = jax.random.normal(k1, (B, N, C), dtype=jnp.float32)
        proj_w = jax.random.normal(k2, (C, C), dtype=jnp.float32) * 0.02
        proj_b = jax.random.normal(k3, (C,), dtype=jnp.float32) * 0.02
        return {'x': x, 'proj_w': proj_w, 'proj_b': proj_b}
    _L1_attn_all = _L1_attn_setup()
    _L1_attn_in = {k: v for k, v in _L1_attn_all.items() if k in ('proj_w', 'proj_b')}
    del _L1_attn_all

    def _L1_ffn_setup():
        import jax, jax.numpy as jnp
        import numpy as np
        B, M, D = (32, 196, 192)
        N, P, H = (64, 1, 768)
        EPS = 1e-12

        def _l2norm(v, axis):
            n = jnp.sqrt(jnp.sum(v * v, axis=axis, keepdims=True))
            return v / jnp.maximum(n, EPS)
        key = jax.random.key(seed)
        ks = jax.random.split(key, 7)
        x = jax.random.normal(ks[0], (B, M, D), dtype=jnp.float32)
        phi = jax.random.normal(ks[1], (D, N, P), dtype=jnp.float32) * (1.0 / D ** 0.5)
        scale = jnp.ones((1,), dtype=jnp.float32)
        w1 = jax.random.normal(ks[2], (N, D, H), dtype=jnp.float32) * (1.0 / D ** 0.5)
        b1 = jnp.zeros((N, H), dtype=jnp.float32)
        w2 = jax.random.normal(ks[3], (N, H, D), dtype=jnp.float32) * (1.0 / H ** 0.5)
        b2 = jnp.zeros((N, D), dtype=jnp.float32)
        return {'x': x, 'phi': phi, 'scale': scale, 'w1': w1, 'b1': b1, 'w2': w2, 'b2': b2}
    _L1_ffn_all = _L1_ffn_setup()
    _L1_ffn_in = {k: v for k, v in _L1_ffn_all.items() if k in ('phi', 'scale', 'w1', 'b1', 'w2', 'b2')}
    del _L1_ffn_all
    return {'x': x, 'x_txt': x_txt, 'L0_tok_gamma': _L0_tok_in['gamma'], 'L0_tok_beta': _L0_tok_in['beta'], 'L0_tok_W1': _L0_tok_in['W1'], 'L0_tok_b1': _L0_tok_in['b1'], 'L0_tok_W2': _L0_tok_in['W2'], 'L0_tok_b2': _L0_tok_in['b2'], 'L0_txt_basin_coords': _L0_txt_in['basin_coords'], 'L0_txt_proj_w': _L0_txt_in['proj_w'], 'L0_txt_norm_w': _L0_txt_in['norm_w'], 'L0_attn_qkv_w': _L0_attn_in['qkv_w'], 'L0_attn_qkv_b': _L0_attn_in['qkv_b'], 'L0_attn_proj_w': _L0_attn_in['proj_w'], 'L0_attn_proj_b': _L0_attn_in['proj_b'], 'L0_attn_scale': _L0_attn_in['scale'], 'L0_attn_riem_scale': _L0_attn_in['riem_scale'], 'L0_attn_grass_scale': _L0_attn_in['grass_scale'], 'L0_attn_conv_w': _L0_attn_in['conv_w'], 'L0_attn_conv_b': _L0_attn_in['conv_b'], 'L0_attn_bn_gamma': _L0_attn_in['bn_gamma'], 'L0_attn_bn_beta': _L0_attn_in['bn_beta'], 'L0_attn_bn_mean': _L0_attn_in['bn_mean'], 'L0_attn_bn_var': _L0_attn_in['bn_var'], 'L0_ffn_f_know': _L0_ffn_in['f_know'], 'L0_ffn_r_know': _L0_ffn_in['r_know'], 'L0_ffn_W_fk': _L0_ffn_in['W_fk'], 'L0_ffn_b_fk': _L0_ffn_in['b_fk'], 'L0_ffn_W_rk': _L0_ffn_in['W_rk'], 'L0_ffn_b_rk': _L0_ffn_in['b_rk'], 'L0_ffn_emb_fk': _L0_ffn_in['emb_fk'], 'L0_ffn_emb_rk': _L0_ffn_in['emb_rk'], 'L1_attn_proj_w': _L1_attn_in['proj_w'], 'L1_attn_proj_b': _L1_attn_in['proj_b'], 'L1_ffn_phi': _L1_ffn_in['phi'], 'L1_ffn_scale': _L1_ffn_in['scale'], 'L1_ffn_w1': _L1_ffn_in['w1'], 'L1_ffn_b1': _L1_ffn_in['b1'], 'L1_ffn_w2': _L1_ffn_in['w2'], 'L1_ffn_b2': _L1_ffn_in['b2']}

def reference(x, x_txt, L0_tok_gamma, L0_tok_beta, L0_tok_W1, L0_tok_b1, L0_tok_W2, L0_tok_b2, L0_txt_basin_coords, L0_txt_proj_w, L0_txt_norm_w, L0_attn_qkv_w, L0_attn_qkv_b, L0_attn_proj_w, L0_attn_proj_b, L0_attn_scale, L0_attn_riem_scale, L0_attn_grass_scale, L0_attn_conv_w, L0_attn_conv_b, L0_attn_bn_gamma, L0_attn_bn_beta, L0_attn_bn_mean, L0_attn_bn_var, L0_ffn_f_know, L0_ffn_r_know, L0_ffn_W_fk, L0_ffn_b_fk, L0_ffn_W_rk, L0_ffn_b_rk, L0_ffn_emb_fk, L0_ffn_emb_rk, L1_attn_proj_w, L1_attn_proj_b, L1_ffn_phi, L1_ffn_scale, L1_ffn_w1, L1_ffn_b1, L1_ffn_w2, L1_ffn_b2):
    import jax
    import jax.numpy as jnp

    def _L0_tok_ref(x, gamma, beta, W1, b1, W2, b2):
        import jax, jax.numpy as jnp
        import numpy as np
        PATCH = 16
        EPS = 1e-05

        def _shift(x, dy, dx):
            H, W = (x.shape[2], x.shape[3])
            if dy > 0:
                x = jnp.pad(x, ((0, 0), (0, 0), (dy, 0), (0, 0)))[:, :, :H, :]
            elif dy < 0:
                x = jnp.pad(x, ((0, 0), (0, 0), (0, -dy), (0, 0)))[:, :, -H:, :]
            if dx > 0:
                x = jnp.pad(x, ((0, 0), (0, 0), (0, 0), (dx, 0)))[:, :, :, :W]
            elif dx < 0:
                x = jnp.pad(x, ((0, 0), (0, 0), (0, 0), (0, -dx)))[:, :, :, -W:]
            return x

        def _patchify(x, p):
            B, C, H, W = x.shape
            gh, gw = (H // p, W // p)
            x = x.reshape(B, C, gh, p, gw, p).transpose(0, 2, 4, 1, 3, 5)
            return x.reshape(B, gh * gw, C * p * p)
        p2 = PATCH // 2
        shifts = [x, _shift(x, p2, 0), _shift(x, -p2, 0), _shift(x, 0, p2), _shift(x, 0, -p2)]
        patches = jnp.concatenate([_patchify(s, PATCH) for s in shifts], axis=-1)
        mu = jnp.mean(patches, axis=-1, keepdims=True)
        var = jnp.mean(jnp.square(patches - mu), axis=-1, keepdims=True)
        h = (patches - mu) * jax.lax.rsqrt(var + EPS) * gamma + beta
        h = jax.nn.gelu(h @ W1 + b1, approximate=False)
        return h @ W2 + b2

    def _L0_txt_ref(token_ids, basin_coords, proj_w, norm_w):
        import jax, jax.numpy as jnp
        import numpy as np
        import math
        VOCAB = 32000
        BASIN_DIM = 64
        D_MODEL = 192
        EPS = 1e-08
        basin = basin_coords[token_ids]
        emb = jnp.einsum('bsk,dk->bsd', basin, proj_w)
        x_f = emb.astype(jnp.float32)
        rms = jnp.sqrt(jnp.mean(x_f * x_f, axis=-1, keepdims=True) + EPS)
        y = (x_f / rms).astype(emb.dtype)
        return y * norm_w

    def _L0_attn_ref(x, qkv_w, qkv_b, proj_w, proj_b, scale, riem_scale, grass_scale, conv_w, conv_b, bn_gamma, bn_beta, bn_mean, bn_var):
        import jax, jax.numpy as jnp
        import numpy as np
        B, N, C, H = (4, 256, 192, 12)
        D = C // H
        EPS_BN = 1e-05
        Bx, Nx, Cx = x.shape
        qkv = (x @ qkv_w.T + qkv_b).reshape(Bx, Nx, 3, H, D).transpose(2, 0, 3, 1, 4)
        q, k, v = (qkv[0], qkv[1], qkv[2])
        qgr, _ = jnp.linalg.qr(q)
        kgr, _ = jnp.linalg.qr(k)
        dots = jnp.einsum('bhnd,bhmd->bhnm', qgr, kgr)
        attn_grass = dots * dots * grass_scale
        qk = jnp.einsum('bhnd,bhmd->bhnm', q, k)
        attn = qk * scale
        qn2 = jnp.sum(q * q, axis=-1)
        kn2 = jnp.sum(k * k, axis=-1)
        d2 = qn2[..., :, None] ** 2 + kn2[..., None, :] ** 2 - 2.0 * (qk * qk)
        attn_riem = -jnp.sqrt(jnp.maximum(d2, 0.0) + 1e-08) * riem_scale
        cat = jnp.concatenate([attn, attn_riem, attn_grass], axis=1)
        y = jnp.einsum('bcnm,oc->bonm', cat, conv_w) + conv_b[None, :, None, None]
        inv = (bn_gamma / jnp.sqrt(bn_var + EPS_BN))[None, :, None, None]
        y = (y - bn_mean[None, :, None, None]) * inv + bn_beta[None, :, None, None]
        p = jax.nn.softmax(y, axis=-1)
        out = jnp.einsum('bhnm,bhmd->bhnd', p, v)
        out = out.transpose(0, 2, 1, 3).reshape(Bx, Nx, Cx)
        return out @ proj_w.T + proj_b

    def _L0_ffn_ref(x, f_know, r_know, W_fk, b_fk, W_rk, b_rk, emb_fk, emb_rk):
        import jax, jax.numpy as jnp
        import numpy as np
        B, S, D = (2, 256, 192)
        NF, NR, R, DS, K = (128, 128, 128, 64, 4)

        @jax.checkpoint
        def feature_fn(x, neurons, weights):
            all_h = jnp.einsum('bsd,ndr->bsnr', x, neurons)
            return jnp.einsum('bsnr,bsn->bsr', all_h, weights)

        @jax.checkpoint
        def restore_fn(h, neurons, weights):
            all_out = jnp.einsum('bsr,nrd->bsnd', h, neurons)
            return jnp.einsum('bsnd,bsn->bsd', all_out, weights)

        def topk_sparsify(weights, k):
            topk_vals, topk_idx = jax.lax.top_k(weights, k)
            N = weights.shape[-1]
            one_hot_mask = jax.nn.one_hot(topk_idx, N, dtype=weights.dtype)
            sparse = (one_hot_mask * topk_vals[..., jnp.newaxis]).sum(axis=-2)
            sparse = sparse / (sparse.sum(axis=-1, keepdims=True) + 1e-08)
            return (sparse, topk_idx)
        emb_fk_n = emb_fk / (jnp.linalg.norm(emb_fk, axis=-1, keepdims=True) + 1e-08)
        emb_rk_n = emb_rk / (jnp.linalg.norm(emb_rk, axis=-1, keepdims=True) + 1e-08)
        logits_fk = jnp.einsum('bsd,nd->bsn', x @ W_fk + b_fk, emb_fk_n)
        logits_rk = jnp.einsum('bsd,nd->bsn', x @ W_rk + b_rk, emb_rk_n)
        w_fk, _ = topk_sparsify(jax.nn.softmax(logits_fk, axis=-1), K)
        w_rk, _ = topk_sparsify(jax.nn.softmax(logits_rk, axis=-1), K)
        h = feature_fn(x, f_know, w_fk)
        out = restore_fn(h, r_know, w_rk)
        return out

    def _L1_attn_ref(x, proj_w, proj_b):
        import jax, jax.numpy as jnp
        import numpy as np
        B, N, C = (64, 80, 192)
        NUM_HEADS = 12
        LENS_Z = 64
        SCALE = (C // NUM_HEADS) ** (-0.5)
        q = x[:, :LENS_Z]
        k = x[:, LENS_Z:]
        v = k
        attn = jnp.einsum('bqc,bkc->bqk', q, k) * SCALE
        attn = jax.nn.softmax(attn, axis=-1)
        out = jnp.einsum('bqk,bkc->bqc', attn, v)
        out = jnp.transpose(out, (0, 2, 1)).reshape(out.shape[0], -1, C)
        out = out @ proj_w.T + proj_b
        return jnp.concatenate([out, k], axis=1)

    def _L1_ffn_ref(x, phi, scale, w1, b1, w2, b2):
        import jax, jax.numpy as jnp
        import numpy as np
        B, M, D = (32, 196, 192)
        N, P, H = (64, 1, 768)
        EPS = 1e-12

        def _l2norm(v, axis):
            n = jnp.sqrt(jnp.sum(v * v, axis=axis, keepdims=True))
            return v / jnp.maximum(n, EPS)
        xn = _l2norm(x, axis=2)
        phin = scale * _l2norm(phi, axis=0)
        logits = jnp.einsum('bmd,dnp->bmnp', xn, phin)
        d = jax.nn.softmax(logits, axis=1)
        b_, m_, n_, p_ = logits.shape
        c = jax.nn.softmax(logits.reshape(b_, m_, n_ * p_), axis=-1).reshape(b_, m_, n_, p_)
        xs = jnp.einsum('bmd,bmnp->bnpd', xn, d)
        h = jax.nn.gelu(jnp.einsum('bnpd,ndh->bnph', xs, w1) + b1[None, :, None, :], approximate=False)
        ys = jnp.einsum('bnph,nhd->bnpd', h, w2) + b2[None, :, None, :]
        y = jnp.einsum('bnpd,bmnp->bmd', ys, c)
        return y
    h = _L0_tok_ref(x, L0_tok_gamma, L0_tok_beta, L0_tok_W1, L0_tok_b1, L0_tok_W2, L0_tok_b2)
    h = jnp.concatenate([h, _L0_txt_ref(x_txt, L0_txt_basin_coords, L0_txt_proj_w, L0_txt_norm_w)], axis=1)
    h = h + _L0_attn_ref(_layernorm(h, axis=-1), L0_attn_qkv_w, L0_attn_qkv_b, L0_attn_proj_w, L0_attn_proj_b, L0_attn_scale, L0_attn_riem_scale, L0_attn_grass_scale, L0_attn_conv_w, L0_attn_conv_b, L0_attn_bn_gamma, L0_attn_bn_beta, L0_attn_bn_mean, L0_attn_bn_var)
    h = h + _L0_ffn_ref(_layernorm(h, axis=-1), L0_ffn_f_know, L0_ffn_r_know, L0_ffn_W_fk, L0_ffn_b_fk, L0_ffn_W_rk, L0_ffn_b_rk, L0_ffn_emb_fk, L0_ffn_emb_rk)
    h = h + _L1_attn_ref(_layernorm(h, axis=-1), L1_attn_proj_w, L1_attn_proj_b)
    h = h + _L1_ffn_ref(_layernorm(h, axis=-1), L1_ffn_phi, L1_ffn_scale, L1_ffn_w1, L1_ffn_b1, L1_ffn_w2, L1_ffn_b2)
    return h

_drawn_inputs = setup_inputs


def setup_inputs(seed=0):
    import zlib

    import numpy as np

    out = dict(_drawn_inputs(seed))
    spreads = {'L0_tok_gamma': (1.0, 0.2),
     'L0_tok_beta': (0.0, 0.1),
     'L0_tok_b1': (0.0, 0.1),
     'L0_tok_b2': (0.0, 0.1),
     'L0_txt_norm_w': (1.0, 0.2),
     'L0_attn_qkv_b': (0.0, 0.1),
     'L0_attn_proj_b': (0.0, 0.1),
     'L0_attn_conv_b': (0.0, 0.8),
     'L0_attn_bn_gamma': (1.0, 0.596),
     'L0_attn_bn_beta': (0.0, 0.8),
     'L0_attn_bn_mean': (0.0, 0.8),
     'L0_attn_bn_var': (1.0, 0.6),
     'L0_ffn_b_fk': (0.0, 0.8),
     'L0_ffn_b_rk': (0.0, 0.643),
     'L1_ffn_b1': (0.0, 0.8),
     'L1_ffn_b2': (0.0, 0.651)}
    factors = {'L0_ffn_f_know': 3.966,
     'L0_ffn_r_know': 3.997,
     'L0_ffn_W_fk': 3.84,
     'L0_ffn_W_rk': 4.001,
     'L0_ffn_emb_fk': 3.697,
     'L0_ffn_emb_rk': 4.279,
     'L1_attn_proj_b': 3.028,
     'L1_ffn_phi': 8.0,
     'L1_ffn_w1': 8.0,
     'L1_ffn_w2': 8.0}
    for name, (base, spread) in spreads.items():
        noise = np.random.default_rng([zlib.crc32(name.encode()), seed]).standard_normal(out[name].shape)
        drawn = base * np.exp(spread * noise) if base else spread * noise
        out[name] = jnp.asarray(drawn.astype(out[name].dtype))
    for name, factor in factors.items():
        out[name] = (out[name] * factor).astype(out[name].dtype)
    return out
```

```python
from contextlib import ExitStack

import numpy as np

import concourse.bass as bass
from concourse import mybir

F32 = mybir.dt.float32
I32 = mybir.dt.int32
U32 = mybir.dt.uint32
ALU = mybir.AluOpType
ACT = mybir.ActivationFunctionType
X = mybir.AxisListType.X

B = 32
SEQ = 48
PATCHES, TEXT = 16, 32
TOK = B * SEQ
D = 192
HALF = 96
PAIR = 2 * SEQ
PAIRS = B // 2
HEADS, HD = 12, 16
HEADS_2 = HEADS // 2
GROUPS, GH = 4, 3
HID = 384
RING = 15
KCH = 30
LN_EPS = 1e-5
VOCAB, BASIN = 32000, 64
RCH = SEQ // 8
NEUR = 128
RANK = 128
TOPK = 4
FT = TOK // 128
SLOT = 128
BLOCKS = 176
SRING = 4
UNR = 4
assert BLOCKS >= TOPK * TOK // SLOT + NEUR - 1 and BLOCKS % UNR == 0
SLOTS, SHID = 64, 768
HCH = SHID // 128


class Steps:

    def __init__(self, eng, sem, base=0, turn=None, per=0):
        self.eng, self.sem, self.n, self.base, self.turn, self.per = eng, sem, 0, base, turn, per

    def value(self, n):
        return self.base + n if self.turn is None else self.turn * self.per + (self.base + n)

    def then(self, ins):
        self.mark(ins)
        self.eng.wait_ge(self.sem, self.value(self.n))

    def mark(self, ins):
        ins.then_inc(self.sem, 1)
        self.n += 1

    def wait(self):
        self.eng.wait_ge(self.sem, self.value(self.n))


def embed(nc, t, h_tok, gathered):
    with ExitStack() as ctx:
        def sb(name, shape, dt=F32):
            return ctx.enter_context(nc.sbuf_tensor(name, shape, dt))

        def pb(name, shape, dt=F32):
            return ctx.enter_context(nc.psum_tensor(name, shape, dt))

        phase = Phase(nc, ctx)
        sem = phase.sem

        quad = sb("quad", [128, 10, 4, 3, B])
        side = sb("side", [128, 8, 5, 3, B])
        sqr = sb("sqr", [128, 8, 4, 3, B])
        w1 = sb("w1", [128, KCH, HID])
        w1g = sb("w1g", [128, RING, HID])
        gb = sb("gb", [128, KCH, 2])
        csum = sb("csum", [128, 2, 32, B])
        half1 = sb("half1", [128, 2, 128])
        qstat = sb("qstat", [128, 2, 10, 10, B])
        st = [sb(f"st{i}", [128, 2, 16, B]) for i in range(4)]
        g1c1 = sb("g1c1", [128, 3, 2])
        b1 = sb("b1", [128, 3])
        w2 = sb("w2", [128, 3, D])
        b2 = sb("b2", [128, D])
        hid = sb("hid", [128, 3, 512])
        img = sb("img", [128, 4, D])
        ident = sb("ident", [128, 128])
        eps = sb("eps", [128, 2])
        ids = sb("ids", [128, 8], I32)
        idf = sb("idf", [128, 2, 8])
        idc = sb("idc", [128, 8], I32)
        rows = sb("rows", [128, 8, BASIN])
        rowsT = sb("rowsT", [BASIN, 2, 512])
        projT = sb("projT", [BASIN, D])
        normw = sb("normw", [128, D])
        txt = sb("txt", [128, 8, D])
        txsq = sb("txsq", [128, D])
        rms = sb("rms", [128, 3, 8])
        psH = [pb(f"psH{m}", [128, 512]) for m in range(3)]
        psC = pb("psC", [128, 3, 2])
        psS = [pb(f"psS{i}", [128, 512]) for i in range(4)]

        x_in, w1_in, s_in, id_in = sem("x_in"), [sem(f"w1_in{i}") for i in range(3)], sem("s_in"), sem("id_in")
        pads, consts = sem("pads"), sem("consts")
        squared, sums_in, sums_out, sums_free = sem("squared"), sem("sums_in"), sem("sums_out"), sem("sums_free")
        dve, scaled, small, main = sem("dve"), sem("scaled"), sem("small"), sem("main")
        var_in, std_out = sem("var_in"), sem("std_out")
        pre_act, acted, img_ps, img_sb, stored = sem("pre_act"), sem("acted"), sem("img_ps"), sem("img_sb"), sem("stored")
        clamped, txT, txT_sb, tx_ps, tx_ss, tx_std, tx_sb = (sem(n) for n in (
            "clamped", "txT", "txT_sb", "tx_ps", "tx_ss", "tx_std", "tx_sb"))
        tx_free = sem("tx_free")

        def patches(k):
            s, c, qy = k // 6, k // 2 % 3, k % 2
            if s < 3:
                y0 = 1 + qy + (0, -1, 1)[s]
                return quad[:, y0:y0 + 7:2, :, c, :]
            x0 = s - 3
            return side[:, qy:qy + 7:2, x0:x0 + 4, c, :]

        scope = ctx.enter_context(ExitStack())
        block = scope.enter_context(nc.Block())

        @block.sync
        def _(sp):
            sp.wait_ge(pads, 1)
            sp.dma_start(quad[:, 1:9], t["x_quads"]).then_inc(x_in, 16)
            for i in range(3):
                sp.dma_start(w1[:, 10 * i:10 * i + 10], t["W1"][:, 10 * i:10 * i + 10]).then_inc(w1_in[i], 16)
            sp.wait_ge(img_sb, 4)
            for gw in range(4):
                sp.dma_start(h_tok[:, 0:PATCHES].rearrange("b (gh gw) d -> gw b gh d", gw=4)[gw],
                             img[32 * gw:32 * gw + 32]).then_inc(stored, 16)
            sp.wait_ge(tx_sb, 8)
            for q in range(4):
                sp.dma_start(h_tok[:, PATCHES:SEQ].rearrange("(i b) s d -> b s i d", b=4)[q],
                             txt[32 * q:32 * q + 32]).then_inc(stored, 16)
            sp.wait_ge(stored, 8 * 16)

        @block.gpsimd
        def _(pool):
            nc.gpsimd.memset(quad[:], 0.0)
            nc.gpsimd.memset(side[:], 0.0)
            nc.gpsimd.memset(qstat[:], 0.0).then_inc(pads, 1)
            nc.gpsimd.memset(half1[:], 1.0)
            nc.gpsimd.memset(eps[:, 0:1], LN_EPS)
            nc.gpsimd.memset(eps[:, 1:2], 1e-8)
            nc.gpsimd.memset(ident[:], 0.0).then_inc(consts, 1)
            pool.wait_ge(consts, 1)
            nc.gpsimd.affine_select(out=half1[:, 0, :], in_=half1[:, 0, :], compare_op=ALU.is_ge, fill=0.0, base=63,
                                    pattern=[[0, 128]], channel_multiplier=-1)
            nc.gpsimd.affine_select(out=half1[:, 1, :], in_=half1[:, 1, :], compare_op=ALU.is_ge, fill=0.0, base=-64,
                                    pattern=[[0, 128]], channel_multiplier=1)
            nc.gpsimd.affine_select(out=ident[:], in_=ident[:], compare_op=ALU.not_equal, fill=1.0, base=0,
                                    pattern=[[-1, 128]], channel_multiplier=1).then_inc(consts, 1)
            pool.wait_ge(clamped, 1)
            for i in range(8):
                nc.gpsimd.indirect_dma_start(rows[:, i, :], None, t["basin"],
                                             bass.IndirectOffsetOnAxis(idc[:, i:i + 1], 0)).then_inc(gathered[i // 4], 16)

        @block.scalar
        def _(act):
            act.dma_start(ids[:], t["text_ids"]).then_inc(id_in, 16)
            act.wait_ge(pads, 1)
            act.dma_start(side[0:64, :, 0:4], t["x_quads"][0:64]).then_inc(x_in, 16)
            act.dma_start(side[64:128, :, 1:5], t["x_quads"][64:128]).then_inc(x_in, 16)
            for dst, src in ((gb, "gb"), (b1, "b1"), (w2, "W2"), (projT, "txt_projT")):
                act.dma_start(dst[:], t[src]).then_inc(s_in, 16)
            for dst, src in ((b2, "b2"), (normw, "txt_norm")):
                act.dma_start(dst[:], t[src].partition_broadcast(128)).then_inc(s_in, 16)
            act.wait_ge(x_in, 48)
            nc.scalar.activation(sqr[:], quad[:, 1:9], ACT.Square).then_inc(squared, 1)
            for stat in range(2):
                act.wait_ge(sums_out, stat + 1)
                for side_ in range(2):
                    for n in range(2):
                        src = psS[2 * side_ + n][:].rearrange("p (y x b) -> p y x b", y=4, x=4)
                        dst = qstat[:, stat, 1 + 4 * n:5 + 4 * n, 1 + side_:8 + side_:2, :]
                        last = nc.scalar.activation(dst, src, ACT.Copy, scale=1.0 / (5 * 768))
                last.then_inc(sums_free, 1)
            act.wait_ge(var_in, 1)
            nc.scalar.activation(st[3][:, 1], st[3][:, 0], ACT.Sqrt, bias=eps[:, 0:1]).then_inc(std_out, 1)
            act.wait_ge(tx_ss, 1)
            nc.scalar.activation(rms[:, 1, :], rms[:, 0, :], ACT.Sqrt, bias=eps[:, 1:2],
                                 scale=1.0 / D).then_inc(tx_std, 1)
            for m in range(3):
                act.wait_ge(pre_act, m + 1)
                nc.scalar.activation(hid[:, m, :], hid[:, m, :], ACT.Gelu,
                                     bias=g1c1[:, m, 1:2]).then_inc(acted, 1)

        @block.tensor
        def _(pe):
            pe.wait_ge(consts, 2)
            for stat in range(2):
                pe.wait_ge(sums_in, stat + 1)
                if stat:
                    pe.wait_ge(sums_free, stat)
                for side_ in range(2):
                    for n in range(2):
                        last = nc.tensor.matmul(psS[2 * side_ + n][:], half1[:, side_, :],
                                                csum[:, stat, 16 * n:16 * n + 16, :], start=True, stop=True)
                last.then_inc(sums_out, 1)
            pe.wait_ge(s_in, 6 * 16)
            for m in range(3):
                for k in range(KCH):
                    pe.wait_ge(w1_in[k // 10], 16)
                    last = nc.tensor.matmul(psC[:, m, :], w1[:, k, 128 * m:128 * m + 128], gb[:, k, :],
                                            start=(k == 0), stop=(k == KCH - 1))
            last.then_inc(small, 1)
            for k in range(KCH):
                pe.wait_ge(scaled, k + 1)
                for m in range(3):
                    last = nc.tensor.matmul(psH[m][:], w1g[:, k % RING, 128 * m:128 * m + 128], patches(k),
                                            start=(k == 0), stop=(k == KCH - 1))
                last.then_inc(main, 1)
            for g in range(2):
                pe.wait_ge(gathered[g], 4 * 16)
                if g == 0:
                    pe.wait_ge(sums_free, 2)
                else:
                    pe.wait_ge(txT_sb, g)
                for i in range(4):
                    last = nc.tensor.transpose(psS[0][0:BASIN, 128 * i:128 * i + 128], rows[:, 4 * g + i, :], ident[:])
                last.then_inc(txT, 1)
                for i in range(4):
                    n = 4 * g + i
                    if i == 0:
                        pe.wait_ge(txT_sb, g + 1)
                    if n >= 3:
                        pe.wait_ge(tx_free, n - 2)
                    nc.tensor.matmul(psS[1 + n % 3][:, 0:D], rowsT[:, g, 128 * i:128 * i + 128], projT[:],
                                     start=True, stop=True).then_inc(tx_ps, 1)
            pe.wait_ge(acted, 3)
            pe.wait_ge(tx_free, 8)
            for gh in range(4):
                for m in range(3):
                    last = nc.tensor.matmul(psS[gh][:, 0:D], hid[:, m, 128 * gh:128 * gh + 128], w2[:, m, :],
                                            start=(m == 0), stop=(m == 2))
                last.then_inc(img_ps, 1)

        @block.vector
        def _(v):
            ch = Steps(v, dve)
            v.wait_ge(id_in, 16)
            ch.then(nc.vector.tensor_copy(idf[:, 0, :], ids[:]))
            ch.then(nc.vector.tensor_scalar(idf[:, 1, :], idf[:, 0, :], 0.0, float(VOCAB), ALU.is_lt, ALU.mult))
            ch.then(nc.vector.tensor_tensor(idf[:, 0, :], idf[:, 0, :], idf[:, 1, :], ALU.add))
            nc.vector.tensor_scalar(idc[:], idf[:, 0, :], 0.0, float(VOCAB - 1), ALU.max,
                                    ALU.min).then_inc(clamped, 1)
            v.wait_ge(x_in, 48)
            nc.vector.tensor_reduce(csum[:, 0], quad[:, 1:9].rearrange("p y x c b -> p (y x) b c"), X,
                                    ALU.add).then_inc(sums_in, 1)
            v.wait_ge(squared, 1)
            nc.vector.tensor_reduce(csum[:, 1], sqr[:].rearrange("p y x c b -> p (y x) b c"), X,
                                    ALU.add).then_inc(sums_in, 1)
            v.wait_ge(s_in, 6 * 16)
            for k in range(KCH):
                v.wait_ge(w1_in[k // 10], 16)
                if k >= RING:
                    v.wait_ge(main, k - RING + 1)
                nc.vector.tensor_scalar(w1g[:, k % RING, :], w1[:, k, :], gb[:, k, 0:1], None, ALU.mult).then_inc(scaled, 1)
            v.wait_ge(sums_free, 2)

            def q(stat, y, x):
                return qstat[:, stat, 1 + y:8 + y:2, 1 + x:8 + x:2, :]

            def grid(a, stat):
                return a[:, stat].rearrange("p (y x) b -> p y x b", y=4)

            def add(dst, a, b):
                for stat in range(2):
                    last = nc.vector.tensor_tensor(grid(dst, stat), a(stat), b(stat), ALU.add)
                ch.mark(last)

            def at(y, x):
                return lambda stat: q(stat, y, x)

            def of(a):
                return lambda stat: grid(a, stat)

            c0, c1, s, u = st
            add(c0, at(0, 0), at(0, 1))
            add(c1, at(1, 0), at(1, 1))
            add(s, at(-1, 0), at(-1, 1))
            add(u, at(2, 0), at(2, 1))
            ch.wait()
            add(c0, of(c0), of(c1))
            add(s, of(s), of(u))
            ch.wait()
            for dy in (0, 1):
                for dx in (-1, 2):
                    add(s, of(s), at(dy, dx))
                    ch.wait()
            ch.then(nc.vector.scalar_tensor_tensor(out=s[:], in0=c0[:], scalar=3.0, in1=s[:], op0=ALU.mult,
                                                   op1=ALU.add))
            ch.then(nc.vector.tensor_tensor(c0[:, 0], s[:, 0], s[:, 0], ALU.mult))
            nc.vector.tensor_tensor(u[:, 0], s[:, 1], c0[:, 0], ALU.subtract).then_inc(var_in, 1)
            v.wait_ge(std_out, 1)
            ch.then(nc.vector.reciprocal(c1[:, 0], u[:, 1]))
            for g in range(2):
                v.wait_ge(txT, g + 1)
                nc.vector.tensor_copy(rowsT[:, g, :], psS[0][0:BASIN, :]).then_inc(txT_sb, 1)
                for i in range(4):
                    n = 4 * g + i
                    v.wait_ge(tx_ps, n + 1)
                    nc.vector.tensor_copy(txt[:, n, :], psS[1 + n % 3][:, 0:D]).then_inc(tx_free, 1)
                    v.wait_ge(tx_free, n + 1)
                    ch.then(nc.vector.tensor_tensor_reduce(txsq[:], txt[:, n, :], txt[:, n, :], 1.0, 0.0, ALU.mult,
                                                           ALU.add, rms[:, 0, n:n + 1]))
            nc.vector.memset(rms[:, 2, 0:1], 0.0).then_inc(tx_ss, 1)
            v.wait_ge(tx_std, 1)
            ch.then(nc.vector.reciprocal(rms[:, 2, :], rms[:, 1, :]))
            for n in range(8):
                nc.vector.scalar_tensor_tensor(out=txt[:, n, :], in0=txt[:, n, :], scalar=rms[:, 2, n:n + 1],
                                               in1=normw[:], op0=ALU.mult, op1=ALU.mult).then_inc(tx_sb, 1)
            v.wait_ge(small, 1)
            ch.then(nc.vector.tensor_scalar(g1c1[:, :, 0], psC[:, :, 0], -1.0, None, ALU.mult))
            ch.then(nc.vector.tensor_tensor(g1c1[:, :, 1], psC[:, :, 1], b1[:], ALU.add))
            v.wait_ge(main, KCH)
            for m in range(3):
                ch.then(nc.vector.scalar_tensor_tensor(out=hid[:, m, :], in0=s[:, 0].rearrange("p g b -> p (g b)"),
                                                       scalar=g1c1[:, m, 0:1], in1=psH[m][:], op0=ALU.mult,
                                                       op1=ALU.add))
                nc.vector.tensor_tensor(hid[:, m, :], hid[:, m, :], c1[:, 0].rearrange("p g b -> p (g b)"),
                                        ALU.mult).then_inc(pre_act, 1)
            for gh in range(4):
                v.wait_ge(img_ps, gh + 1)
                nc.vector.tensor_tensor(img[:, gh, :], psS[gh][:, 0:D], b2[:], ALU.add).then_inc(img_sb, 1)
        scope.close()
        phase.clear()


class Phase:

    def __init__(self, nc, ctx):
        self.nc, self.ctx, self.sems = nc, ctx, []

    def sem(self, name):
        self.sems.append(self.ctx.enter_context(self.nc.semaphore(name)))
        return self.sems[-1]

    def clear(self):
        with self.nc.Block() as block:
            @block.sync
            def _(sp):
                for sem in self.sems:
                    sp.sem_clear(sem)


def spread(a, n):
    return a.unsqueeze(a.ndim).to_broadcast(list(a.shape) + [n])


def centred(nc, ch, ln_sq, ln_std, h, xc, sq, stats):
    v = nc.vector
    ch.then(v.tensor_reduce(stats[:, 0], h, X, ALU.add))
    ch.then(v.tensor_scalar(stats[:, 0], stats[:, 0], 1.0 / D, None, ALU.mult))
    ch.then(v.tensor_tensor(xc, h, spread(stats[:, 0], D), ALU.subtract))
    ch.then(v.tensor_tensor(sq, xc, xc, ALU.mult))
    v.tensor_reduce(stats[:, 1], sq, X, ALU.add).then_inc(ln_sq, 1)
    ch.eng.wait_ge(ln_std, 1)
    ch.then(v.reciprocal(stats[:, 3], stats[:, 2]))


def qkv(nc, t, keep, h_tok):
    with ExitStack() as ctx:
        def sb(name, shape, dt=F32):
            return ctx.enter_context(nc.sbuf_tensor(name, shape, dt))

        phase = Phase(nc, ctx)
        sem = phase.sem

        h, xT, qkT, fac, ident = keep["h"], keep["xT"], keep["qkT"], keep["fac"], keep["ident"]
        xc, sq = sb("xc", [HALF, PAIRS, D]), sb("sq", [HALF, PAIRS, D])
        stats = sb("stats", [HALF, 4, PAIRS])
        eps = sb("eps2", [HALF, 1])
        wqk, wg = sb("wqk", [HALF, 2, 4 * HALF]), sb("wg", [HALF, 2, GROUPS, HALF])
        bqk, bg = sb("bqk", [HALF, 4]), sb("bg", [128, HALF])
        stage = sb("stage", [HALF, 2, 2, 4, B])
        st_sb = sem("st_sb")
        ps = [ctx.enter_context(nc.psum_tensor(f"psq{i}", [128, 512], F32)) for i in range(8)]
        h_in, w_in, dve, ln_sq, ln_std, eps_set = (sem(n) for n in (
            "h_in2", "w_in2", "dve2", "ln_sq", "ln_std", "eps_set"))
        xn_ready, x_ps, x_sb, q_ps, q_sb, f_ps, f_sb = (sem(n) for n in (
            "xn_ready", "x_ps", "x_sb", "q_ps", "q_sb", "f_ps", "f_sb"))
        scope = ctx.enter_context(ExitStack())
        block = scope.enter_context(nc.Block())

        @block.sync
        def _(sp):
            sp.dma_start(h[:], h_tok.rearrange("(r b) s d -> (b s) r d", b=2)).then_inc(h_in, 16)
            for dst, src in ((wqk, "wqk"), (wg, "wqk_groups"), (bqk, "bqk"), (bg, "bqk_groups"), (ident, "ident")):
                sp.dma_start(dst[:], t[src]).then_inc(w_in, 16)

        @block.vector
        def _(v):
            ch = Steps(v, dve)
            nc.vector.memset(eps[:], LN_EPS).then_inc(eps_set, 1)
            v.wait_ge(h_in, 16)
            centred(nc, ch, ln_sq, ln_std, h[:], xc[:], sq[:], stats)
            nc.vector.tensor_tensor(sq[:], xc[:], spread(stats[:, 3], D), ALU.mult).then_inc(xn_ready, 1)
            v.wait_ge(w_in, 5 * 16)
            with v.Fori(0, 6) as i:
                for u in range(2):
                    v.wait_ge(f_ps, i * 2 + (u + 1))
                    nc.vector.tensor_tensor(
                        fac[:].rearrange("p m n -> p n m")[:, bass.ds(i * 8 + 4 * u, 4), :],
                        ps[6 + u][:, 0:4 * HALF].rearrange("p (n m) -> p n m", n=4),
                        bg[:].unsqueeze(1).to_broadcast([128, 4, HALF]), ALU.add).then_inc(f_sb, 1)

        @block.scalar
        def _(act):
            act.wait_ge(eps_set, 1)
            act.wait_ge(ln_sq, 1)
            nc.scalar.activation(stats[:, 2], stats[:, 1], ACT.Sqrt, bias=eps[:, 0:1], scale=1.0 / D).then_inc(ln_std, 1)
            for g in range(8):
                half, r = g % 2, g // 2
                act.wait_ge(x_ps, g + 1)
                nc.scalar.activation(xT[:, half, 384 * r:384 * r + 384], ps[g % 4][0:HALF, 0:384],
                                     ACT.Copy).then_inc(x_sb, 1)
            act.wait_ge(x_sb, 8)
            by_row = xT[:].rearrange("p h (b n) -> p h n b", n=SEQ)
            with act.Fori(0, 6) as i:
                for u in range(2):
                    if u == 0:
                        act.wait_ge(f_ps, i * 2)
                    nc.scalar.activation(stage[:, u], by_row[:, :, bass.ds(i * 8 + 4 * u, 4), :],
                                         ACT.Copy).then_inc(st_sb, 1)
            for g in range(12):
                oh, n = g // 3, g % 3
                act.wait_ge(q_ps, g + 1)
                nc.scalar.activation(qkT[:, oh, 512 * n:512 * n + 512], ps[g % 4][0:HALF, :], ACT.Identity,
                                     bias=bqk[:, oh:oh + 1]).then_inc(q_sb, 1)

        @block.tensor
        def _(pe):
            pe.wait_ge(xn_ready, 1)
            pe.wait_ge(w_in, 5 * 16)
            for g in range(8):
                half, r = g % 2, g // 2
                if g >= 4:
                    pe.wait_ge(x_sb, g - 3)
                for j in range(4):
                    last = nc.tensor.transpose(ps[g % 4][0:HALF, HALF * j:HALF * j + HALF],
                                               sq[:, 4 * r + j, HALF * half:HALF * half + HALF],
                                               ident[0:HALF, 0:HALF])
                last.then_inc(x_ps, 1)
            pe.wait_ge(x_sb, 8)
            with pe.Fori(0, 6) as i:
                for u in range(2):
                    pe.wait_ge(st_sb, i * 2 + (u + 1))
                    if u == 0:
                        pe.wait_ge(f_sb, i * 2)
                    for j in range(4):
                        for g in range(GROUPS):
                            for half in range(2):
                                last = nc.tensor.matmul(
                                    ps[6 + u][32 * g:32 * g + 32, HALF * j:HALF * j + HALF],
                                    stage[:, u, half, j, :],
                                    wg[:, half, g, :], start=(half == 0), stop=(half == 1))
                    last.then_inc(f_ps, 1)
            for g in range(12):
                oh, n = g // 3, g % 3
                if g >= 4:
                    pe.wait_ge(q_sb, g - 3)
                for half in range(2):
                    last = nc.tensor.matmul(ps[g % 4][0:HALF, :], wqk[:, half, HALF * oh:HALF * oh + HALF],
                                            xT[:, half, 512 * n:512 * n + 512], start=(half == 0), stop=(half == 1))
                last.then_inc(q_ps, 1)
        scope.close()
        phase.clear()


def factor(nc, t, keep, m_dram):
    with ExitStack() as ctx:
        def sb(name, shape, dt=F32):
            return ctx.enter_context(nc.sbuf_tensor(name, shape, dt))

        phase = Phase(nc, ctx)
        sem = phase.sem

        NM = 2 * GH
        A = keep["fac"][:].rearrange("p (m d) n -> p m d n", m=NM)
        tmp = sb("tmp", [128, NM * (HD - 1) * SEQ])
        n2, nrm, sg = sb("n2", [128, NM]), sb("nrm", [128, NM]), sb("sg", [128, NM])
        w, w2 = sb("wv", [128, NM, HD]), sb("wv2", [128, NM])
        rinv = sb("rinv", [128, NM, HD])
        Xk, Y, M = (sb(n, [128, GH, HD, HD]) for n in ("Xk", "Yq", "Mm"))
        dve, sq_sum, norm_out, m_ready, m_out = (sem(n) for n in ("dve3", "sq_sum", "norm_out", "m_ready", "m_out"))
        xT, qkT, v_all, kn4, qn4, qn4c = (keep[n] for n in ("xT", "qkT", "v_all", "kn4", "qn4", "qn4c"))
        qk2 = sb("qk2", [HALF, 4, TOK])
        headsum, rowmask = sb("headsum", [HALF, 64]), sb("rowmask", [128, 8])
        wv_, bv, ones1 = sb("wvT", [HALF, 2, D]), sb("bvr", [1, D]), sb("ones1", [1, SEQ])
        xst = sb("xst", [HALF, 2, 2, PAIR])
        ps = [ctx.enter_context(nc.psum_tensor(f"psf{i}", [128, 512], F32)) for i in range(8)]
        c_in, qk2_sb, n_ps, n_sb, xst_sb, v_ps, v_sb, ones_set = (sem(n) for n in (
            "c_in", "qk2_sb", "n_ps", "n_sb", "xst_sb", "v_ps", "v_sb", "ones_set"))
        scope = ctx.enter_context(ExitStack())
        block = scope.enter_context(nc.Block())

        @block.gpsimd
        def _(pool):
            nc.gpsimd.memset(keep["Mbd"][:], 0.0)
            nc.gpsimd.memset(ones1[:], 1.0).then_inc(ones_set, 1)

        @block.tensor
        def _(pe):
            pe.wait_ge(c_in, 4 * 16)
            pe.wait_ge(qk2_sb, 1)
            for qk in range(2):
                for n in range(3):
                    for half in range(2):
                        last = nc.tensor.matmul(ps[3 * qk + n][64 * half:64 * half + 64, :], headsum[:],
                                                qk2[:, 2 * qk + half, 512 * n:512 * n + 512], start=True, stop=True)
                    last.then_inc(n_ps, 1)
            pe.wait_ge(ones_set, 1)
            with pe.Fori(0, PAIRS // 2) as i:
                for u in range(2):
                    pe.wait_ge(xst_sb, i * 2 + (u + 1))
                    if u == 0:
                        pe.wait_ge(v_sb, i * 2)
                    for bb in range(2):
                        out = ps[6 + u][0:SEQ, D * bb:D * bb + D]
                        for half in range(2):
                            nc.tensor.matmul(out, xst[:, u, half, SEQ * bb:SEQ * bb + SEQ], wv_[:, half, :],
                                             start=(half == 0), stop=False)
                        last = nc.tensor.matmul(out, ones1[:], bv[:], start=False, stop=True)
                    last.then_inc(v_ps, 1)

        @block.scalar
        def _(act):
            nc.scalar.activation(qk2[:], qkT[:], ACT.Square).then_inc(qk2_sb, 1)
            for n in range(6):
                act.wait_ge(n_ps, n + 1)
                dst = (qn4 if n < 3 else kn4)[:, 512 * (n % 3):512 * (n % 3) + 512]
                nc.scalar.activation(dst, ps[n][:], ACT.Square).then_inc(n_sb, 1)
            with act.Fori(0, PAIRS // 2) as i:
                for u in range(2):
                    if u == 0:
                        act.wait_ge(v_ps, i * 2)
                    nc.scalar.activation(xst[:, u], xT[:, :, bass.ds((i * 2 + u) * PAIR, PAIR)],
                                         ACT.Copy).then_inc(xst_sb, 1)
                for u in range(2):
                    act.wait_ge(v_ps, i * 2 + (u + 1))
                    nc.scalar.activation(v_all[:, bass.ds(i * 4 + 2 * u, 2), :],
                                         ps[6 + u][0:SEQ, 0:2 * D].rearrange("p (b d) -> p b d", b=2),
                                         ACT.Copy).then_inc(v_sb, 1)
            for j in range(HD):
                act.wait_ge(sq_sum, j + 1)
                nc.scalar.activation(nrm[:], n2[:], ACT.Sqrt).then_inc(norm_out, 1)

        @block.sync
        def _(sp):
            for dst, src in ((headsum, "headsum"), (rowmask, "rowmask"), (wv_, "wv"), (bv, "bv")):
                sp.dma_start(dst[:], t[src]).then_inc(c_in, 16)
            sp.wait_ge(m_ready, 1)
            sp.dma_start(m_dram, M[:]).then_inc(m_out, 16)
            sp.wait_ge(m_out, 16)

        @block.vector
        def _(v):
            ch = Steps(v, dve)
            op = nc.vector
            ch.then(op.memset(Xk[:], 0.0))
            for j in range(HD):
                L, C = SEQ - j, HD - 1 - j
                u = A[:, :, j, j:SEQ]
                sq = tmp[:, 0:NM * L].rearrange("p (m l) -> p m l", m=NM)
                ch.then(op.tensor_tensor(sq, u, u, ALU.mult))
                op.tensor_reduce(n2[:], sq, X, ALU.add).then_inc(sq_sum, 1)
                ch.then(op.tensor_scalar(sg[:], A[:, :, j, j], 0.0, 2.0, ALU.is_ge, ALU.mult))
                v.wait_ge(norm_out, j + 1)
                nb = sg
                ch.then(op.scalar_tensor_tensor(out=nb[:], in0=sg[:], scalar=-1.0, in1=nrm[:], op0=ALU.add,
                                                op1=ALU.mult))
                ch.then(op.tensor_tensor(A[:, :, j, j], A[:, :, j, j], nb[:], ALU.add))
                ch.mark(op.tensor_scalar(rinv[:, :, j], nb[:], -1.0, None, ALU.mult))
                if C == 0:
                    ch.wait()
                    continue
                ch.mark(op.tensor_tensor(w2[:], nb[:], A[:, :, j, j], ALU.mult))
                us = u.unsqueeze(2).to_broadcast([128, NM, C, L])
                prod = tmp[:, 0:NM * C * L].rearrange("p (m c l) -> p m c l", m=NM, c=C)
                rest = A[:, :, j + 1:HD, j:SEQ]
                ch.then(op.tensor_tensor(prod, rest, us, ALU.mult))
                ch.mark(op.tensor_reduce(w[:, :, 0:C], prod, X, ALU.add))
                ch.then(op.reciprocal(w2[:], w2[:]))
                ch.then(op.tensor_tensor(w[:, :, 0:C], w[:, :, 0:C], spread(w2[:], C), ALU.mult))
                ch.then(op.tensor_tensor(prod, us, w[:, :, 0:C].unsqueeze(3).to_broadcast([128, NM, C, L]), ALU.mult))
                ch.then(op.tensor_tensor(rest, rest, prod, ALU.subtract))
            ch.then(op.reciprocal(rinv[:], rinv[:]))
            for j in range(HD - 1, -1, -1):
                C = HD - 1 - j
                ch.mark(op.tensor_copy(Xk[:, :, j, j], rinv[:, GH:NM, j]))
                if C == 0:
                    ch.wait()
                    continue
                prod = tmp[:, 0:GH * C * C].rearrange("p (m c i) -> p m c i", m=GH, c=C)
                row = A[:, GH:NM, j + 1:HD, j].unsqueeze(2).to_broadcast([128, GH, C, C])
                ch.then(op.tensor_tensor(prod, Xk[:, :, j + 1:HD, j + 1:HD], row, ALU.mult))
                ch.then(op.tensor_reduce(w[:, 0:GH, 0:C], prod, X, ALU.add, negate=True))
                ch.then(op.tensor_tensor(Xk[:, :, j + 1:HD, j], w[:, 0:GH, 0:C], spread(rinv[:, GH:NM, j], C), ALU.mult))
            for j in range(HD - 1, -1, -1):
                C = HD - 1 - j
                rhs = Xk[:, :, j, :]
                if C:
                    prod = tmp[:, 0:GH * HD * C].rearrange("p (m c i) -> p m c i", m=GH, c=HD)
                    row = A[:, 0:GH, j + 1:HD, j].unsqueeze(2).to_broadcast([128, GH, HD, C])
                    ch.then(op.tensor_tensor(prod, Y[:, :, :, j + 1:HD], row, ALU.mult))
                    ch.then(op.tensor_reduce(w[:, 0:GH, :], prod, X, ALU.add))
                    ch.then(op.tensor_tensor(w[:, 0:GH, :], rhs, w[:, 0:GH, :], ALU.subtract))
                    rhs = w[:, 0:GH, :]
                ch.then(op.tensor_tensor(Y[:, :, :, j], rhs, spread(rinv[:, 0:GH, j], HD), ALU.mult))
            op.tensor_copy(M[:].rearrange("p m a c -> p m c a"), Y[:]).then_inc(m_ready, 1)
            v.wait_ge(n_sb, 6)
            v.wait_ge(c_in, 4 * 16)
            own = rowmask[:].unsqueeze(1).to_broadcast([128, TOK // 8, 8])
            by8 = qn4[:].rearrange("p (c r) -> p c r", r=8)
            ch.then(op.tensor_tensor(by8, by8, own, ALU.mult))
            ch.then(op.tensor_reduce(qn4c[:], by8, X, ALU.add))
        scope.close()
        phase.clear()


def attend(nc, t, keep, m_dram, *to_clear):
    with ExitStack() as ctx:
        def sb(name, shape, dt=F32):
            return ctx.enter_context(nc.sbuf_tensor(name, shape, dt))

        phase = Phase(nc, ctx)
        sem = phase.sem

        qkT, v_all, kn4, qn4c, Mbd, ident, oT = (keep[n] for n in ("qkT", "v_all", "kn4", "qn4c", "Mbd", "ident", "oT"))
        mask6 = sb("mask6", [HALF, HEADS_2])
        mix, mixr, scl, bncol = sb("mix", [128, 3, HALF]), sb("mixr", [128, 2, HALF]), sb("scl", [128, 3]), sb("bncol", [HALF, 5])
        inv, bias, eps = sb("inv", [HALF, 2]), sb("bias", [HALF, 1]), sb("eps4", [128, 2])
        CLEAR = BLOCKS * 16
        zeros = sb("zeros", [128, CLEAR])
        kst = sb("kst", [HALF, 2, PAIR])
        Mst = sb("Mst", [HALF, 2, 2, HALF])
        QX, GX = sb("QX", [HALF, 2, PAIR, HEADS_2]), sb("GX", [HALF, 2, PAIR, HEADS_2])
        S = [sb(f"S{k}", [128, 2, RCH * SEQ]) for k in range(3)]
        aq, sq, wq = (sb(n, [128, 2, RCH * SEQ]) for n in ("aq", "sq4", "wq"))
        P = sb("P", [HALF, 2, RCH, SEQ])
        mx, rs = sb("mx", [HALF, 2, RCH]), sb("rs", [HALF, 2, 2, RCH])
        pT, vst, osb = sb("pT", [SEQ, 2, SEQ * HEADS]), sb("vst", [SEQ, 2, D]), sb("osb", [SEQ, 2, D])
        psS = ctx.enter_context(nc.psum_tensor("psSc", [128, 2, 2, 512], F32))
        psY = ctx.enter_context(nc.psum_tensor("psY", [128, 2, 512], F32))
        psX = ctx.enter_context(nc.psum_tensor("psX", [128, 2, 512], F32))
        W = RCH * SEQ
        Yv, Tv = psY[0:HALF, :, 0:W], psX[0:SEQ, :, 0:W]
        psA = psX[0:HALF, 0, 0:D].rearrange("p (h n) -> p h n", h=2)
        psO = psY[0:SEQ, 0, 0:2 * D].rearrange("p (b d) -> p b d", b=2)
        psOT = psY[0:HALF, 1, 0:D].rearrange("p (h n) -> p h n", h=2)

        names = ("c_in4 m_in zeros cleared dve4 dve4b sk_ps gaps inv_in inv_std mix_set m_st a_ps qx gx s_ps s_sq s_g s_k a_sb w_sb s_r y_ps "
                 "z_sb e_sb p_sb t_ps t_sb v_st o_ps o_sb ot_ps ot_sb").split()
        q = {n: sem("at_" + n) for n in names}
        scope = ctx.enter_context(ExitStack())
        block = scope.enter_context(nc.Block())

        def pair(a, p, axis_len=PAIR):
            return a[:, :, bass.ds(p * axis_len, axis_len)]

        @block.sync
        def _(sp):
            for dst, src in ((mask6, "mask6"), (mix, "mix"), (bncol, "bncol")):
                sp.dma_start(dst[:], t[src]).then_inc(q["c_in4"], 16)
            for dst, src in ((mixr, "bnrow"), (scl, "scales")):
                sp.dma_start(dst[:], t[src].partition_broadcast(128)).then_inc(q["c_in4"], 16)
            for half in range(2):
                for h in range(HEADS_2):
                    g, m = divmod(HEADS_2 * half + h, GH)
                    sp.dma_start(Mbd[HD * h:HD * h + HD, half, :, HD * h:HD * h + HD],
                                 m_dram[B * g:B * g + B, m].rearrange("b a c -> a b c")).then_inc(q["m_in"], 16)
            sp.wait_ge(q["zeros"], 1)
            for dram in to_clear:
                rows = dram.rearrange("(p r) d -> p (r d)", p=128)
                for n in range(0, rows.shape[1], CLEAR):
                    sp.dma_start(rows[:, n:n + CLEAR], zeros[:]).then_inc(q["cleared"], 16)
            sp.wait_ge(q["cleared"], 16 * sum(dram.shape[0] * dram.shape[1] // (128 * CLEAR) for dram in to_clear))

        @block.gpsimd
        def _(pool):
            def head(p):
                pool.wait_ge(q["a_ps"], p)
                nc.gpsimd.tensor_copy(Mst[:], Mbd[:, :, bass.ds(p * 2, 2), :]).then_inc(q["m_st"], 1)
                pool.wait_ge(q["s_ps"], p)
                nc.gpsimd.tensor_copy(kst[:], pair(qkT[:, 2:4], p))
                nc.gpsimd.tensor_tensor(QX[:], spread(pair(qkT[:, 0:2], p), HEADS_2),
                                        mask6[:].unsqueeze(1).unsqueeze(1).to_broadcast([HALF, 2, PAIR, HEADS_2]),
                                        ALU.mult).then_inc(q["qx"], 1)
                pool.wait_ge(q["w_sb"], p)
                nc.gpsimd.tensor_tensor(
                    aq[:].rearrange("p b (c m) -> p b c m", c=RCH),
                    kn4[:, bass.ds(p * PAIR, PAIR)].rearrange("p (b m) -> p b m", b=2).unsqueeze(2).to_broadcast([128, 2, RCH, SEQ]),
                    spread(qn4c[:, bass.ds(p * 2 * RCH, 2 * RCH)].rearrange("p (b c) -> p b c", b=2), SEQ),
                    ALU.add).then_inc(q["a_sb"], 1)

            def tail(p):
                pool.wait_ge(q["o_ps"], p * 2)
                nc.gpsimd.tensor_copy(vst[:], v_all[:, bass.ds(p * 2, 2), :]).then_inc(q["v_st"], 1)

            nc.gpsimd.memset(zeros[:], 0.0).then_inc(q["zeros"], 1)
            pool.wait_ge(q["c_in4"], 5 * 16)
            pool.wait_ge(q["m_in"], 12 * 16)
            head(0)
            with pool.Fori(0, PAIRS - 1) as i:
                tail(i)
                head(i + 1)
            tail(PAIRS - 1)

        @block.tensor
        def _(pe):
            def head(p):
                pe.wait_ge(q["m_st"], p + 1)
                for half in range(2):
                    for bb in range(2):
                        last = nc.tensor.matmul(psA[:, half, SEQ * bb:SEQ * bb + SEQ], Mst[:, half, bb, :],
                                                qkT[:, half, bass.ds((p * 2 + bb) * SEQ, SEQ)], start=True, stop=True)
                last.then_inc(q["a_ps"], 1)
                pe.wait_ge(q["s_sq"], p)
                pe.wait_ge(q["s_g"], p)
                pe.wait_ge(q["s_k"], p)
                pe.wait_ge(q["qx"], p + 1)
                for kind, rows, ready in ((0, QX, None), (1, GX, "gx")):
                    if ready:
                        pe.wait_ge(q[ready], p + 1)
                    for bb in range(2):
                        for c in range(RCH):
                            for half in range(2):
                                last = nc.tensor.matmul(
                                    psS[64 * half:64 * half + SEQ, kind, bb, SEQ * c:SEQ * c + SEQ],
                                    rows[:, half, SEQ * bb + 8 * c:SEQ * bb + 8 * c + 8, :].rearrange("p n h -> p (n h)"),
                                    kst[:, half, SEQ * bb:SEQ * bb + SEQ], start=True, stop=True)
                    last.then_inc(q["s_ps"] if kind else q["sk_ps"], 1)

            def tail_mix(p):
                pe.wait_ge(q["s_r"], p + 1)
                pe.wait_ge(q["s_g"], p + 1)
                pe.wait_ge(q["s_k"], p + 1)
                pe.wait_ge(q["o_sb"], p)
                pe.wait_ge(q["ot_sb"], p)
                for bb in range(2):
                    for k in range(3):
                        last = nc.tensor.matmul(Yv[:, bb, :], mix[:, k, :], S[k][:, bb, :], start=(k == 0), stop=(k == 2))
                last.then_inc(q["y_ps"], 1)

            def tail_values(p):
                pe.wait_ge(q["p_sb"], p + 1)
                pe.wait_ge(q["v_st"], p + 1)
                pe.wait_ge(q["z_sb"], p + 1)
                for bb in range(2):
                    pe.wait_ge(q["t_sb"], p * 2 + bb)
                    nc.tensor.transpose(psX[0:HALF, 0, 0:HALF], P[:, bb, 0:2, :].rearrange("p c m -> p (c m)"),
                                        ident[0:HALF, 0:HALF])
                    for c in range(1, RCH):
                        last = nc.tensor.transpose(Tv[:, c // 3, HALF * (c % 3):HALF * (c % 3) + HALF], P[:, bb, c, :],
                                                   ident[0:HALF, 0:HALF])
                    last.then_inc(q["t_ps"], 1)
                    pe.wait_ge(q["t_sb"], p * 2 + (bb + 1))
                    nc.tensor.matmul(psY[0:HALF, 0, 2 * D:2 * D + 1], pT[:, bb, 0:HALF], vst[:, bb, 0:1],
                                     start=True, stop=True)
                    for o in range(HEADS):
                        last = nc.tensor.matmul(psO[:, bb, HD * o:HD * o + HD], pT[:, bb, o:SEQ * HEADS:HEADS],
                                                vst[:, bb, HD * o:HD * o + HD], start=True, stop=True)
                    last.then_inc(q["o_ps"], 1)
                pe.wait_ge(q["o_sb"], p + 1)
                for half in range(2):
                    for bb in range(2):
                        last = nc.tensor.matmul(psOT[:, half, SEQ * bb:SEQ * bb + SEQ],
                                                osb[:, bb, HALF * half:HALF * half + HALF], ident[0:SEQ, 0:SEQ],
                                                start=True, stop=True)
                last.then_inc(q["ot_ps"], 1)

            pe.wait_ge(q["gaps"], 1)
            pe.wait_ge(q["mix_set"], 1)
            head(0)
            with pe.Fori(0, PAIRS - 1) as i:
                tail_mix(i)
                head(i + 1)
                tail_values(i)
            tail_mix(PAIRS - 1)
            tail_values(PAIRS - 1)

        @block.scalar
        def _(act):
            def head(p):
                act.wait_ge(q["sk_ps"], p + 1)
                act.wait_ge(q["w_sb"], p)
                nc.scalar.activation(sq[:], psS[:, 0, :, 0:W], ACT.Square, scale=float(np.sqrt(2.0))).then_inc(q["s_sq"], 1)
                act.wait_ge(q["y_ps"], p)
                nc.scalar.activation(S[0][:], psS[:, 0, :, 0:W], ACT.Copy).then_inc(q["s_k"], 1)
                act.wait_ge(q["s_ps"], p + 1)
                nc.scalar.activation(S[2][:], psS[:, 1, :, 0:W], ACT.Square).then_inc(q["s_g"], 1)

            def roots(p):
                act.wait_ge(q["w_sb"], p + 1)
                nc.scalar.activation(S[1][:], wq[:], ACT.Sqrt).then_inc(q["s_r"], 1)

            def tail_exp(p):
                act.wait_ge(q["z_sb"], p + 1)
                nc.scalar.activation(P[:], P[:], ACT.Exp).then_inc(q["e_sb"], 1)

            def tail_turned(p):
                for bb in range(2):
                    act.wait_ge(q["t_ps"], p * 2 + (bb + 1))
                    act.wait_ge(q["o_ps"], p * 2)
                    nc.scalar.activation(pT[:, bb, :].rearrange("p (a n) -> p a n", a=2), Tv, ACT.Copy).then_inc(q["t_sb"], 1)

            act.wait_ge(q["inv_in"], 1)
            act.wait_ge(q["c_in4"], 5 * 16)
            nc.scalar.activation(mixr[:, 1, :], mixr[:, 1, :], ACT.Sqrt, bias=eps[:, 0:1])
            nc.scalar.activation(inv[:, 0:1], bncol[:, 4:5], ACT.Sqrt, bias=eps[0:HALF, 0:1]).then_inc(q["inv_std"], 1)
            head(0)
            roots(0)
            with act.Fori(0, PAIRS - 1) as i:
                tail_exp(i)
                head(i + 1)
                tail_turned(i)
                roots(i + 1)
            tail_exp(PAIRS - 1)
            tail_turned(PAIRS - 1)

        @block.vector
        def _(v):
            op = nc.vector

            def head_rows(p):
                v.wait_ge(q["a_ps"], p + 1)
                v.wait_ge(q["s_ps"], p)
                op.tensor_tensor(GX[:], spread(psA, HEADS_2),
                                 mask6[:].unsqueeze(1).unsqueeze(1).to_broadcast([HALF, 2, PAIR, HEADS_2]),
                                 ALU.mult).then_inc(q["gx"], 1)

            def head_riem(p, ch):
                v.wait_ge(q["s_sq"], p + 1)
                v.wait_ge(q["a_sb"], p + 1)
                v.wait_ge(q["s_r"], p)
                ch.then(op.tensor_tensor(wq[:], aq[:], sq[:], ALU.subtract))
                op.tensor_scalar(wq[:], wq[:], 0.0, 1e-8, ALU.max, ALU.add).then_inc(q["w_sb"], 1)

            def tail_max(p, ch):
                v.wait_ge(q["y_ps"], p + 1)
                Y = Yv.rearrange("p b (c m) -> p b c m", c=RCH)
                ch.then(op.tensor_reduce(mx[:], Y, X, ALU.max))
                ch.then(op.tensor_scalar(mx[:], mx[:], bias[:, 0:1], None, ALU.add))
                v.wait_ge(q["t_ps"], p * 2)
                for bb in range(2):
                    last = op.scalar_tensor_tensor(out=P[:, bb], in0=Y[:, bb], scalar=bias[:, 0:1],
                                                   in1=spread(mx[:, bb], SEQ), op0=ALU.add, op1=ALU.subtract)
                last.then_inc(q["z_sb"], 1)

            def tail_norm(p, ch):
                v.wait_ge(q["e_sb"], p + 1)
                ch.then(op.tensor_reduce(rs[:, 0], P[:], X, ALU.add))
                ch.then(op.reciprocal(rs[:, 1], rs[:, 0]))
                flat = P[:].rearrange("p b c m -> p (b c) m")
                op.tensor_tensor(flat, flat, spread(rs[:, 1].rearrange("p b c -> p (b c)"), SEQ), ALU.mult).then_inc(q["p_sb"], 1)

            def tail_out(p):
                v.wait_ge(q["o_ps"], p * 2 + 2)
                v.wait_ge(q["ot_ps"], p)
                op.tensor_copy(osb[:], psO).then_inc(q["o_sb"], 1)
                v.wait_ge(q["ot_ps"], p + 1)
                op.tensor_copy(pair(oT[:], p), psOT).then_inc(q["ot_sb"], 1)

            op.memset(psS[:], 0.0).then_inc(q["gaps"], 1)
            op.memset(eps[:], LN_EPS).then_inc(q["inv_in"], 1)
            ch = Steps(v, q["dve4"])
            v.wait_ge(q["c_in4"], 5 * 16)
            v.wait_ge(q["inv_std"], 1)
            ch.mark(op.reciprocal(mixr[:, 1, :], mixr[:, 1, :]))
            ch.then(op.reciprocal(inv[:, 1:2], inv[:, 0:1]))
            ch.mark(op.tensor_tensor(mixr[:, 0, :], mixr[:, 0, :], mixr[:, 1, :], ALU.mult))
            ch.mark(op.tensor_tensor(inv[:, 1:2], inv[:, 1:2], bncol[:, 2:3], ALU.mult))
            ch.mark(op.tensor_scalar(scl[:, 1:2], scl[:, 1:2], -1.0, None, ALU.mult))
            ch.then(op.tensor_tensor(bias[:], bncol[:, 0:1], bncol[:, 1:2], ALU.subtract))
            ch.then(op.scalar_tensor_tensor(out=bias[:], in0=bias[:], scalar=inv[:, 1:2], in1=bncol[:, 3:4],
                                            op0=ALU.mult, op1=ALU.add))
            for k in range(3):
                last = op.scalar_tensor_tensor(out=mix[:, k, :], in0=mix[:, k, :], scalar=scl[:, k:k + 1],
                                               in1=mixr[:, 0, :], op0=ALU.mult, op1=ALU.mult)
            last.then_inc(q["mix_set"], 1)
            ch = Steps(v, q["dve4b"])
            head_rows(0)
            head_riem(0, ch)
            PER = 5
            with v.Fori(0, PAIRS - 1) as i:
                ch = Steps(v, q["dve4b"], base=1, turn=i, per=PER)
                tail_max(i, ch)
                head_rows(i + 1)
                tail_norm(i, ch)
                head_riem(i + 1, ch)
                tail_out(i)
                assert ch.n == PER
            ch = Steps(v, q["dve4b"], base=1 + PER * (PAIRS - 1))
            tail_max(PAIRS - 1, ch)
            tail_norm(PAIRS - 1, ch)
            tail_out(PAIRS - 1)
        scope.close()
        phase.clear()


def route(nc, t, keep, xn_dram):
    with ExitStack() as ctx:
        def sb(name, shape, dt=F32):
            return ctx.enter_context(nc.sbuf_tensor(name, shape, dt))

        h, xT, oT, ident = keep["h"], keep["xT"], keep["oT"], keep["ident"]
        pos, w4, eid, xr = keep["pos"], keep["w4"], keep["eid"], keep["rows_in"]
        xc, sq, stats = sb("xc5", [HALF, PAIRS, D]), sb("sq5", [HALF, PAIRS, D]), sb("stats5", [HALF, 4, PAIRS])
        projT, projb = sb("projT5", [HALF, 2, D]), sb("projb5", [1, D])
        ones = sb("ones5", [128, 128])
        eps = sb("eps5", [128, 1])
        Wf, bf = sb("Wf", [HALF, 2, 128]), sb("bf", [128, 1])
        emb, emb2, est = sb("emb", [128, 2, 64]), sb("emb2", [128, 2, 64]), sb("est", [128, 3, 2])
        embT, fT = sb("embT", [128, 128]), sb("fT", [128, TOK])
        upper, iota = sb("upper", [128, 128]), sb("iota", [128, BLOCKS])
        L, prod = sb("L", [128, FT, 2, NEUR]), sb("prod5", [128, FT, 2, NEUR])
        O = [sb(f"O{k}", [128, FT, 2, NEUR]) for k in range(TOPK)]
        cum = sb("cum", [128, FT, 2 * NEUR])
        red, vals, idx, idf = (sb("red", [128, 2, 2 * FT]), sb("vals", [128, 2 * FT, 8]),
                               sb("idx", [128, 2 * FT, 8], U32), sb("idf5", [128, 2 * FT, TOPK]))
        posf = sb("posf", [128, 2 * FT, TOPK])
        cnt, cnti, nbf = sb("cnt", [128, 2]), sb("cnti", [128, 2, 2], I32), sb("nbf", [128, 2])
        nbw, start, endc = sb("nbw", [128, 2, NEUR]), sb("start", [128, 2 * NEUR]), sb("endc", [128, 2])
        gt, ef = sb("gt", [128, 2, BLOCKS]), sb("ef", [1, 2 * BLOCKS])
        ps = [ctx.enter_context(nc.psum_tensor(f"psr{i}", [128, 512], F32)) for i in range(8)]
        names = ("c_in dve set_up o_ps h_sb ln_sq ln_std xn xn_out xr_in x_ps x_sb e_sq e_std e_n e_ps e_sb f_ps f_sb "
                 "l_ps l_sb l_sub l_exp chosen cums r_ps r_sb c_ps nb st_ps en_ps gts b_ps st_sb").split()
        phase = Phase(nc, ctx)
        q = {n: phase.sem("rt_" + n) for n in names}
        LBANK = [0, 3, 1, 5, 2, 6]
        scope = ctx.enter_context(ExitStack())
        block = scope.enter_context(nc.Block())

        @block.sync
        def _(sp):
            for dst, src in ((projT, "attn_projT"), (projb, "attn_projb"), (Wf, "Wf"), (bf, "bf"), (emb, "emb"),
                             (upper, "upper"), (iota, "iota")):
                sp.dma_start(dst[:], t[src]).then_inc(q["c_in"], 16)
            sp.wait_ge(q["xn"], 1)
            sp.dma_start(xn_dram.rearrange("(r p) d -> p r d", p=PAIR), sq[:]).then_inc(q["xn_out"], 16)
            sp.wait_ge(q["xn_out"], 16)
            sp.dma_start(xr[:], xn_dram.rearrange("(t p) d -> p t d", p=128)).then_inc(q["xr_in"], 16)
            sp.wait_ge(q["xr_in"], 16)

        @block.tensor
        def _(pe):
            pe.wait_ge(q["c_in"], 7 * 16)
            pe.wait_ge(q["set_up"], 1)
            for g in range(8):
                if g >= 4:
                    pe.wait_ge(q["h_sb"], g - 3)
                for j in range(2):
                    out = ps[g % 4][0:HALF, D * j:D * j + D]
                    for half in range(2):
                        nc.tensor.matmul(out, oT[:, half, PAIR * (2 * g + j):PAIR * (2 * g + j + 1)], projT[:, half, :],
                                         start=(half == 0), stop=False)
                    last = nc.tensor.matmul(out, ones[0:1, 0:HALF], projb[:], start=False, stop=True)
                last.then_inc(q["o_ps"], 1)
            pe.wait_ge(q["e_n"], 1)
            nc.tensor.transpose(ps[4][:, 0:128], emb2[:].rearrange("p f d -> p (f d)"), ident[:]).then_inc(q["e_ps"], 1)
            pe.wait_ge(q["xn"], 1)
            for g in range(8):
                half, r = g % 2, g // 2
                if g < 4:
                    pe.wait_ge(q["h_sb"], 5 + g)
                else:
                    pe.wait_ge(q["x_sb"], g - 3)
                for j in range(4):
                    last = nc.tensor.transpose(ps[g % 4][0:HALF, HALF * j:HALF * j + HALF],
                                               sq[:, 4 * r + j, HALF * half:HALF * half + HALF], ident[0:HALF, 0:HALF])
                last.then_inc(q["x_ps"], 1)
            pe.wait_ge(q["x_sb"], 8)
            for n in range(3):
                for half in range(2):
                    last = nc.tensor.matmul(ps[5 + n][:], Wf[:, half, :], xT[:, half, 512 * n:512 * n + 512],
                                            start=(half == 0), stop=(half == 1))
                last.then_inc(q["f_ps"], 1)
            pe.wait_ge(q["e_sb"], 1)
            pe.wait_ge(q["f_sb"], 3)
            for g in range(6):
                n, f = g // 2, g % 2
                for j in range(4):
                    last = nc.tensor.matmul(ps[LBANK[g]][:, 128 * j:128 * j + 128],
                                            fT[64 * f:64 * f + 64, 128 * (4 * n + j):128 * (4 * n + j + 1)],
                                            embT[64 * f:64 * f + 64, :], start=True, stop=True)
                last.then_inc(q["l_ps"], 1)
            pe.wait_ge(q["cums"], 1)
            nc.tensor.matmul(ps[4][:, 0:1], cum[:, FT - 1, 0:NEUR], ones[:, 0:1], start=True, stop=True)
            nc.tensor.matmul(ps[4][:, 1:2], cum[:, FT - 1, NEUR:], ones[:, 0:1], start=True, stop=True).then_inc(q["c_ps"], 1)
            pe.wait_ge(q["nb"], 1)
            for f in range(2):
                last = nc.tensor.matmul(ps[5][:, 128 * f:128 * f + 128], nbw[:, f, :], upper[:], start=True, stop=True)
            last.then_inc(q["st_ps"], 1)
            nc.tensor.matmul(ps[6][:, 0:2], upper[:], nbf[:], start=True, stop=False)
            nc.tensor.matmul(ps[6][:, 0:2], ident[:], nbf[:], start=False, stop=True).then_inc(q["en_ps"], 1)
            for i in range(FT):
                if i < 4:
                    pe.wait_ge(q["l_sb"], 6)
                else:
                    pe.wait_ge(q["r_sb"], i - 3)
                last = nc.tensor.matmul(ps[i % 4][:, 0:256], upper[:], L[:, i].rearrange("p f e -> p (f e)"), start=True,
                                        stop=(i == 0))
                if i:
                    last = nc.tensor.matmul(ps[i % 4][:, 0:256], ones[:], cum[:, i - 1, :], start=False, stop=True)
                last.then_inc(q["r_ps"], 1)
            pe.wait_ge(q["gts"], 1)
            nc.tensor.matmul(ps[7][0:1, 0:2 * BLOCKS], ones[:, 0:1], gt[:].rearrange("p f j -> p (f j)"), start=True,
                             stop=True).then_inc(q["b_ps"], 1)

        @block.scalar
        def _(act):
            act.wait_ge(q["set_up"], 1)
            act.wait_ge(q["e_sq"], 1)
            nc.scalar.activation(est[:, 1], est[:, 0], ACT.Sqrt).then_inc(q["e_std"], 1)
            act.wait_ge(q["ln_sq"], 1)
            nc.scalar.activation(stats[:, 2], stats[:, 1], ACT.Sqrt, bias=eps[0:HALF], scale=1.0 / D).then_inc(q["ln_std"], 1)
            act.wait_ge(q["e_ps"], 1)
            nc.scalar.activation(embT[:], ps[4][:, 0:128], ACT.Copy).then_inc(q["e_sb"], 1)
            for g in range(8):
                half, r = g % 2, g // 2
                act.wait_ge(q["x_ps"], g + 1)
                nc.scalar.activation(xT[:, half, 384 * r:384 * r + 384], ps[g % 4][0:HALF, 0:384],
                                     ACT.Copy).then_inc(q["x_sb"], 1)
            for n in range(3):
                act.wait_ge(q["f_ps"], n + 1)
                nc.scalar.activation(fT[:, 512 * n:512 * n + 512], ps[5 + n][:], ACT.Identity,
                                     bias=bf[:]).then_inc(q["f_sb"], 1)
            for g in range(6):
                act.wait_ge(q["l_ps"], g + 1)
                nc.scalar.activation(L[:, 4 * (g // 2):4 * (g // 2) + 4, g % 2, :],
                                     ps[LBANK[g]][:].rearrange("p (t e) -> p t e", t=4), ACT.Copy).then_inc(q["l_sb"], 1)
            act.wait_ge(q["l_sub"], 1)
            nc.scalar.activation(L[:], L[:], ACT.Exp).then_inc(q["l_exp"], 1)

        @block.vector
        def _(v):
            op = nc.vector
            ch = Steps(v, q["dve"])
            ch.then(op.memset(ones[:], 1.0))
            op.memset(eps[:], LN_EPS).then_inc(q["set_up"], 1)
            v.wait_ge(q["c_in"], 7 * 16)
            ch.then(op.tensor_tensor(emb2[:], emb[:], emb[:], ALU.mult))
            op.tensor_reduce(est[:, 0], emb2[:], X, ALU.add).then_inc(q["e_sq"], 1)
            v.wait_ge(q["e_std"], 1)
            ch.then(op.tensor_scalar(est[:, 1], est[:, 1], 1e-8, None, ALU.add))
            ch.then(op.reciprocal(est[:, 2], est[:, 1]))
            op.tensor_tensor(emb2[:], emb[:], spread(est[:, 2], 64), ALU.mult).then_inc(q["e_n"], 1)
            for g in range(8):
                v.wait_ge(q["o_ps"], g + 1)
                hh = h[:, 2 * g:2 * g + 2, :]
                op.tensor_tensor(hh, hh, ps[g % 4][0:HALF, 0:2 * D].rearrange("p (r d) -> p r d", r=2),
                                 ALU.add).then_inc(q["h_sb"], 1)
            v.wait_ge(q["h_sb"], 8)
            centred(nc, ch, q["ln_sq"], q["ln_std"], h[:], xc[:], sq[:], stats)
            op.tensor_tensor(sq[:], xc[:], spread(stats[:, 3], D), ALU.mult).then_inc(q["xn"], 1)
            v.wait_ge(q["l_sb"], 6)
            rows = L[:].rearrange("p t f e -> p (t f) e")
            prod3 = prod[:].rearrange("p t f e -> p (t f) e")
            ch.then(op.tensor_reduce(red[:, 0], rows, X, ALU.max))
            op.tensor_tensor(rows, rows, spread(red[:, 0], NEUR), ALU.subtract).then_inc(q["l_sub"], 1)
            v.wait_ge(q["l_exp"], 1)
            ch.then(op.tensor_reduce(red[:, 0], rows, X, ALU.add))
            ch.then(op.reciprocal(red[:, 1], red[:, 0]))
            ch.then(op.tensor_tensor(rows, rows, spread(red[:, 1], NEUR), ALU.mult))
            for r in range(2 * FT):
                ch.mark(op.max(vals[:, r, :], rows[:, r, :]))
            ch.wait()
            for r in range(2 * FT):
                ch.mark(op.max_index(idx[:, r, :], vals[:, r, :], rows[:, r, :]))
            ch.mark(op.tensor_reduce(red[:, 0], vals[:, :, 0:TOPK], X, ALU.add))
            ch.wait()
            ch.mark(op.tensor_copy(idf[:], idx[:, :, 0:TOPK]))
            ch.then(op.tensor_scalar(red[:, 0], red[:, 0], 1e-8, None, ALU.add))
            ch.then(op.reciprocal(red[:, 1], red[:, 0]))
            ch.mark(op.tensor_tensor(w4[:], vals[:, :, 0:TOPK], spread(red[:, 1], TOPK), ALU.mult))
            for k in range(TOPK):
                ch.mark(op.tensor_tensor(O[k][:].rearrange("p t f e -> p (t f) e"),
                                         iota[:, 0:NEUR].unsqueeze(1).to_broadcast([128, 2 * FT, NEUR]),
                                         spread(idf[:, :, k], NEUR), ALU.is_equal))
            ch.wait()
            ch.mark(op.tensor_tensor(L[:], O[0][:], O[1][:], ALU.add))
            ch.then(op.tensor_tensor(prod[:], O[2][:], O[3][:], ALU.add))
            ch.then(op.tensor_tensor(L[:], L[:], prod[:], ALU.add))
            by_tile = L[:].rearrange("p t f e -> p t (f e)")
            ch.then(op.tensor_copy(cum[:, 0, :], by_tile[:, 0]))
            for i in range(1, FT):
                ch.then(op.tensor_tensor(cum[:, i, :], cum[:, i - 1, :], by_tile[:, i], ALU.add))
            op.memset(red[:, 0, 0:1], 0.0).then_inc(q["cums"], 1)
            v.wait_ge(q["c_ps"], 1)
            ch.then(op.tensor_scalar(cnt[:], ps[4][:, 0:2], float(SLOT - 1), None, ALU.add))
            ch.then(op.tensor_copy(cnti[:, 0], cnt[:]))
            ch.then(op.tensor_scalar(cnti[:, 1], cnti[:, 0], 7, None, ALU.arith_shift_right))
            ch.then(op.tensor_copy(nbf[:], cnti[:, 1]))
            op.tensor_copy(nbw[:], spread(nbf[:], NEUR)).then_inc(q["nb"], 1)
            v.wait_ge(q["st_ps"], 1)
            ch.mark(op.tensor_scalar(start[:], ps[5][:, 0:256], float(SLOT), None, ALU.mult))
            v.wait_ge(q["en_ps"], 1)
            ch.then(op.tensor_copy(endc[:], ps[6][:, 0:2]))
            for f in range(2):
                last = op.tensor_scalar(gt[:, f, :], iota[:], endc[:, f:f + 1], None, ALU.is_ge)
            last.then_inc(q["gts"], 1)
            for i in range(FT):
                v.wait_ge(q["r_ps"], min(i + 2, FT))
                op.tensor_tensor(cum[:, i, :], ps[i % 4][:, 0:256], start[:], ALU.add).then_inc(q["r_sb"], 1)
            v.wait_ge(q["r_sb"], FT)
            places = cum[:].rearrange("p t (f e) -> p t f e", f=2)
            for k in range(TOPK):
                ch.then(op.tensor_tensor(prod[:], O[k][:], places, ALU.mult))
                ch.then(op.tensor_reduce(posf[:, :, k], prod3, X, ALU.add))
            ch.mark(op.tensor_copy(pos[:], posf[:]))
            v.wait_ge(q["b_ps"], 1)
            ch.then(op.tensor_scalar(ef[:], ps[7][0:1, 0:2 * BLOCKS], float(NEUR - 1), None, ALU.min))
            ch.then(op.tensor_copy(eid[:], ef[:]))
        scope.close()
        phase.clear()


def routed(nc, t, keep, bank, scat, gath, w_in, w_out, slots_in, slots_out, weights, out_rows):
    HW = min(w_in, HALF) if w_in == D else w_in
    PARTS = w_in // HW
    with ExitStack() as ctx:
        def sb(name, shape, dt=F32):
            return ctx.enter_context(nc.sbuf_tensor(f"{name}_b{bank}", shape, dt))

        rows_in, pos, w4, eid, ident = (keep[n] for n in ("rows_in", "pos", "w4", "eid", "ident"))
        xb = [sb(f"xb{u}", [SLOT, w_in]) for u in range(UNR)]
        wb = [sb(f"wb{u}", [HW, PARTS, w_out]) for u in range(UNR)]
        xT = [sb(f"xbT{u}", [HW, PARTS, SLOT]) for u in range(UNR)]
        yb = [sb(f"yb{u}", [SLOT, w_out]) for u in range(UNR)]
        got = sb("got", [128, FT, TOPK, w_out])
        psT = [ctx.enter_context(nc.psum_tensor(f"psT{bank}_{u}", [128, 512], F32)) for u in range(UNR)]
        psO = [ctx.enter_context(nc.psum_tensor(f"psO{bank}_{u}", [128, 512], F32)) for u in range(UNR)]

        phase = Phase(nc, ctx)

        def sem(n):
            return phase.sem(f"rd{bank}_{n}")

        x_ld, w_ld, st = [sem(f"x_ld{u}") for u in range(UNR)], [sem(f"w_ld{u}") for u in range(UNR)], [sem(f"st{u}") for u in range(UNR)]
        t_ps, t_sb, y_ps, y_sb, acc = (sem(n) for n in ("t_ps", "t_sb", "y_ps", "y_sb", "acc"))
        TURNS = BLOCKS // UNR
        scope = ctx.enter_context(ExitStack())
        block = scope.enter_context(nc.Block())

        @block.gpsimd
        def _(pool):
            for i in range(FT):
                for k in range(TOPK):
                    nc.gpsimd.indirect_dma_start(slots_in, bass.IndirectOffsetOnAxis(pos[:, 2 * i + bank, k:k + 1], 0),
                                                 rows_in[:, i, 0:w_in], None).then_inc(scat, 16)
            for u in range(UNR):
                pool.wait_ge(st[u], 16 * TURNS)
            for i in range(FT):
                for k in range(TOPK):
                    nc.gpsimd.indirect_dma_start(got[:, i, k, :], None, slots_out,
                                                 bass.IndirectOffsetOnAxis(pos[:, 2 * i + bank, k:k + 1], 0)).then_inc(gath, 16)

        @block.sync
        def _(sp):
            sp.wait_ge(scat, 16 * FT * TOPK)
            with sp.Fori(0, TURNS) as i:
                for u in range(UNR):
                    if u == 0:
                        sp.wait_ge(y_ps, i * UNR)
                    j = i * UNR + u
                    sp.dma_start(xb[u][:], slots_in[bass.ds(j * SLOT, SLOT), :]).then_inc(x_ld[u], 16)
                    e = sp.value_load(eid[0:1, bass.ds(j + bank * BLOCKS, 1)], min_val=0, max_val=NEUR - 1)
                    sp.dma_start(wb[u][:], weights[bass.ds(e, 1)].rearrange("e (c p) n -> p (e c) n", p=HW)).then_inc(w_ld[u], 16)

        @block.tensor
        def _(pe):
            def turn(i, u):
                pe.wait_ge(x_ld[u], i * 16 + 16)
                if u == 0:
                    pe.wait_ge(t_sb, i * UNR)
                for c in range(PARTS):
                    last = nc.tensor.transpose(psT[u][0:HW, SLOT * c:SLOT * c + SLOT], xb[u][:, HW * c:HW * c + HW], ident[:])
                last.then_inc(t_ps, 1)

            def product(i, u):
                pe.wait_ge(w_ld[u], i * 16 + 16)
                if u == 0:
                    pe.wait_ge(y_sb, i * UNR)
                pe.wait_ge(t_sb, i * UNR + (u + 1))
                for c in range(PARTS):
                    last = nc.tensor.matmul(psO[u][:, 0:w_out], xT[u][:, c, :], wb[u][:, c, :], start=(c == 0),
                                            stop=(c == PARTS - 1))
                last.then_inc(y_ps, 1)

            with pe.Fori(0, TURNS) as i:
                turn(i, 0)
                for u in range(UNR):
                    if u + 1 < UNR:
                        turn(i, u + 1)
                    product(i, u)

        @block.scalar
        def _(act):
            with act.Fori(0, TURNS) as i:
                for u in range(UNR):
                    act.wait_ge(t_ps, i * UNR + (u + 1))
                    if u == 0:
                        act.wait_ge(y_ps, i * UNR)
                    nc.scalar.activation(xT[u][:].rearrange("p c n -> p (c n)"), psT[u][0:HW, 0:PARTS * SLOT],
                                         ACT.Copy).then_inc(t_sb, 1)
                for u in range(UNR):
                    act.wait_ge(y_sb, i * UNR + (u + 1))
                    act.dma_start(slots_out[bass.ds((i * UNR + u) * SLOT, SLOT), :], yb[u][:]).then_inc(st[u], 16)

        @block.vector
        def _(v):
            with v.Fori(0, TURNS) as i:
                for u in range(UNR):
                    v.wait_ge(y_ps, i * UNR + (u + 1))
                    v.wait_ge(st[u], i * 16)
                    nc.vector.tensor_copy(yb[u][:], psO[u][:, 0:w_out]).then_inc(y_sb, 1)
            v.wait_ge(gath, 16 * FT * TOPK)
            n = 0
            for k in range(TOPK):
                for i in range(FT):
                    out, w = out_rows[:, i, :], w4[:, 2 * i + bank, k:k + 1]
                    if k == 0:
                        nc.vector.tensor_scalar(out, got[:, i, k, :], w, None, ALU.mult).then_inc(acc, 1)
                    else:
                        v.wait_ge(acc, n - FT + 1)
                        nc.vector.scalar_tensor_tensor(out=out, in0=got[:, i, k, :], scalar=w, in1=out, op0=ALU.mult,
                                                       op1=ALU.add).then_inc(acc, 1)
                    n += 1
        scope.close()
        phase.clear()


def slots(nc, t, keep, ffn_dram, out):
    with ExitStack() as ctx:
        def sb(name, shape, dt=F32):
            return ctx.enter_context(nc.sbuf_tensor(name + "_s", shape, dt))

        h, xT, ident = keep["h"], keep["xT"], keep["ident"]
        xg, xn, sq = (sb(n, [HALF, PAIRS, D]) for n in ("xg", "xn", "sq"))
        stats, l2 = sb("stats", [HALF, 4, PAIRS]), sb("l2", [HALF, 3, PAIRS])
        projb, eps = sb("projb", [HALF, D]), sb("eps", [HALF, 1])
        ones = sb("ones", [HALF, HALF])
        phi, phi2, scl, pn = sb("phi", [HALF, 2, SLOTS]), sb("phi2", [HALF, 2, SLOTS]), sb("scl", [HALF, 1]), sb("pn", [HALF, 2, SLOTS])
        dT, dred = sb("dT", [SLOTS, B, SEQ]), sb("dred", [SLOTS, 2, B])
        C, cred = sb("C", [HALF, PAIRS, SLOTS]), sb("cred", [HALF, 2, PAIRS])
        own = sb("own", [HALF, 2])
        Dp, Cp = (sb(n, [HALF, PAIRS, 2, SLOTS]) for n in ("Dp", "Cp"))
        CT = sb("CT", [128, PAIRS, PAIR])
        xsT, ysT = sb("xsT", [HALF, 2, SLOTS, B]), sb("ysT", [HALF, 2, B, SLOTS])
        w1 = [sb(f"w1{u}", [HALF, 2, SHID]) for u in range(SRING)]
        w2 = [sb(f"w2{u}", [128, HCH, D]) for u in range(SRING)]
        b1, b2 = sb("b1", [128, SLOTS, HCH]), sb("b2", [HALF, 2, SLOTS])
        hb = [sb(f"hb{u}", [128, HCH, B]) for u in range(2)]
        ys = sb("ys", [128, PAIRS, D])
        ps = [ctx.enter_context(nc.psum_tensor(f"pss{i}", [128, 512], F32)) for i in range(8)]
        phase = Phase(nc, ctx)
        names = ("h_in c_in set_up dve ln_sq ln_std l2_sq l2_std xn x_ps x_sb p_sq p_ps p_std phin lt_ps lt_sb ln_ps "
                 "ln_sb d_sub d_exp c_sub c_exp d_nrm dt_ps d_sb c_nrm ct_ps ct_sb xs_ps xs_sb h_ps h_pre h_act y_ps y_sb "
                 "ys_ps ys_sb f_ps f_sb stored").split()
        q = {n: phase.sem("sl_" + n) for n in names}
        w_ld = [phase.sem(f"sl_w{u}") for u in range(SRING)]
        TURNS = SLOTS // SRING
        CS = 8
        scope = ctx.enter_context(ExitStack())
        block = scope.enter_context(nc.Block())

        def bank(i, rows, cols):
            return ps[i][0:rows, 0:cols]

        @block.sync
        def _(sp):
            sp.dma_start(sq[:], ffn_dram.rearrange("(r p) d -> p r d", p=PAIR)).then_inc(q["h_in"], 16)
            for dst, src in ((phi, "phi"), (own, "own"), (b1, "slot_b1"), (b2, "slot_b2")):
                sp.dma_start(dst[:], t[src]).then_inc(q["c_in"], 16)
            for dst, src in ((projb, "second_projb"), (scl, "phi_scale")):
                sp.dma_start(dst[:], t[src].partition_broadcast(HALF)).then_inc(q["c_in"], 16)
            with sp.Fori(0, TURNS) as i:
                for u in range(SRING):
                    if u == 0:
                        sp.wait_ge(q["y_ps"], i * SRING)
                    e = i * SRING + u
                    sp.dma_start(w1[u][:], t["slot_w1"][bass.ds(e, 1)].rearrange("e (c p) n -> p (e c) n", p=HALF)).then_inc(w_ld[u], 16)
                    sp.dma_start(w2[u][:], t["slot_w2"][bass.ds(e, 1)].rearrange("e (p c) n -> p (e c) n", p=128)).then_inc(w_ld[u], 16)
            sp.wait_ge(q["f_sb"], 8)
            sp.dma_start(out.rearrange("(r b) s d -> (b s) r d", b=2), h[:]).then_inc(q["stored"], 16)
            sp.wait_ge(q["stored"], 16)

        @block.tensor
        def _(pe):
            pe.wait_ge(q["p_sq"], 1)
            for half in range(2):
                last = nc.tensor.matmul(bank(4, HALF, SLOTS), ones[:], phi2[:, half, :], start=(half == 0), stop=(half == 1))
            last.then_inc(q["p_ps"], 1)
            pe.wait_ge(q["xn"], 1)
            for g in range(8):
                half, r = g % 2, g // 2
                if g >= 4:
                    pe.wait_ge(q["x_sb"], g - 3)
                for j in range(4):
                    last = nc.tensor.transpose(ps[g % 4][0:HALF, HALF * j:HALF * j + HALF],
                                               xn[:, 4 * r + j, HALF * half:HALF * half + HALF], ident[0:HALF, 0:HALF])
                last.then_inc(q["x_ps"], 1)
            pe.wait_ge(q["x_sb"], 8)
            pe.wait_ge(q["phin"], 1)
            for n in range(3):
                for half in range(2):
                    last = nc.tensor.matmul(bank(5 + n, SLOTS, 512), phi[:, half, :], xT[:, half, 512 * n:512 * n + 512],
                                            start=(half == 0), stop=(half == 1))
                last.then_inc(q["lt_ps"], 1)
            for g in range(2):
                for j in range(8):
                    for half in range(2):
                        r = 8 * g + j
                        last = nc.tensor.matmul(ps[g][0:HALF, SLOTS * j:SLOTS * j + SLOTS],
                                                xT[:, half, PAIR * r:PAIR * r + PAIR], phi[:, half, :],
                                                start=(half == 0), stop=(half == 1))
                last.then_inc(q["ln_ps"], 1)
            pe.wait_ge(q["d_nrm"], 1)
            for g in range(2):
                for j in range(8):
                    r = 8 * g + j
                    last = nc.tensor.transpose(ps[2 + g][0:HALF, SLOTS * j:SLOTS * j + SLOTS],
                                               dT[:, 2 * r:2 * r + 2, :].rearrange("p b m -> p (b m)"), ident[0:SLOTS, 0:SLOTS])
                last.then_inc(q["dt_ps"], 1)
            pe.wait_ge(q["c_nrm"], 1)
            for g in range(4):
                for j in range(4):
                    last = nc.tensor.transpose(ps[4 + g][:, PAIR * j:PAIR * j + PAIR],
                                               Cp[:, 4 * g + j].rearrange("p b n -> p (b n)"), ident[0:HALF, 0:HALF])
                last.then_inc(q["ct_ps"], 1)
            pe.wait_ge(q["d_sb"], 1)
            for g in range(8):
                half, r = g % 2, g // 2
                if g >= 4:
                    pe.wait_ge(q["ct_sb"], g - 3)
                for j in range(4):
                    last = nc.tensor.matmul(ps[g][0:HALF, 128 * j:128 * j + 128],
                                            xn[:, 4 * r + j, HALF * half:HALF * half + HALF],
                                            Dp[:, 4 * r + j].rearrange("p b n -> p (b n)"), start=True, stop=True)
                last.then_inc(q["xs_ps"], 1)

            def first(i, u):
                pe.wait_ge(w_ld[u], i * 32 + 32)
                if u % 2 == 0:
                    pe.wait_ge(q["h_pre"], i * SRING + u)
                for c in range(HCH):
                    for half in range(2):
                        last = nc.tensor.matmul(ps[u % 2][:, B * c:B * c + B], w1[u][:, half, c:SHID:HCH],
                                                xsT[:, half, bass.ds(i * SRING + u, 1), :].rearrange("p e b -> p (e b)"),
                                                start=(half == 0), stop=(half == 1))
                last.then_inc(q["h_ps"], 1)

            def second(i, u):
                pe.wait_ge(q["h_act"], i * SRING + (u + 1))
                if u % 2 == 0:
                    pe.wait_ge(q["y_sb"], i * SRING + u)
                for half in range(2):
                    for c in range(HCH):
                        last = nc.tensor.matmul(ps[2 + u % 2][0:HALF, B * half:B * half + B],
                                                w2[u][:, c, HALF * half:HALF * half + HALF], hb[u % 2][:, c, :],
                                                start=(c == 0), stop=(c == HCH - 1))
                last.then_inc(q["y_ps"], 1)

            pe.wait_ge(q["xs_sb"], 8)
            with pe.Fori(0, TURNS) as i:
                first(i, 0)
                for u in range(SRING):
                    if u + 1 < SRING:
                        first(i, u + 1)
                    second(i, u)
            pe.wait_ge(q["y_sb"], SLOTS)
            for r in range(PAIRS):
                g = r // 2
                if r % 2 == 0 and g >= 4:
                    pe.wait_ge(q["ys_sb"], g - 3)
                for half in range(2):
                    last = nc.tensor.transpose(ps[4 + g % 4][:, D * (r % 2) + HALF * half:D * (r % 2) + HALF * half + HALF],
                                               ysT[:, half, 2 * r:2 * r + 2, :].rearrange("p b n -> p (b n)"),
                                               ident[0:HALF, 0:HALF])
                if r % 2:
                    last.then_inc(q["ys_ps"], 1)
            for r in range(PAIRS):
                g = r // 2
                if r % 2 == 0:
                    pe.wait_ge(q["ys_sb"], g + 1)
                    if g >= 4:
                        pe.wait_ge(q["f_sb"], g - 3)
                last = nc.tensor.matmul(ps[g % 4][0:HALF, D * (r % 2):D * (r % 2) + D], CT[:, r, :], ys[:, r, :],
                                        start=True, stop=True)
                if r % 2:
                    last.then_inc(q["f_ps"], 1)

        @block.scalar
        def _(act):
            act.wait_ge(q["set_up"], 1)
            act.wait_ge(q["p_ps"], 1)
            nc.scalar.activation(pn[:, 0, :], bank(4, HALF, SLOTS), ACT.Sqrt).then_inc(q["p_std"], 1)
            act.wait_ge(q["ln_sq"], 1)
            nc.scalar.activation(stats[:, 2], stats[:, 1], ACT.Sqrt, bias=eps[:], scale=1.0 / D).then_inc(q["ln_std"], 1)
            act.wait_ge(q["l2_sq"], 1)
            nc.scalar.activation(l2[:, 1], l2[:, 0], ACT.Sqrt).then_inc(q["l2_std"], 1)
            for g in range(8):
                half, r = g % 2, g // 2
                act.wait_ge(q["x_ps"], g + 1)
                nc.scalar.activation(xT[:, half, 384 * r:384 * r + 384], bank(g % 4, HALF, 384), ACT.Copy).then_inc(q["x_sb"], 1)
            flat = dT[:].rearrange("p b m -> p (b m)")
            for n in range(3):
                act.wait_ge(q["lt_ps"], n + 1)
                nc.scalar.activation(flat[:, 512 * n:512 * n + 512], bank(5 + n, SLOTS, 512), ACT.Copy).then_inc(q["lt_sb"], 1)
            for g in range(2):
                act.wait_ge(q["ln_ps"], g + 1)
                nc.scalar.activation(C[:, 8 * g:8 * g + 8, :], bank(g, HALF, 512).rearrange("p (r n) -> p r n", r=8),
                                     ACT.Copy).then_inc(q["ln_sb"], 1)
            act.wait_ge(q["d_sub"], 1)
            nc.scalar.activation(dT[:], dT[:], ACT.Exp).then_inc(q["d_exp"], 1)
            act.wait_ge(q["c_sub"], 1)
            nc.scalar.activation(C[:], C[:], ACT.Exp).then_inc(q["c_exp"], 1)
            for g in range(4):
                act.wait_ge(q["ct_ps"], g + 1)
                nc.scalar.activation(CT[:, 4 * g:4 * g + 4, :], bank(4 + g, 128, 384).rearrange("p (r m) -> p r m", r=4),
                                     ACT.Copy).then_inc(q["ct_sb"], 1)
            for g in range(8):
                half, r = g % 2, g // 2
                act.wait_ge(q["xs_ps"], g + 1)
                nc.scalar.activation(xsT[:, half].rearrange("p n b -> p b n")[:, CS * r:CS * r + CS, :],
                                     bank(g, HALF, 512).rearrange("p (b n) -> p b n", b=CS), ACT.Copy).then_inc(q["xs_sb"], 1)
            with act.Fori(0, TURNS) as i:
                for u in range(SRING):
                    act.wait_ge(q["h_pre"], i * SRING + (u + 1))
                    nc.scalar.activation(hb[u % 2][:], hb[u % 2][:], ACT.Gelu).then_inc(q["h_act"], 1)
            for g in range(8):
                act.wait_ge(q["ys_ps"], g + 1)
                nc.scalar.activation(ys[:, 2 * g:2 * g + 2, :], bank(4 + g % 4, 128, 2 * D).rearrange("p (r d) -> p r d", r=2),
                                     ACT.Copy).then_inc(q["ys_sb"], 1)

        @block.vector
        def _(v):
            op = nc.vector
            ch = Steps(v, q["dve"])
            ch.mark(op.memset(ones[:], 1.0))
            op.memset(eps[:], LN_EPS).then_inc(q["set_up"], 1)
            v.wait_ge(q["c_in"], 6 * 16)
            op.tensor_tensor(phi2[:], phi[:], phi[:], ALU.mult).then_inc(q["p_sq"], 1)
            v.wait_ge(q["h_in"], 16)
            ch.then(op.tensor_tensor(h[:], h[:], sq[:], ALU.add))
            ch.then(op.tensor_tensor(h[:], h[:], projb[:].unsqueeze(1).to_broadcast([HALF, PAIRS, D]), ALU.add))
            centred(nc, ch, q["ln_sq"], q["ln_std"], h[:], xg[:], sq[:], stats)
            ch.then(op.tensor_tensor(xg[:], xg[:], spread(stats[:, 3], D), ALU.mult))
            ch.then(op.tensor_tensor(sq[:], xg[:], xg[:], ALU.mult))
            op.tensor_reduce(l2[:, 0], sq[:], X, ALU.add).then_inc(q["l2_sq"], 1)
            v.wait_ge(q["p_std"], 1)
            ch.then(op.tensor_scalar(pn[:, 0, :], pn[:, 0, :], 1e-12, None, ALU.max))
            ch.then(op.reciprocal(pn[:, 1, :], pn[:, 0, :]))
            op.scalar_tensor_tensor(out=phi[:], in0=phi[:], scalar=scl[:, 0:1],
                                    in1=pn[:, 1, :].unsqueeze(1).to_broadcast([HALF, 2, SLOTS]), op0=ALU.mult,
                                    op1=ALU.mult).then_inc(q["phin"], 1)
            v.wait_ge(q["l2_std"], 1)
            ch.then(op.tensor_scalar(l2[:, 1], l2[:, 1], 1e-12, None, ALU.max))
            ch.then(op.reciprocal(l2[:, 2], l2[:, 1]))
            op.tensor_tensor(xn[:], xg[:], spread(l2[:, 2], D), ALU.mult).then_inc(q["xn"], 1)
            v.wait_ge(q["lt_sb"], 3)
            ch.then(op.tensor_reduce(dred[:, 0], dT[:], X, ALU.max))
            op.tensor_tensor(dT[:], dT[:], spread(dred[:, 0], SEQ), ALU.subtract).then_inc(q["d_sub"], 1)
            v.wait_ge(q["ln_sb"], 2)
            ch.then(op.tensor_reduce(cred[:, 0], C[:], X, ALU.max))
            op.tensor_tensor(C[:], C[:], spread(cred[:, 0], SLOTS), ALU.subtract).then_inc(q["c_sub"], 1)
            v.wait_ge(q["d_exp"], 1)
            ch.then(op.tensor_reduce(dred[:, 0], dT[:], X, ALU.add))
            ch.then(op.reciprocal(dred[:, 1], dred[:, 0]))
            op.tensor_tensor(dT[:], dT[:], spread(dred[:, 1], SEQ), ALU.mult).then_inc(q["d_nrm"], 1)
            v.wait_ge(q["c_exp"], 1)
            ch.then(op.tensor_reduce(cred[:, 0], C[:], X, ALU.add))
            ch.then(op.reciprocal(cred[:, 1], cred[:, 0]))
            ch.then(op.tensor_tensor(C[:], C[:], spread(cred[:, 1], SLOTS), ALU.mult))
            for bb in range(2):
                last = op.tensor_scalar(Cp[:, :, bb, :], C[:], own[:, bb:bb + 1], None, ALU.mult)
                ch.mark(last)
            ch.wait()
            op.memset(cred[:, 0, 0:1], 0.0).then_inc(q["c_nrm"], 1)
            v.wait_ge(q["dt_ps"], 2)
            for g in range(2):
                for bb in range(2):
                    ch.mark(op.tensor_scalar(Dp[:, 8 * g:8 * g + 8, bb, :],
                                             bank(2 + g, HALF, 512).rearrange("p (r n) -> p r n", r=8),
                                             own[:, bb:bb + 1], None, ALU.mult))
            ch.wait()
            op.memset(dred[:, 0, 0:1], 0.0).then_inc(q["d_sb"], 1)
            with v.Fori(0, TURNS) as i:
                def bias(u):
                    v.wait_ge(q["h_ps"], i * SRING + (u + 1))
                    if u % 2 == 0:
                        v.wait_ge(q["y_ps"], i * SRING + u)
                    op.tensor_tensor(hb[u % 2][:], ps[u % 2][:, 0:HCH * B].rearrange("p (c b) -> p c b", c=HCH),
                                     spread(b1[:, bass.ds(i * SRING + u, 1), :].rearrange("p e c -> p (e c)"), B),
                                     ALU.add).then_inc(q["h_pre"], 1)

                def result(u):
                    v.wait_ge(q["y_ps"], i * SRING + (u + 1))
                    op.tensor_tensor(ysT[:, :, :, bass.ds(i * SRING + u, 1)].rearrange("p c b e -> p c (b e)"),
                                     ps[2 + u % 2][0:HALF, 0:2 * B].rearrange("p (c b) -> p c b", c=2),
                                     spread(b2[:, :, bass.ds(i * SRING + u, 1)].rearrange("p c e -> p (c e)"), B),
                                     ALU.add).then_inc(q["y_sb"], 1)

                for u in range(0, SRING, 2):
                    bias(u)
                    bias(u + 1)
                    result(u)
                    result(u + 1)
            for g in range(8):
                v.wait_ge(q["f_ps"], g + 1)
                hh = h[:, 2 * g:2 * g + 2, :]
                op.tensor_tensor(hh, hh, bank(g % 4, HALF, 2 * D).rearrange("p (r d) -> p r d", r=2),
                                 ALU.add).then_inc(q["f_sb"], 1)
        scope.close()
        phase.clear()


def build(nc, t):
    def dram(name, *shape):
        return nc.dram_tensor(name, shape, F32).ap()

    h_tok, m_dram, xn_dram = dram("h_tok", B, SEQ, D), dram("m_dram", 128, GH, HD, HD), dram("xn_dram", TOK, D)
    x_slots, f_slots = dram("x_slots", BLOCKS * SLOT, D), dram("f_slots", BLOCKS * SLOT, RANK)
    g_slots, r_slots = dram("g_slots", BLOCKS * SLOT, RANK), dram("r_slots", BLOCKS * SLOT, D)
    ffn_dram = dram("ffn_dram", TOK, D)
    with ExitStack() as ctx:
        gathered = [ctx.enter_context(nc.semaphore(f"gathered{g}")) for g in range(2)]
        scat, gath = ([ctx.enter_context(nc.semaphore(f"{n}{bank}")) for bank in range(2)] for n in ("scattered", "routed_in"))
        embed(nc, t, h_tok, gathered)

        def hold(scope, *tensors):
            for name, shape, dt in tensors:
                keep[name] = scope.enter_context(nc.sbuf_tensor("keep_" + name, shape, dt))

        keep = {}
        hold(ctx, ("h", [HALF, PAIRS, D], F32), ("ident", [128, 128], F32), ("xT", [HALF, 2, TOK], F32),
             ("oT", [HALF, 2, TOK], F32))
        with ExitStack() as scope:
            hold(scope, ("qkT", [HALF, 4, TOK], F32), ("fac", [128, 2 * GH * HD, SEQ], F32), ("v_all", [SEQ, B, D], F32),
                 ("Mbd", [HALF, 2, B, HALF], F32), ("kn4", [128, TOK], F32), ("qn4", [128, TOK], F32),
                 ("qn4c", [128, B * RCH], F32))
            qkv(nc, t, keep, h_tok)
            factor(nc, t, keep, m_dram)
            attend(nc, t, keep, m_dram, x_slots, g_slots)
        with ExitStack() as scope:
            hold(scope, ("pos", [128, 2 * FT, TOPK], I32), ("w4", [128, 2 * FT, TOPK], F32), ("eid", [1, 2 * BLOCKS], I32),
                 ("rows_in", [128, FT, D], F32))
            route(nc, t, keep, xn_dram)
            hf = scope.enter_context(nc.sbuf_tensor("hf", [128, FT, RANK], F32))
            routed(nc, t, keep, 0, scat[0], gath[0], D, RANK, x_slots, f_slots, t["f_know"], hf)
            keep["rows_in"] = hf
            ffn = scope.enter_context(nc.sbuf_tensor("ffn", [128, FT, D], F32))
            routed(nc, t, keep, 1, scat[1], gath[1], RANK, D, g_slots, r_slots, t["r_know"], ffn)
            with nc.semaphore("ffn_out") as ffn_out, nc.Block() as block:
                @block.sync
                def _(sp):
                    sp.dma_start(ffn_dram.rearrange("(t p) d -> p t d", p=128), ffn[:]).then_inc(ffn_out, 16)
                    sp.wait_ge(ffn_out, 16)
        slots(nc, t, keep, ffn_dram, t["out"])


def lay_out(a):
    x = a["x"].reshape(B, 3, 8, 8, 4, 2, 8)
    w1 = a["L0_tok_W1"].reshape(5, 3, 2, 8, 2, 8, HID)
    gb = np.stack([a["L0_tok_gamma"], a["L0_tok_beta"]], -1).reshape(5, 3, 2, 8, 2, 8, 2)

    def features(w):
        w = np.concatenate([w[:3], w[3:, :, :, :, ::-1]])
        return w.transpose(4, 3, 5, 0, 1, 2, 6).reshape(128, KCH, -1)

    out = {
        "x_quads": x.transpose(5, 3, 6, 2, 4, 1, 0).reshape(128, 8, 4, 3, B),
        "W1": features(w1),
        "gb": features(gb),
        "b1": a["L0_tok_b1"].reshape(3, 128).T,
        "W2": a["L0_tok_W2"].reshape(3, 128, D).transpose(1, 0, 2),
        "b2": a["L0_tok_b2"],
        "text_ids": a["x_txt"].reshape(8, 128).T,
        "basin": a["L0_txt_basin_coords"],
        "txt_projT": a["L0_txt_proj_w"].T,
        "txt_norm": a["L0_txt_norm_w"],
    }
    qk = a["L0_attn_qkv_w"][:2 * D].reshape(2, GROUPS, GH * HD, 2, HALF)
    qkb = a["L0_attn_qkv_b"][:2 * D].reshape(2, GROUPS, GH * HD)
    out |= {
        "ident": np.eye(128, dtype=np.float32),
        "wqk": a["L0_attn_qkv_w"][:2 * D].T.reshape(2, HALF, 2 * D).transpose(1, 0, 2),
        "bqk": a["L0_attn_qkv_b"][:2 * D].reshape(4, HALF).T,
        "wqk_groups": qk.transpose(4, 3, 1, 0, 2).reshape(HALF, 2, GROUPS, HALF),
        "bqk_groups": np.repeat(qkb.transpose(1, 0, 2).reshape(GROUPS, HALF), B, axis=0),
    }
    d96, d128 = np.arange(HALF), np.arange(128)
    row, head = d128 % 64 // HEADS_2, d128 % 64 % HEADS_2
    used = d128 % 64 < SEQ
    conv = a["L0_attn_conv_w"].reshape(HEADS, 3, 2, HEADS_2)
    mix = np.zeros((128, 3, 8, HEADS), np.float32)
    for p in d128[used]:
        mix[p, :, row[p], :] = conv[:, :, p // 64, head[p]].T
    bn = [a["L0_attn_" + n] for n in ("conv_b", "bn_mean", "bn_gamma", "bn_beta", "bn_var")]
    out |= {
        "headsum": ((d96[:, None] // HD == np.arange(64) % HEADS_2) & (np.arange(64) < SEQ)).astype(np.float32),
        "rowmask": ((row[:, None] == np.arange(8)) & used[:, None]).astype(np.float32),
        "mask6": (d96[:, None] // HD == np.arange(HEADS_2)).astype(np.float32),
        "wv": a["L0_attn_qkv_w"][2 * D:].T.reshape(2, HALF, D).transpose(1, 0, 2),
        "bv": a["L0_attn_qkv_b"][2 * D:].reshape(1, D),
        "mix": mix.reshape(128, 3, HALF),
        "bncol": np.tile(np.stack(bn, -1), (8, 1)),
        "bnrow": np.tile(np.stack([a["L0_attn_bn_gamma"], a["L0_attn_bn_var"]]), (1, 8)),
        "attn_projT": a["L0_attn_proj_w"].T.reshape(2, HALF, D).transpose(1, 0, 2),
        "attn_projb": a["L0_attn_proj_b"].reshape(1, D),
        "Wf": np.concatenate([a["L0_ffn_W_fk"], a["L0_ffn_W_rk"]], 1).reshape(2, HALF, 128).transpose(1, 0, 2),
        "bf": np.concatenate([a["L0_ffn_b_fk"], a["L0_ffn_b_rk"]]).reshape(128, 1),
        "emb": np.stack([a["L0_ffn_emb_fk"], a["L0_ffn_emb_rk"]], 1),
        "upper": np.triu(np.ones((128, 128), np.float32), 1),
        "iota": np.tile(np.arange(BLOCKS, dtype=np.float32), (128, 1)),
        "own": (np.arange(HALF)[:, None] // SEQ == np.arange(2)).astype(np.float32),
        "second_projb": a["L1_attn_proj_b"],
        "phi": a["L1_ffn_phi"].reshape(2, HALF, SLOTS).transpose(1, 0, 2),
        "phi_scale": a["L1_ffn_scale"],
        "slot_w1": a["L1_ffn_w1"],
        "slot_w2": a["L1_ffn_w2"],
        "slot_b1": a["L1_ffn_b1"].reshape(SLOTS, 128, HCH).transpose(1, 0, 2),
        "slot_b2": a["L1_ffn_b2"].T.reshape(2, HALF, SLOTS).transpose(1, 0, 2),
        "f_know": a["L0_ffn_f_know"],
        "r_know": a["L0_ffn_r_know"],
        "scales": np.stack([a["L0_attn_scale"], a["L0_attn_riem_scale"], a["L0_attn_grass_scale"]]),
    }
    return {n: np.ascontiguousarray(v) for n, v in out.items()}


def kernel(**inputs):
    import concourse.bacc as bacc
    from concourse.bass_utils import run_bass_kernel_spmd

    nc = bacc.Bacc("TRN2", target_bir_lowering=False, num_devices=1)
    arrays = {"in_" + n: v for n, v in lay_out({n: np.asarray(v) for n, v in inputs.items()}).items()}
    t = {n[3:]: nc.dram_tensor(n, v.shape, mybir.dt.from_np(v.dtype), kind="ExternalInput").ap()
         for n, v in arrays.items()}
    t["out"] = nc.dram_tensor("out_h", (B, SEQ, D), F32, kind="ExternalOutput").ap()
    build(nc, t)
    done = run_bass_kernel_spmd(nc, [arrays], core_ids=[0])
    return done.results[0]["out_h"]
```

```python
from contextlib import ExitStack

import numpy as np

import concourse.bass as bass
from concourse import mybir

F32 = mybir.dt.float32
I32 = mybir.dt.int32
U32 = mybir.dt.uint32
ALU = mybir.AluOpType
ACT = mybir.ActivationFunctionType
X = mybir.AxisListType.X

B = 32
SEQ = 48
PATCHES, TEXT = 16, 32
TOK = B * SEQ
D = 192
HALF = 96
PAIR = 2 * SEQ
PAIRS = B // 2
HEADS, HD = 12, 16
HEADS_2 = HEADS // 2
GROUPS, GH = 4, 3
HID = 384
RING = 15
KCH = 30
LN_EPS = 1e-5
VOCAB, BASIN = 32000, 64
RCH = SEQ // 8
NEUR = 128
RANK = 128
TOPK = 4
FT = TOK // 128
SLOT = 128
BLOCKS = 176
EPT = 4
UNR = 16
assert BLOCKS >= TOPK * TOK // SLOT + NEUR - 1 and BLOCKS % UNR == 0
SLOTS, SHID = 64, 768
HCH = SHID // 128


class Steps:

    def __init__(self, eng, sem, base=0, turn=None, per=0):
        self.eng, self.sem, self.n, self.base, self.turn, self.per = eng, sem, 0, base, turn, per

    def value(self, n):
        return self.base + n if self.turn is None else self.turn * self.per + (self.base + n)

    def then(self, ins):
        self.mark(ins)
        self.eng.wait_ge(self.sem, self.value(self.n))

    def mark(self, ins):
        ins.then_inc(self.sem, 1)
        self.n += 1

    def wait(self):
        self.eng.wait_ge(self.sem, self.value(self.n))


def embed(nc, t, h_tok, gathered):
    with ExitStack() as ctx:
        def sb(name, shape, dt=F32):
            return ctx.enter_context(nc.sbuf_tensor(name, shape, dt))

        def pb(name, shape, dt=F32):
            return ctx.enter_context(nc.psum_tensor(name, shape, dt))

        phase = Phase(nc, ctx)
        sem = phase.sem

        quad = sb("quad", [128, 10, 4, 3, B])
        side = sb("side", [128, 8, 5, 3, B])
        sqr = sb("sqr", [128, 8, 4, 3, B])
        w1 = sb("w1", [128, KCH, HID])
        w1g = sb("w1g", [128, RING, HID])
        gb = sb("gb", [128, KCH, 2])
        csum = sb("csum", [128, 2, 32, B])
        half1 = sb("half1", [128, 2, 128])
        qstat = sb("qstat", [128, 2, 10, 10, B])
        st = [sb(f"st{i}", [128, 2, 16, B]) for i in range(4)]
        g1c1 = sb("g1c1", [128, 3, 2])
        b1 = sb("b1", [128, 3])
        w2 = sb("w2", [128, 3, D])
        b2 = sb("b2", [128, D])
        hid = sb("hid", [128, 3, 512])
        img = sb("img", [128, 4, D])
        ident = sb("ident", [128, 128])
        eps = sb("eps", [128, 2])
        ids = sb("ids", [128, 8], I32)
        idf = sb("idf", [128, 2, 8])
        idc = sb("idc", [128, 8], I32)
        rows = sb("rows", [128, 8, BASIN])
        rowsT = sb("rowsT", [BASIN, 2, 512])
        projT = sb("projT", [BASIN, D])
        normw = sb("normw", [128, D])
        txt = sb("txt", [128, 8, D])
        txsq = sb("txsq", [128, D])
        rms = sb("rms", [128, 3, 8])
        psH = [pb(f"psH{m}", [128, 512]) for m in range(3)]
        psC = pb("psC", [128, 3, 2])
        psS = [pb(f"psS{i}", [128, 512]) for i in range(4)]

        x_in, w1_in, s_in, id_in = sem("x_in"), [sem(f"w1_in{i}") for i in range(3)], sem("s_in"), sem("id_in")
        pads, consts = sem("pads"), sem("consts")
        squared, sums_in, sums_out, sums_free = sem("squared"), sem("sums_in"), sem("sums_out"), sem("sums_free")
        dve, scaled, small, main = sem("dve"), sem("scaled"), sem("small"), sem("main")
        var_in, std_out = sem("var_in"), sem("std_out")
        pre_act, acted, img_ps, img_sb, stored = sem("pre_act"), sem("acted"), sem("img_ps"), sem("img_sb"), sem("stored")
        clamped, txT, txT_sb, tx_ps, tx_ss, tx_std, tx_sb = (sem(n) for n in (
            "clamped", "txT", "txT_sb", "tx_ps", "tx_ss", "tx_std", "tx_sb"))
        tx_free = sem("tx_free")

        def patches(k):
            s, c, qy = k // 6, k // 2 % 3, k % 2
            if s < 3:
                y0 = 1 + qy + (0, -1, 1)[s]
                return quad[:, y0:y0 + 7:2, :, c, :]
            x0 = s - 3
            return side[:, qy:qy + 7:2, x0:x0 + 4, c, :]

        scope = ctx.enter_context(ExitStack())
        block = scope.enter_context(nc.Block())

        @block.sync
        def _(sp):
            sp.wait_ge(pads, 1)
            sp.dma_start(quad[:, 1:9], t["x_quads"]).then_inc(x_in, 16)
            for i in range(3):
                sp.dma_start(w1[:, 10 * i:10 * i + 10], t["W1"][:, 10 * i:10 * i + 10]).then_inc(w1_in[i], 16)
            sp.wait_ge(img_sb, 4)
            for gw in range(4):
                sp.dma_start(h_tok[:, 0:PATCHES].rearrange("b (gh gw) d -> gw b gh d", gw=4)[gw],
                             img[32 * gw:32 * gw + 32]).then_inc(stored, 16)
            sp.wait_ge(tx_sb, 8)
            for q in range(4):
                sp.dma_start(h_tok[:, PATCHES:SEQ].rearrange("(i b) s d -> b s i d", b=4)[q],
                             txt[32 * q:32 * q + 32]).then_inc(stored, 16)
            sp.wait_ge(stored, 8 * 16)

        @block.gpsimd
        def _(pool):
            nc.gpsimd.memset(quad[:], 0.0)
            nc.gpsimd.memset(side[:], 0.0)
            nc.gpsimd.memset(qstat[:], 0.0).then_inc(pads, 1)
            nc.gpsimd.memset(half1[:], 1.0)
            nc.gpsimd.memset(eps[:, 0:1], LN_EPS)
            nc.gpsimd.memset(eps[:, 1:2], 1e-8)
            nc.gpsimd.memset(ident[:], 0.0).then_inc(consts, 1)
            pool.wait_ge(consts, 1)
            nc.gpsimd.affine_select(out=half1[:, 0, :], in_=half1[:, 0, :], compare_op=ALU.is_ge, fill=0.0, base=63,
                                    pattern=[[0, 128]], channel_multiplier=-1)
            nc.gpsimd.affine_select(out=half1[:, 1, :], in_=half1[:, 1, :], compare_op=ALU.is_ge, fill=0.0, base=-64,
                                    pattern=[[0, 128]], channel_multiplier=1)
            nc.gpsimd.affine_select(out=ident[:], in_=ident[:], compare_op=ALU.not_equal, fill=1.0, base=0,
                                    pattern=[[-1, 128]], channel_multiplier=1).then_inc(consts, 1)
            pool.wait_ge(clamped, 1)
            for i in range(8):
                nc.gpsimd.indirect_dma_start(rows[:, i, :], None, t["basin"],
                                             bass.IndirectOffsetOnAxis(idc[:, i:i + 1], 0)).then_inc(gathered[i // 4], 16)

        @block.scalar
        def _(act):
            act.dma_start(ids[:], t["text_ids"]).then_inc(id_in, 16)
            act.wait_ge(pads, 1)
            act.dma_start(side[0:64, :, 0:4], t["x_quads"][0:64]).then_inc(x_in, 16)
            act.dma_start(side[64:128, :, 1:5], t["x_quads"][64:128]).then_inc(x_in, 16)
            for dst, src in ((gb, "gb"), (b1, "b1"), (w2, "W2"), (projT, "txt_projT")):
                act.dma_start(dst[:], t[src]).then_inc(s_in, 16)
            for dst, src in ((b2, "b2"), (normw, "txt_norm")):
                act.dma_start(dst[:], t[src].partition_broadcast(128)).then_inc(s_in, 16)
            act.wait_ge(x_in, 48)
            nc.scalar.activation(sqr[:], quad[:, 1:9], ACT.Square).then_inc(squared, 1)
            for stat in range(2):
                act.wait_ge(sums_out, stat + 1)
                for side_ in range(2):
                    for n in range(2):
                        src = psS[2 * side_ + n][:].rearrange("p (y x b) -> p y x b", y=4, x=4)
                        dst = qstat[:, stat, 1 + 4 * n:5 + 4 * n, 1 + side_:8 + side_:2, :]
                        last = nc.scalar.activation(dst, src, ACT.Copy, scale=1.0 / (5 * 768))
                last.then_inc(sums_free, 1)
            act.wait_ge(var_in, 1)
            nc.scalar.activation(st[3][:, 1], st[3][:, 0], ACT.Sqrt, bias=eps[:, 0:1]).then_inc(std_out, 1)
            act.wait_ge(tx_ss, 1)
            nc.scalar.activation(rms[:, 1, :], rms[:, 0, :], ACT.Sqrt, bias=eps[:, 1:2],
                                 scale=1.0 / D).then_inc(tx_std, 1)
            for m in range(3):
                act.wait_ge(pre_act, m + 1)
                nc.scalar.activation(hid[:, m, :], hid[:, m, :], ACT.Gelu,
                                     bias=g1c1[:, m, 1:2]).then_inc(acted, 1)

        @block.tensor
        def _(pe):
            pe.wait_ge(consts, 2)
            for stat in range(2):
                pe.wait_ge(sums_in, stat + 1)
                if stat:
                    pe.wait_ge(sums_free, stat)
                for side_ in range(2):
                    for n in range(2):
                        last = nc.tensor.matmul(psS[2 * side_ + n][:], half1[:, side_, :],
                                                csum[:, stat, 16 * n:16 * n + 16, :], start=True, stop=True)
                last.then_inc(sums_out, 1)
            pe.wait_ge(s_in, 6 * 16)
            for m in range(3):
                for k in range(KCH):
                    pe.wait_ge(w1_in[k // 10], 16)
                    last = nc.tensor.matmul(psC[:, m, :], w1[:, k, 128 * m:128 * m + 128], gb[:, k, :],
                                            start=(k == 0), stop=(k == KCH - 1))
            last.then_inc(small, 1)
            for k in range(KCH):
                pe.wait_ge(scaled, k + 1)
                for m in range(3):
                    last = nc.tensor.matmul(psH[m][:], w1g[:, k % RING, 128 * m:128 * m + 128], patches(k),
                                            start=(k == 0), stop=(k == KCH - 1))
                last.then_inc(main, 1)
            for g in range(2):
                pe.wait_ge(gathered[g], 4 * 16)
                if g == 0:
                    pe.wait_ge(sums_free, 2)
                else:
                    pe.wait_ge(txT_sb, g)
                for i in range(4):
                    last = nc.tensor.transpose(psS[0][0:BASIN, 128 * i:128 * i + 128], rows[:, 4 * g + i, :], ident[:])
                last.then_inc(txT, 1)
                for i in range(4):
                    n = 4 * g + i
                    if i == 0:
                        pe.wait_ge(txT_sb, g + 1)
                    if n >= 3:
                        pe.wait_ge(tx_free, n - 2)
                    nc.tensor.matmul(psS[1 + n % 3][:, 0:D], rowsT[:, g, 128 * i:128 * i + 128], projT[:],
                                     start=True, stop=True).then_inc(tx_ps, 1)
            pe.wait_ge(acted, 3)
            pe.wait_ge(tx_free, 8)
            for gh in range(4):
                for m in range(3):
                    last = nc.tensor.matmul(psS[gh][:, 0:D], hid[:, m, 128 * gh:128 * gh + 128], w2[:, m, :],
                                            start=(m == 0), stop=(m == 2))
                last.then_inc(img_ps, 1)

        @block.vector
        def _(v):
            ch = Steps(v, dve)
            v.wait_ge(id_in, 16)
            ch.then(nc.vector.tensor_copy(idf[:, 0, :], ids[:]))
            ch.then(nc.vector.tensor_scalar(idf[:, 1, :], idf[:, 0, :], 0.0, float(VOCAB), ALU.is_lt, ALU.mult))
            ch.then(nc.vector.tensor_tensor(idf[:, 0, :], idf[:, 0, :], idf[:, 1, :], ALU.add))
            nc.vector.tensor_scalar(idc[:], idf[:, 0, :], 0.0, float(VOCAB - 1), ALU.max,
                                    ALU.min).then_inc(clamped, 1)
            v.wait_ge(x_in, 48)
            nc.vector.tensor_reduce(csum[:, 0], quad[:, 1:9].rearrange("p y x c b -> p (y x) b c"), X,
                                    ALU.add).then_inc(sums_in, 1)
            v.wait_ge(squared, 1)
            nc.vector.tensor_reduce(csum[:, 1], sqr[:].rearrange("p y x c b -> p (y x) b c"), X,
                                    ALU.add).then_inc(sums_in, 1)
            v.wait_ge(s_in, 6 * 16)
            for k in range(KCH):
                v.wait_ge(w1_in[k // 10], 16)
                if k >= RING:
                    v.wait_ge(main, k - RING + 1)
                nc.vector.tensor_scalar(w1g[:, k % RING, :], w1[:, k, :], gb[:, k, 0:1], None, ALU.mult).then_inc(scaled, 1)
            v.wait_ge(sums_free, 2)

            def q(stat, y, x):
                return qstat[:, stat, 1 + y:8 + y:2, 1 + x:8 + x:2, :]

            def grid(a, stat):
                return a[:, stat].rearrange("p (y x) b -> p y x b", y=4)

            def add(dst, a, b):
                for stat in range(2):
                    last = nc.vector.tensor_tensor(grid(dst, stat), a(stat), b(stat), ALU.add)
                ch.mark(last)

            def at(y, x):
                return lambda stat: q(stat, y, x)

            def of(a):
                return lambda stat: grid(a, stat)

            c0, c1, s, u = st
            add(c0, at(0, 0), at(0, 1))
            add(c1, at(1, 0), at(1, 1))
            add(s, at(-1, 0), at(-1, 1))
            add(u, at(2, 0), at(2, 1))
            ch.wait()
            add(c0, of(c0), of(c1))
            add(s, of(s), of(u))
            ch.wait()
            for dy in (0, 1):
                for dx in (-1, 2):
                    add(s, of(s), at(dy, dx))
                    ch.wait()
            ch.then(nc.vector.scalar_tensor_tensor(out=s[:], in0=c0[:], scalar=3.0, in1=s[:], op0=ALU.mult,
                                                   op1=ALU.add))
            ch.then(nc.vector.tensor_tensor(c0[:, 0], s[:, 0], s[:, 0], ALU.mult))
            nc.vector.tensor_tensor(u[:, 0], s[:, 1], c0[:, 0], ALU.subtract).then_inc(var_in, 1)
            v.wait_ge(std_out, 1)
            ch.then(nc.vector.reciprocal(c1[:, 0], u[:, 1]))
            for g in range(2):
                v.wait_ge(txT, g + 1)
                nc.vector.tensor_copy(rowsT[:, g, :], psS[0][0:BASIN, :]).then_inc(txT_sb, 1)
                for i in range(4):
                    n = 4 * g + i
                    v.wait_ge(tx_ps, n + 1)
                    nc.vector.tensor_copy(txt[:, n, :], psS[1 + n % 3][:, 0:D]).then_inc(tx_free, 1)
                    v.wait_ge(tx_free, n + 1)
                    ch.then(nc.vector.tensor_tensor_reduce(txsq[:], txt[:, n, :], txt[:, n, :], 1.0, 0.0, ALU.mult,
                                                           ALU.add, rms[:, 0, n:n + 1]))
            nc.vector.memset(rms[:, 2, 0:1], 0.0).then_inc(tx_ss, 1)
            v.wait_ge(tx_std, 1)
            ch.then(nc.vector.reciprocal(rms[:, 2, :], rms[:, 1, :]))
            for n in range(8):
                nc.vector.scalar_tensor_tensor(out=txt[:, n, :], in0=txt[:, n, :], scalar=rms[:, 2, n:n + 1],
                                               in1=normw[:], op0=ALU.mult, op1=ALU.mult).then_inc(tx_sb, 1)
            v.wait_ge(small, 1)
            ch.then(nc.vector.tensor_scalar(g1c1[:, :, 0], psC[:, :, 0], -1.0, None, ALU.mult))
            ch.then(nc.vector.tensor_tensor(g1c1[:, :, 1], psC[:, :, 1], b1[:], ALU.add))
            v.wait_ge(main, KCH)
            for m in range(3):
                ch.then(nc.vector.scalar_tensor_tensor(out=hid[:, m, :], in0=s[:, 0].rearrange("p g b -> p (g b)"),
                                                       scalar=g1c1[:, m, 0:1], in1=psH[m][:], op0=ALU.mult,
                                                       op1=ALU.add))
                nc.vector.tensor_tensor(hid[:, m, :], hid[:, m, :], c1[:, 0].rearrange("p g b -> p (g b)"),
                                        ALU.mult).then_inc(pre_act, 1)
            for gh in range(4):
                v.wait_ge(img_ps, gh + 1)
                nc.vector.tensor_tensor(img[:, gh, :], psS[gh][:, 0:D], b2[:], ALU.add).then_inc(img_sb, 1)
        scope.close()
        phase.clear()


class Phase:

    def __init__(self, nc, ctx):
        self.nc, self.ctx, self.sems = nc, ctx, []

    def sem(self, name):
        self.sems.append(self.ctx.enter_context(self.nc.semaphore(name)))
        return self.sems[-1]

    def clear(self):
        with self.nc.Block() as block:
            @block.sync
            def _(sp):
                for sem in self.sems:
                    sp.sem_clear(sem)


def spread(a, n):
    return a.unsqueeze(a.ndim).to_broadcast(list(a.shape) + [n])


def centred(nc, ch, ln_sq, ln_std, h, xc, sq, stats):
    v = nc.vector
    ch.then(v.tensor_reduce(stats[:, 0], h, X, ALU.add))
    ch.then(v.tensor_scalar(stats[:, 0], stats[:, 0], 1.0 / D, None, ALU.mult))
    ch.then(v.tensor_tensor(xc, h, spread(stats[:, 0], D), ALU.subtract))
    ch.then(v.tensor_tensor(sq, xc, xc, ALU.mult))
    v.tensor_reduce(stats[:, 1], sq, X, ALU.add).then_inc(ln_sq, 1)
    ch.eng.wait_ge(ln_std, 1)
    ch.then(v.reciprocal(stats[:, 3], stats[:, 2]))


def qkv(nc, t, keep, h_tok):
    with ExitStack() as ctx:
        def sb(name, shape, dt=F32):
            return ctx.enter_context(nc.sbuf_tensor(name, shape, dt))

        phase = Phase(nc, ctx)
        sem = phase.sem

        h, xT, qkT, fac, ident = keep["h"], keep["xT"], keep["qkT"], keep["fac"], keep["ident"]
        xc, sq = sb("xc", [HALF, PAIRS, D]), sb("sq", [HALF, PAIRS, D])
        stats = sb("stats", [HALF, 4, PAIRS])
        eps = sb("eps2", [HALF, 1])
        wqk, wg = sb("wqk", [HALF, 2, 4 * HALF]), sb("wg", [HALF, 2, GROUPS, HALF])
        bqk, bg = sb("bqk", [HALF, 4]), sb("bg", [128, HALF])
        stage = sb("stage", [HALF, 2, 2, 4, B])
        st_sb = sem("st_sb")
        ps = [ctx.enter_context(nc.psum_tensor(f"psq{i}", [128, 512], F32)) for i in range(8)]
        h_in, w_in, dve, ln_sq, ln_std, eps_set = (sem(n) for n in (
            "h_in2", "w_in2", "dve2", "ln_sq", "ln_std", "eps_set"))
        xn_ready, x_ps, x_sb, q_ps, q_sb, f_ps, f_sb = (sem(n) for n in (
            "xn_ready", "x_ps", "x_sb", "q_ps", "q_sb", "f_ps", "f_sb"))
        scope = ctx.enter_context(ExitStack())
        block = scope.enter_context(nc.Block())

        @block.sync
        def _(sp):
            sp.dma_start(h[:], h_tok.rearrange("(r b) s d -> (b s) r d", b=2)).then_inc(h_in, 16)
            for dst, src in ((wqk, "wqk"), (wg, "wqk_groups"), (bqk, "bqk"), (bg, "bqk_groups"), (ident, "ident")):
                sp.dma_start(dst[:], t[src]).then_inc(w_in, 16)

        @block.vector
        def _(v):
            ch = Steps(v, dve)
            nc.vector.memset(eps[:], LN_EPS).then_inc(eps_set, 1)
            v.wait_ge(h_in, 16)
            centred(nc, ch, ln_sq, ln_std, h[:], xc[:], sq[:], stats)
            nc.vector.tensor_tensor(sq[:], xc[:], spread(stats[:, 3], D), ALU.mult).then_inc(xn_ready, 1)
            v.wait_ge(w_in, 5 * 16)
            with v.Fori(0, 6) as i:
                for u in range(2):
                    v.wait_ge(f_ps, i * 2 + (u + 1))
                    nc.vector.tensor_tensor(
                        fac[:].rearrange("p m n -> p n m")[:, bass.ds(i * 8 + 4 * u, 4), :],
                        ps[6 + u][:, 0:4 * HALF].rearrange("p (n m) -> p n m", n=4),
                        bg[:].unsqueeze(1).to_broadcast([128, 4, HALF]), ALU.add).then_inc(f_sb, 1)

        @block.scalar
        def _(act):
            act.wait_ge(eps_set, 1)
            act.wait_ge(ln_sq, 1)
            nc.scalar.activation(stats[:, 2], stats[:, 1], ACT.Sqrt, bias=eps[:, 0:1], scale=1.0 / D).then_inc(ln_std, 1)
            for g in range(8):
                half, r = g % 2, g // 2
                act.wait_ge(x_ps, g + 1)
                nc.scalar.activation(xT[:, half, 384 * r:384 * r + 384], ps[g % 4][0:HALF, 0:384],
                                     ACT.Copy).then_inc(x_sb, 1)
            act.wait_ge(x_sb, 8)
            by_row = xT[:].rearrange("p h (b n) -> p h n b", n=SEQ)
            with act.Fori(0, 6) as i:
                for u in range(2):
                    if u == 0:
                        act.wait_ge(f_ps, i * 2)
                    nc.scalar.activation(stage[:, u], by_row[:, :, bass.ds(i * 8 + 4 * u, 4), :],
                                         ACT.Copy).then_inc(st_sb, 1)
            for g in range(12):
                oh, n = g // 3, g % 3
                act.wait_ge(q_ps, g + 1)
                nc.scalar.activation(qkT[:, oh, 512 * n:512 * n + 512], ps[g % 4][0:HALF, :], ACT.Identity,
                                     bias=bqk[:, oh:oh + 1]).then_inc(q_sb, 1)

        @block.tensor
        def _(pe):
            pe.wait_ge(xn_ready, 1)
            pe.wait_ge(w_in, 5 * 16)
            for g in range(8):
                half, r = g % 2, g // 2
                if g >= 4:
                    pe.wait_ge(x_sb, g - 3)
                for j in range(4):
                    last = nc.tensor.transpose(ps[g % 4][0:HALF, HALF * j:HALF * j + HALF],
                                               sq[:, 4 * r + j, HALF * half:HALF * half + HALF],
                                               ident[0:HALF, 0:HALF])
                last.then_inc(x_ps, 1)
            pe.wait_ge(x_sb, 8)
            with pe.Fori(0, 6) as i:
                for u in range(2):
                    pe.wait_ge(st_sb, i * 2 + (u + 1))
                    if u == 0:
                        pe.wait_ge(f_sb, i * 2)
                    for j in range(4):
                        for g in range(GROUPS):
                            for half in range(2):
                                last = nc.tensor.matmul(
                                    ps[6 + u][32 * g:32 * g + 32, HALF * j:HALF * j + HALF],
                                    stage[:, u, half, j, :],
                                    wg[:, half, g, :], start=(half == 0), stop=(half == 1))
                    last.then_inc(f_ps, 1)
            for g in range(12):
                oh, n = g // 3, g % 3
                if g >= 4:
                    pe.wait_ge(q_sb, g - 3)
                for half in range(2):
                    last = nc.tensor.matmul(ps[g % 4][0:HALF, :], wqk[:, half, HALF * oh:HALF * oh + HALF],
                                            xT[:, half, 512 * n:512 * n + 512], start=(half == 0), stop=(half == 1))
                last.then_inc(q_ps, 1)
        scope.close()
        phase.clear()


def factor(nc, t, keep, m_dram):
    with ExitStack() as ctx:
        def sb(name, shape, dt=F32):
            return ctx.enter_context(nc.sbuf_tensor(name, shape, dt))

        phase = Phase(nc, ctx)
        sem = phase.sem

        NM = 2 * GH
        A = keep["fac"][:].rearrange("p (m d) n -> p m d n", m=NM)
        tmp = sb("tmp", [128, NM * (HD - 1) * SEQ])
        n2, nrm, sg = sb("n2", [128, NM]), sb("nrm", [128, NM]), sb("sg", [128, NM])
        w, w2 = sb("wv", [128, NM, HD]), sb("wv2", [128, NM])
        rinv = sb("rinv", [128, NM, HD])
        Xk, Y, M = (sb(n, [128, GH, HD, HD]) for n in ("Xk", "Yq", "Mm"))
        dve, sq_sum, norm_out, m_ready, m_out = (sem(n) for n in ("dve3", "sq_sum", "norm_out", "m_ready", "m_out"))
        xT, qkT, v_all, kn4, qn4, qn4c = (keep[n] for n in ("xT", "qkT", "v_all", "kn4", "qn4", "qn4c"))
        qk2 = sb("qk2", [HALF, 4, TOK])
        headsum, rowmask = sb("headsum", [HALF, 64]), sb("rowmask", [128, 8])
        wv_, bv, ones1 = sb("wvT", [HALF, 2, D]), sb("bvr", [1, D]), sb("ones1", [1, SEQ])
        xst = sb("xst", [HALF, 2, 2, PAIR])
        ps = [ctx.enter_context(nc.psum_tensor(f"psf{i}", [128, 512], F32)) for i in range(8)]
        c_in, qk2_sb, n_ps, n_sb, xst_sb, v_ps, v_sb, ones_set = (sem(n) for n in (
            "c_in", "qk2_sb", "n_ps", "n_sb", "xst_sb", "v_ps", "v_sb", "ones_set"))
        scope = ctx.enter_context(ExitStack())
        block = scope.enter_context(nc.Block())

        @block.gpsimd
        def _(pool):
            nc.gpsimd.memset(keep["Mbd"][:], 0.0)
            nc.gpsimd.memset(ones1[:], 1.0).then_inc(ones_set, 1)

        @block.tensor
        def _(pe):
            pe.wait_ge(c_in, 4 * 16)
            pe.wait_ge(qk2_sb, 1)
            for qk in range(2):
                for n in range(3):
                    for half in range(2):
                        last = nc.tensor.matmul(ps[3 * qk + n][64 * half:64 * half + 64, :], headsum[:],
                                                qk2[:, 2 * qk + half, 512 * n:512 * n + 512], start=True, stop=True)
                    last.then_inc(n_ps, 1)
            pe.wait_ge(ones_set, 1)
            with pe.Fori(0, PAIRS // 2) as i:
                for u in range(2):
                    pe.wait_ge(xst_sb, i * 2 + (u + 1))
                    if u == 0:
                        pe.wait_ge(v_sb, i * 2)
                    for bb in range(2):
                        out = ps[6 + u][0:SEQ, D * bb:D * bb + D]
                        for half in range(2):
                            nc.tensor.matmul(out, xst[:, u, half, SEQ * bb:SEQ * bb + SEQ], wv_[:, half, :],
                                             start=(half == 0), stop=False)
                        last = nc.tensor.matmul(out, ones1[:], bv[:], start=False, stop=True)
                    last.then_inc(v_ps, 1)

        @block.scalar
        def _(act):
            nc.scalar.activation(qk2[:], qkT[:], ACT.Square).then_inc(qk2_sb, 1)
            for n in range(6):
                act.wait_ge(n_ps, n + 1)
                dst = (qn4 if n < 3 else kn4)[:, 512 * (n % 3):512 * (n % 3) + 512]
                nc.scalar.activation(dst, ps[n][:], ACT.Square).then_inc(n_sb, 1)
            with act.Fori(0, PAIRS // 2) as i:
                for u in range(2):
                    if u == 0:
                        act.wait_ge(v_ps, i * 2)
                    nc.scalar.activation(xst[:, u], xT[:, :, bass.ds((i * 2 + u) * PAIR, PAIR)],
                                         ACT.Copy).then_inc(xst_sb, 1)
                for u in range(2):
                    act.wait_ge(v_ps, i * 2 + (u + 1))
                    nc.scalar.activation(v_all[:, bass.ds(i * 4 + 2 * u, 2), :],
                                         ps[6 + u][0:SEQ, 0:2 * D].rearrange("p (b d) -> p b d", b=2),
                                         ACT.Copy).then_inc(v_sb, 1)
            for j in range(HD):
                act.wait_ge(sq_sum, j + 1)
                nc.scalar.activation(nrm[:], n2[:], ACT.Sqrt).then_inc(norm_out, 1)

        @block.sync
        def _(sp):
            for dst, src in ((headsum, "headsum"), (rowmask, "rowmask"), (wv_, "wv"), (bv, "bv")):
                sp.dma_start(dst[:], t[src]).then_inc(c_in, 16)
            sp.wait_ge(m_ready, 1)
            sp.dma_start(m_dram, M[:]).then_inc(m_out, 16)
            sp.wait_ge(m_out, 16)

        @block.vector
        def _(v):
            ch = Steps(v, dve)
            op = nc.vector
            ch.then(op.memset(Xk[:], 0.0))
            for j in range(HD):
                L, C = SEQ - j, HD - 1 - j
                u = A[:, :, j, j:SEQ]
                sq = tmp[:, 0:NM * L].rearrange("p (m l) -> p m l", m=NM)
                ch.then(op.tensor_tensor(sq, u, u, ALU.mult))
                op.tensor_reduce(n2[:], sq, X, ALU.add).then_inc(sq_sum, 1)
                ch.then(op.tensor_scalar(sg[:], A[:, :, j, j], 0.0, 2.0, ALU.is_ge, ALU.mult))
                v.wait_ge(norm_out, j + 1)
                nb = sg
                ch.then(op.scalar_tensor_tensor(out=nb[:], in0=sg[:], scalar=-1.0, in1=nrm[:], op0=ALU.add,
                                                op1=ALU.mult))
                ch.then(op.tensor_tensor(A[:, :, j, j], A[:, :, j, j], nb[:], ALU.add))
                ch.mark(op.tensor_scalar(rinv[:, :, j], nb[:], -1.0, None, ALU.mult))
                if C == 0:
                    ch.wait()
                    continue
                ch.mark(op.tensor_tensor(w2[:], nb[:], A[:, :, j, j], ALU.mult))
                us = u.unsqueeze(2).to_broadcast([128, NM, C, L])
                prod = tmp[:, 0:NM * C * L].rearrange("p (m c l) -> p m c l", m=NM, c=C)
                rest = A[:, :, j + 1:HD, j:SEQ]
                ch.then(op.tensor_tensor(prod, rest, us, ALU.mult))
                ch.mark(op.tensor_reduce(w[:, :, 0:C], prod, X, ALU.add))
                ch.then(op.reciprocal(w2[:], w2[:]))
                ch.then(op.tensor_tensor(w[:, :, 0:C], w[:, :, 0:C], spread(w2[:], C), ALU.mult))
                ch.then(op.tensor_tensor(prod, us, w[:, :, 0:C].unsqueeze(3).to_broadcast([128, NM, C, L]), ALU.mult))
                ch.then(op.tensor_tensor(rest, rest, prod, ALU.subtract))
            ch.then(op.reciprocal(rinv[:], rinv[:]))
            for j in range(HD - 1, -1, -1):
                C = HD - 1 - j
                ch.mark(op.tensor_copy(Xk[:, :, j, j], rinv[:, GH:NM, j]))
                if C == 0:
                    ch.wait()
                    continue
                prod = tmp[:, 0:GH * C * C].rearrange("p (m c i) -> p m c i", m=GH, c=C)
                row = A[:, GH:NM, j + 1:HD, j].unsqueeze(2).to_broadcast([128, GH, C, C])
                ch.then(op.tensor_tensor(prod, Xk[:, :, j + 1:HD, j + 1:HD], row, ALU.mult))
                ch.then(op.tensor_reduce(w[:, 0:GH, 0:C], prod, X, ALU.add, negate=True))
                ch.then(op.tensor_tensor(Xk[:, :, j + 1:HD, j], w[:, 0:GH, 0:C], spread(rinv[:, GH:NM, j], C), ALU.mult))
            for j in range(HD - 1, -1, -1):
                C = HD - 1 - j
                rhs = Xk[:, :, j, :]
                if C:
                    prod = tmp[:, 0:GH * HD * C].rearrange("p (m c i) -> p m c i", m=GH, c=HD)
                    row = A[:, 0:GH, j + 1:HD, j].unsqueeze(2).to_broadcast([128, GH, HD, C])
                    ch.then(op.tensor_tensor(prod, Y[:, :, :, j + 1:HD], row, ALU.mult))
                    ch.then(op.tensor_reduce(w[:, 0:GH, :], prod, X, ALU.add))
                    ch.then(op.tensor_tensor(w[:, 0:GH, :], rhs, w[:, 0:GH, :], ALU.subtract))
                    rhs = w[:, 0:GH, :]
                ch.then(op.tensor_tensor(Y[:, :, :, j], rhs, spread(rinv[:, 0:GH, j], HD), ALU.mult))
            op.tensor_copy(M[:].rearrange("p m a c -> p m c a"), Y[:]).then_inc(m_ready, 1)
            v.wait_ge(n_sb, 6)
            v.wait_ge(c_in, 4 * 16)
            own = rowmask[:].unsqueeze(1).to_broadcast([128, TOK // 8, 8])
            by8 = qn4[:].rearrange("p (c r) -> p c r", r=8)
            ch.then(op.tensor_tensor(by8, by8, own, ALU.mult))
            ch.then(op.tensor_reduce(qn4c[:], by8, X, ALU.add))
        scope.close()
        phase.clear()


def attend(nc, t, keep, m_dram, *to_clear):
    with ExitStack() as ctx:
        def sb(name, shape, dt=F32):
            return ctx.enter_context(nc.sbuf_tensor(name, shape, dt))

        phase = Phase(nc, ctx)
        sem = phase.sem

        qkT, v_all, kn4, qn4c, Mbd, ident, oT = (keep[n] for n in ("qkT", "v_all", "kn4", "qn4c", "Mbd", "ident", "oT"))
        mask6 = sb("mask6", [HALF, HEADS_2])
        mix, mixr, scl, bncol = sb("mix", [128, 3, HALF]), sb("mixr", [128, 2, HALF]), sb("scl", [128, 3]), sb("bncol", [HALF, 5])
        inv, bias, eps = sb("inv", [HALF, 2]), sb("bias", [HALF, 1]), sb("eps4", [128, 2])
        CLEAR = BLOCKS * 16
        zeros = sb("zeros", [128, CLEAR])
        kst = sb("kst", [HALF, 2, PAIR])
        Mst = sb("Mst", [HALF, 2, 2, HALF])
        QX, GX = sb("QX", [HALF, 2, PAIR, HEADS_2]), sb("GX", [HALF, 2, PAIR, HEADS_2])
        S = [sb(f"S{k}", [128, 2, RCH * SEQ]) for k in range(3)]
        aq, sq, wq = (sb(n, [128, 2, RCH * SEQ]) for n in ("aq", "sq4", "wq"))
        P = sb("P", [HALF, 2, RCH, SEQ])
        mx, rs = sb("mx", [HALF, 2, RCH]), sb("rs", [HALF, 2, 2, RCH])
        pT, vst, osb = sb("pT", [SEQ, 2, SEQ * HEADS]), sb("vst", [SEQ, 2, D]), sb("osb", [SEQ, 2, D])
        psS = ctx.enter_context(nc.psum_tensor("psSc", [128, 2, 2, 512], F32))
        psY = ctx.enter_context(nc.psum_tensor("psY", [128, 2, 512], F32))
        psX = ctx.enter_context(nc.psum_tensor("psX", [128, 2, 512], F32))
        W = RCH * SEQ
        Yv, Tv = psY[0:HALF, :, 0:W], psX[0:SEQ, :, 0:W]
        psA = psX[0:HALF, 0, 0:D].rearrange("p (h n) -> p h n", h=2)
        psO = psY[0:SEQ, 0, 0:2 * D].rearrange("p (b d) -> p b d", b=2)
        psOT = psY[0:HALF, 1, 0:D].rearrange("p (h n) -> p h n", h=2)

        names = ("c_in4 m_in zeros cleared dve4 dve4b sk_ps gaps inv_in inv_std mix_set m_st a_ps qx gx s_ps s_sq s_g s_k a_sb w_sb s_r y_ps "
                 "z_sb e_sb p_sb t_ps t_sb v_st o_ps o_sb ot_ps ot_sb").split()
        q = {n: sem("at_" + n) for n in names}
        scope = ctx.enter_context(ExitStack())
        block = scope.enter_context(nc.Block())

        def pair(a, p, axis_len=PAIR):
            return a[:, :, bass.ds(p * axis_len, axis_len)]

        @block.sync
        def _(sp):
            for dst, src in ((mask6, "mask6"), (mix, "mix"), (bncol, "bncol")):
                sp.dma_start(dst[:], t[src]).then_inc(q["c_in4"], 16)
            for dst, src in ((mixr, "bnrow"), (scl, "scales")):
                sp.dma_start(dst[:], t[src].partition_broadcast(128)).then_inc(q["c_in4"], 16)
            for half in range(2):
                for h in range(HEADS_2):
                    g, m = divmod(HEADS_2 * half + h, GH)
                    sp.dma_start(Mbd[HD * h:HD * h + HD, half, :, HD * h:HD * h + HD],
                                 m_dram[B * g:B * g + B, m].rearrange("b a c -> a b c")).then_inc(q["m_in"], 16)
            sp.wait_ge(q["zeros"], 1)
            for dram in to_clear:
                rows = dram.rearrange("(p r) d -> p (r d)", p=128)
                for n in range(0, rows.shape[1], CLEAR):
                    sp.dma_start(rows[:, n:n + CLEAR], zeros[:]).then_inc(q["cleared"], 16)
            sp.wait_ge(q["cleared"], 16 * sum(dram.shape[0] * dram.shape[1] // (128 * CLEAR) for dram in to_clear))

        @block.gpsimd
        def _(pool):
            def head(p):
                pool.wait_ge(q["a_ps"], p)
                nc.gpsimd.tensor_copy(Mst[:], Mbd[:, :, bass.ds(p * 2, 2), :]).then_inc(q["m_st"], 1)
                pool.wait_ge(q["s_ps"], p)
                nc.gpsimd.tensor_copy(kst[:], pair(qkT[:, 2:4], p))
                nc.gpsimd.tensor_tensor(QX[:], spread(pair(qkT[:, 0:2], p), HEADS_2),
                                        mask6[:].unsqueeze(1).unsqueeze(1).to_broadcast([HALF, 2, PAIR, HEADS_2]),
                                        ALU.mult).then_inc(q["qx"], 1)
                pool.wait_ge(q["w_sb"], p)
                nc.gpsimd.tensor_tensor(
                    aq[:].rearrange("p b (c m) -> p b c m", c=RCH),
                    kn4[:, bass.ds(p * PAIR, PAIR)].rearrange("p (b m) -> p b m", b=2).unsqueeze(2).to_broadcast([128, 2, RCH, SEQ]),
                    spread(qn4c[:, bass.ds(p * 2 * RCH, 2 * RCH)].rearrange("p (b c) -> p b c", b=2), SEQ),
                    ALU.add).then_inc(q["a_sb"], 1)

            def tail(p):
                pool.wait_ge(q["o_ps"], p * 2)
                nc.gpsimd.tensor_copy(vst[:], v_all[:, bass.ds(p * 2, 2), :]).then_inc(q["v_st"], 1)

            nc.gpsimd.memset(zeros[:], 0.0).then_inc(q["zeros"], 1)
            pool.wait_ge(q["c_in4"], 5 * 16)
            pool.wait_ge(q["m_in"], 12 * 16)
            head(0)
            with pool.Fori(0, PAIRS - 1) as i:
                tail(i)
                head(i + 1)
            tail(PAIRS - 1)

        @block.tensor
        def _(pe):
            def head(p):
                pe.wait_ge(q["m_st"], p + 1)
                for half in range(2):
                    for bb in range(2):
                        last = nc.tensor.matmul(psA[:, half, SEQ * bb:SEQ * bb + SEQ], Mst[:, half, bb, :],
                                                qkT[:, half, bass.ds((p * 2 + bb) * SEQ, SEQ)], start=True, stop=True)
                last.then_inc(q["a_ps"], 1)
                pe.wait_ge(q["s_sq"], p)
                pe.wait_ge(q["s_g"], p)
                pe.wait_ge(q["s_k"], p)
                pe.wait_ge(q["qx"], p + 1)
                for kind, rows, ready in ((0, QX, None), (1, GX, "gx")):
                    if ready:
                        pe.wait_ge(q[ready], p + 1)
                    for bb in range(2):
                        for c in range(RCH):
                            for half in range(2):
                                last = nc.tensor.matmul(
                                    psS[64 * half:64 * half + SEQ, kind, bb, SEQ * c:SEQ * c + SEQ],
                                    rows[:, half, SEQ * bb + 8 * c:SEQ * bb + 8 * c + 8, :].rearrange("p n h -> p (n h)"),
                                    kst[:, half, SEQ * bb:SEQ * bb + SEQ], start=True, stop=True)
                    last.then_inc(q["s_ps"] if kind else q["sk_ps"], 1)

            def tail_mix(p):
                pe.wait_ge(q["s_r"], p + 1)
                pe.wait_ge(q["s_g"], p + 1)
                pe.wait_ge(q["s_k"], p + 1)
                pe.wait_ge(q["o_sb"], p)
                pe.wait_ge(q["ot_sb"], p)
                for bb in range(2):
                    for k in range(3):
                        last = nc.tensor.matmul(Yv[:, bb, :], mix[:, k, :], S[k][:, bb, :], start=(k == 0), stop=(k == 2))
                last.then_inc(q["y_ps"], 1)

            def tail_values(p):
                pe.wait_ge(q["p_sb"], p + 1)
                pe.wait_ge(q["v_st"], p + 1)
                pe.wait_ge(q["z_sb"], p + 1)
                for bb in range(2):
                    pe.wait_ge(q["t_sb"], p * 2 + bb)
                    nc.tensor.transpose(psX[0:HALF, 0, 0:HALF], P[:, bb, 0:2, :].rearrange("p c m -> p (c m)"),
                                        ident[0:HALF, 0:HALF])
                    for c in range(1, RCH):
                        last = nc.tensor.transpose(Tv[:, c // 3, HALF * (c % 3):HALF * (c % 3) + HALF], P[:, bb, c, :],
                                                   ident[0:HALF, 0:HALF])
                    last.then_inc(q["t_ps"], 1)
                    pe.wait_ge(q["t_sb"], p * 2 + (bb + 1))
                    nc.tensor.matmul(psY[0:HALF, 0, 2 * D:2 * D + 1], pT[:, bb, 0:HALF], vst[:, bb, 0:1],
                                     start=True, stop=True)
                    for o in range(HEADS):
                        last = nc.tensor.matmul(psO[:, bb, HD * o:HD * o + HD], pT[:, bb, o:SEQ * HEADS:HEADS],
                                                vst[:, bb, HD * o:HD * o + HD], start=True, stop=True)
                    last.then_inc(q["o_ps"], 1)
                pe.wait_ge(q["o_sb"], p + 1)
                for half in range(2):
                    for bb in range(2):
                        last = nc.tensor.matmul(psOT[:, half, SEQ * bb:SEQ * bb + SEQ],
                                                osb[:, bb, HALF * half:HALF * half + HALF], ident[0:SEQ, 0:SEQ],
                                                start=True, stop=True)
                last.then_inc(q["ot_ps"], 1)

            pe.wait_ge(q["gaps"], 1)
            pe.wait_ge(q["mix_set"], 1)
            head(0)
            with pe.Fori(0, PAIRS - 1) as i:
                tail_mix(i)
                head(i + 1)
                tail_values(i)
            tail_mix(PAIRS - 1)
            tail_values(PAIRS - 1)

        @block.scalar
        def _(act):
            def head(p):
                act.wait_ge(q["sk_ps"], p + 1)
                act.wait_ge(q["w_sb"], p)
                nc.scalar.activation(sq[:], psS[:, 0, :, 0:W], ACT.Square, scale=float(np.sqrt(2.0))).then_inc(q["s_sq"], 1)
                act.wait_ge(q["y_ps"], p)
                nc.scalar.activation(S[0][:], psS[:, 0, :, 0:W], ACT.Copy).then_inc(q["s_k"], 1)
                act.wait_ge(q["s_ps"], p + 1)
                nc.scalar.activation(S[2][:], psS[:, 1, :, 0:W], ACT.Square).then_inc(q["s_g"], 1)

            def roots(p):
                act.wait_ge(q["w_sb"], p + 1)
                nc.scalar.activation(S[1][:], wq[:], ACT.Sqrt).then_inc(q["s_r"], 1)

            def tail_exp(p):
                act.wait_ge(q["z_sb"], p + 1)
                nc.scalar.activation(P[:], P[:], ACT.Exp).then_inc(q["e_sb"], 1)

            def tail_turned(p):
                for bb in range(2):
                    act.wait_ge(q["t_ps"], p * 2 + (bb + 1))
                    act.wait_ge(q["o_ps"], p * 2)
                    nc.scalar.activation(pT[:, bb, :].rearrange("p (a n) -> p a n", a=2), Tv, ACT.Copy).then_inc(q["t_sb"], 1)

            act.wait_ge(q["inv_in"], 1)
            act.wait_ge(q["c_in4"], 5 * 16)
            nc.scalar.activation(mixr[:, 1, :], mixr[:, 1, :], ACT.Sqrt, bias=eps[:, 0:1])
            nc.scalar.activation(inv[:, 0:1], bncol[:, 4:5], ACT.Sqrt, bias=eps[0:HALF, 0:1]).then_inc(q["inv_std"], 1)
            head(0)
            roots(0)
            with act.Fori(0, PAIRS - 1) as i:
                tail_exp(i)
                head(i + 1)
                tail_turned(i)
                roots(i + 1)
            tail_exp(PAIRS - 1)
            tail_turned(PAIRS - 1)

        @block.vector
        def _(v):
            op = nc.vector

            def head_rows(p):
                v.wait_ge(q["a_ps"], p + 1)
                v.wait_ge(q["s_ps"], p)
                op.tensor_tensor(GX[:], spread(psA, HEADS_2),
                                 mask6[:].unsqueeze(1).unsqueeze(1).to_broadcast([HALF, 2, PAIR, HEADS_2]),
                                 ALU.mult).then_inc(q["gx"], 1)

            def head_riem(p, ch):
                v.wait_ge(q["s_sq"], p + 1)
                v.wait_ge(q["a_sb"], p + 1)
                v.wait_ge(q["s_r"], p)
                ch.then(op.tensor_tensor(wq[:], aq[:], sq[:], ALU.subtract))
                op.tensor_scalar(wq[:], wq[:], 0.0, 1e-8, ALU.max, ALU.add).then_inc(q["w_sb"], 1)

            def tail_max(p, ch):
                v.wait_ge(q["y_ps"], p + 1)
                Y = Yv.rearrange("p b (c m) -> p b c m", c=RCH)
                ch.then(op.tensor_reduce(mx[:], Y, X, ALU.max))
                ch.then(op.tensor_scalar(mx[:], mx[:], bias[:, 0:1], None, ALU.add))
                v.wait_ge(q["t_ps"], p * 2)
                for bb in range(2):
                    last = op.scalar_tensor_tensor(out=P[:, bb], in0=Y[:, bb], scalar=bias[:, 0:1],
                                                   in1=spread(mx[:, bb], SEQ), op0=ALU.add, op1=ALU.subtract)
                last.then_inc(q["z_sb"], 1)

            def tail_norm(p, ch):
                v.wait_ge(q["e_sb"], p + 1)
                ch.then(op.tensor_reduce(rs[:, 0], P[:], X, ALU.add))
                ch.then(op.reciprocal(rs[:, 1], rs[:, 0]))
                flat = P[:].rearrange("p b c m -> p (b c) m")
                op.tensor_tensor(flat, flat, spread(rs[:, 1].rearrange("p b c -> p (b c)"), SEQ), ALU.mult).then_inc(q["p_sb"], 1)

            def tail_out(p):
                v.wait_ge(q["o_ps"], p * 2 + 2)
                v.wait_ge(q["ot_ps"], p)
                op.tensor_copy(osb[:], psO).then_inc(q["o_sb"], 1)
                v.wait_ge(q["ot_ps"], p + 1)
                op.tensor_copy(pair(oT[:], p), psOT).then_inc(q["ot_sb"], 1)

            op.memset(psS[:], 0.0).then_inc(q["gaps"], 1)
            op.memset(eps[:], LN_EPS).then_inc(q["inv_in"], 1)
            ch = Steps(v, q["dve4"])
            v.wait_ge(q["c_in4"], 5 * 16)
            v.wait_ge(q["inv_std"], 1)
            ch.mark(op.reciprocal(mixr[:, 1, :], mixr[:, 1, :]))
            ch.then(op.reciprocal(inv[:, 1:2], inv[:, 0:1]))
            ch.mark(op.tensor_tensor(mixr[:, 0, :], mixr[:, 0, :], mixr[:, 1, :], ALU.mult))
            ch.mark(op.tensor_tensor(inv[:, 1:2], inv[:, 1:2], bncol[:, 2:3], ALU.mult))
            ch.mark(op.tensor_scalar(scl[:, 1:2], scl[:, 1:2], -1.0, None, ALU.mult))
            ch.then(op.tensor_tensor(bias[:], bncol[:, 0:1], bncol[:, 1:2], ALU.subtract))
            ch.then(op.scalar_tensor_tensor(out=bias[:], in0=bias[:], scalar=inv[:, 1:2], in1=bncol[:, 3:4],
                                            op0=ALU.mult, op1=ALU.add))
            for k in range(3):
                last = op.scalar_tensor_tensor(out=mix[:, k, :], in0=mix[:, k, :], scalar=scl[:, k:k + 1],
                                               in1=mixr[:, 0, :], op0=ALU.mult, op1=ALU.mult)
            last.then_inc(q["mix_set"], 1)
            ch = Steps(v, q["dve4b"])
            head_rows(0)
            head_riem(0, ch)
            PER = 5
            with v.Fori(0, PAIRS - 1) as i:
                ch = Steps(v, q["dve4b"], base=1, turn=i, per=PER)
                tail_max(i, ch)
                head_rows(i + 1)
                tail_norm(i, ch)
                head_riem(i + 1, ch)
                tail_out(i)
                assert ch.n == PER
            ch = Steps(v, q["dve4b"], base=1 + PER * (PAIRS - 1))
            tail_max(PAIRS - 1, ch)
            tail_norm(PAIRS - 1, ch)
            tail_out(PAIRS - 1)
        scope.close()
        phase.clear()


def route(nc, t, keep, xn_dram):
    with ExitStack() as ctx:
        def sb(name, shape, dt=F32):
            return ctx.enter_context(nc.sbuf_tensor(name, shape, dt))

        h, xT, oT, ident = keep["h"], keep["xT"], keep["oT"], keep["ident"]
        pos, w4, eid, xr = keep["pos"], keep["w4"], keep["eid"], keep["rows_in"]
        xc, sq, stats = sb("xc5", [HALF, PAIRS, D]), sb("sq5", [HALF, PAIRS, D]), sb("stats5", [HALF, 4, PAIRS])
        projT, projb = sb("projT5", [HALF, 2, D]), sb("projb5", [1, D])
        ones = sb("ones5", [128, 128])
        eps = sb("eps5", [128, 1])
        Wf, bf = sb("Wf", [HALF, 2, 128]), sb("bf", [128, 1])
        emb, emb2, est = sb("emb", [128, 2, 64]), sb("emb2", [128, 2, 64]), sb("est", [128, 3, 2])
        embT, fT = sb("embT", [128, 128]), sb("fT", [128, TOK])
        upper, iota = sb("upper", [128, 128]), sb("iota", [128, BLOCKS])
        L, prod = sb("L", [128, FT, 2, NEUR]), sb("prod5", [128, FT, 2, NEUR])
        O = [sb(f"O{k}", [128, FT, 2, NEUR]) for k in range(TOPK)]
        cum = sb("cum", [128, FT, 2 * NEUR])
        red, vals, idx, idf = (sb("red", [128, 2, 2 * FT]), sb("vals", [128, 2 * FT, 8]),
                               sb("idx", [128, 2 * FT, 8], U32), sb("idf5", [128, 2 * FT, TOPK]))
        posf = sb("posf", [128, 2 * FT, TOPK])
        cnt, cnti, nbf = sb("cnt", [128, 2]), sb("cnti", [128, 2, 2], I32), sb("nbf", [128, 2])
        nbw, start, endc = sb("nbw", [128, 2, NEUR]), sb("start", [128, 2 * NEUR]), sb("endc", [128, 2])
        gt, ef = sb("gt", [128, 2, BLOCKS]), sb("ef", [1, 2 * BLOCKS])
        ps = [ctx.enter_context(nc.psum_tensor(f"psr{i}", [128, 512], F32)) for i in range(8)]
        names = ("c_in dve set_up o_ps h_sb ln_sq ln_std xn xn_out xr_in x_ps x_sb e_sq e_std e_n e_ps e_sb f_ps f_sb "
                 "l_ps l_sb l_sub l_exp chosen cums r_ps r_sb c_ps nb st_ps en_ps gts b_ps st_sb").split()
        phase = Phase(nc, ctx)
        q = {n: phase.sem("rt_" + n) for n in names}
        LBANK = [0, 3, 1, 5, 2, 6]
        scope = ctx.enter_context(ExitStack())
        block = scope.enter_context(nc.Block())

        @block.sync
        def _(sp):
            for dst, src in ((projT, "attn_projT"), (projb, "attn_projb"), (Wf, "Wf"), (bf, "bf"), (emb, "emb"),
                             (upper, "upper"), (iota, "iota")):
                sp.dma_start(dst[:], t[src]).then_inc(q["c_in"], 16)
            sp.wait_ge(q["xn"], 1)
            sp.dma_start(xn_dram.rearrange("(r p) d -> p r d", p=PAIR), sq[:]).then_inc(q["xn_out"], 16)
            sp.wait_ge(q["xn_out"], 16)
            sp.dma_start(xr[:], xn_dram.rearrange("(t p) d -> p t d", p=128)).then_inc(q["xr_in"], 16)
            sp.wait_ge(q["xr_in"], 16)

        @block.tensor
        def _(pe):
            pe.wait_ge(q["c_in"], 7 * 16)
            pe.wait_ge(q["set_up"], 1)
            for g in range(8):
                if g >= 4:
                    pe.wait_ge(q["h_sb"], g - 3)
                for j in range(2):
                    out = ps[g % 4][0:HALF, D * j:D * j + D]
                    for half in range(2):
                        nc.tensor.matmul(out, oT[:, half, PAIR * (2 * g + j):PAIR * (2 * g + j + 1)], projT[:, half, :],
                                         start=(half == 0), stop=False)
                    last = nc.tensor.matmul(out, ones[0:1, 0:HALF], projb[:], start=False, stop=True)
                last.then_inc(q["o_ps"], 1)
            pe.wait_ge(q["e_n"], 1)
            nc.tensor.transpose(ps[4][:, 0:128], emb2[:].rearrange("p f d -> p (f d)"), ident[:]).then_inc(q["e_ps"], 1)
            pe.wait_ge(q["xn"], 1)
            for g in range(8):
                half, r = g % 2, g // 2
                if g < 4:
                    pe.wait_ge(q["h_sb"], 5 + g)
                else:
                    pe.wait_ge(q["x_sb"], g - 3)
                for j in range(4):
                    last = nc.tensor.transpose(ps[g % 4][0:HALF, HALF * j:HALF * j + HALF],
                                               sq[:, 4 * r + j, HALF * half:HALF * half + HALF], ident[0:HALF, 0:HALF])
                last.then_inc(q["x_ps"], 1)
            pe.wait_ge(q["x_sb"], 8)
            for n in range(3):
                for half in range(2):
                    last = nc.tensor.matmul(ps[5 + n][:], Wf[:, half, :], xT[:, half, 512 * n:512 * n + 512],
                                            start=(half == 0), stop=(half == 1))
                last.then_inc(q["f_ps"], 1)
            pe.wait_ge(q["e_sb"], 1)
            pe.wait_ge(q["f_sb"], 3)
            for g in range(6):
                n, f = g // 2, g % 2
                for j in range(4):
                    last = nc.tensor.matmul(ps[LBANK[g]][:, 128 * j:128 * j + 128],
                                            fT[64 * f:64 * f + 64, 128 * (4 * n + j):128 * (4 * n + j + 1)],
                                            embT[64 * f:64 * f + 64, :], start=True, stop=True)
                last.then_inc(q["l_ps"], 1)
            pe.wait_ge(q["cums"], 1)
            nc.tensor.matmul(ps[4][:, 0:1], cum[:, FT - 1, 0:NEUR], ones[:, 0:1], start=True, stop=True)
            nc.tensor.matmul(ps[4][:, 1:2], cum[:, FT - 1, NEUR:], ones[:, 0:1], start=True, stop=True).then_inc(q["c_ps"], 1)
            pe.wait_ge(q["nb"], 1)
            for f in range(2):
                last = nc.tensor.matmul(ps[5][:, 128 * f:128 * f + 128], nbw[:, f, :], upper[:], start=True, stop=True)
            last.then_inc(q["st_ps"], 1)
            nc.tensor.matmul(ps[6][:, 0:2], upper[:], nbf[:], start=True, stop=False)
            nc.tensor.matmul(ps[6][:, 0:2], ident[:], nbf[:], start=False, stop=True).then_inc(q["en_ps"], 1)
            for i in range(FT):
                if i < 4:
                    pe.wait_ge(q["l_sb"], 6)
                else:
                    pe.wait_ge(q["r_sb"], i - 3)
                last = nc.tensor.matmul(ps[i % 4][:, 0:256], upper[:], L[:, i].rearrange("p f e -> p (f e)"), start=True,
                                        stop=(i == 0))
                if i:
                    last = nc.tensor.matmul(ps[i % 4][:, 0:256], ones[:], cum[:, i - 1, :], start=False, stop=True)
                last.then_inc(q["r_ps"], 1)
            pe.wait_ge(q["gts"], 1)
            nc.tensor.matmul(ps[7][0:1, 0:2 * BLOCKS], ones[:, 0:1], gt[:].rearrange("p f j -> p (f j)"), start=True,
                             stop=True).then_inc(q["b_ps"], 1)

        @block.scalar
        def _(act):
            act.wait_ge(q["set_up"], 1)
            act.wait_ge(q["e_sq"], 1)
            nc.scalar.activation(est[:, 1], est[:, 0], ACT.Sqrt).then_inc(q["e_std"], 1)
            act.wait_ge(q["ln_sq"], 1)
            nc.scalar.activation(stats[:, 2], stats[:, 1], ACT.Sqrt, bias=eps[0:HALF], scale=1.0 / D).then_inc(q["ln_std"], 1)
            act.wait_ge(q["e_ps"], 1)
            nc.scalar.activation(embT[:], ps[4][:, 0:128], ACT.Copy).then_inc(q["e_sb"], 1)
            for g in range(8):
                half, r = g % 2, g // 2
                act.wait_ge(q["x_ps"], g + 1)
                nc.scalar.activation(xT[:, half, 384 * r:384 * r + 384], ps[g % 4][0:HALF, 0:384],
                                     ACT.Copy).then_inc(q["x_sb"], 1)
            for n in range(3):
                act.wait_ge(q["f_ps"], n + 1)
                nc.scalar.activation(fT[:, 512 * n:512 * n + 512], ps[5 + n][:], ACT.Identity,
                                     bias=bf[:]).then_inc(q["f_sb"], 1)
            for g in range(6):
                act.wait_ge(q["l_ps"], g + 1)
                nc.scalar.activation(L[:, 4 * (g // 2):4 * (g // 2) + 4, g % 2, :],
                                     ps[LBANK[g]][:].rearrange("p (t e) -> p t e", t=4), ACT.Copy).then_inc(q["l_sb"], 1)
            act.wait_ge(q["l_sub"], 1)
            nc.scalar.activation(L[:], L[:], ACT.Exp).then_inc(q["l_exp"], 1)

        @block.vector
        def _(v):
            op = nc.vector
            ch = Steps(v, q["dve"])
            ch.then(op.memset(ones[:], 1.0))
            op.memset(eps[:], LN_EPS).then_inc(q["set_up"], 1)
            v.wait_ge(q["c_in"], 7 * 16)
            ch.then(op.tensor_tensor(emb2[:], emb[:], emb[:], ALU.mult))
            op.tensor_reduce(est[:, 0], emb2[:], X, ALU.add).then_inc(q["e_sq"], 1)
            v.wait_ge(q["e_std"], 1)
            ch.then(op.tensor_scalar(est[:, 1], est[:, 1], 1e-8, None, ALU.add))
            ch.then(op.reciprocal(est[:, 2], est[:, 1]))
            op.tensor_tensor(emb2[:], emb[:], spread(est[:, 2], 64), ALU.mult).then_inc(q["e_n"], 1)
            for g in range(8):
                v.wait_ge(q["o_ps"], g + 1)
                hh = h[:, 2 * g:2 * g + 2, :]
                op.tensor_tensor(hh, hh, ps[g % 4][0:HALF, 0:2 * D].rearrange("p (r d) -> p r d", r=2),
                                 ALU.add).then_inc(q["h_sb"], 1)
            v.wait_ge(q["h_sb"], 8)
            centred(nc, ch, q["ln_sq"], q["ln_std"], h[:], xc[:], sq[:], stats)
            op.tensor_tensor(sq[:], xc[:], spread(stats[:, 3], D), ALU.mult).then_inc(q["xn"], 1)
            v.wait_ge(q["l_sb"], 6)
            rows = L[:].rearrange("p t f e -> p (t f) e")
            prod3 = prod[:].rearrange("p t f e -> p (t f) e")
            ch.then(op.tensor_reduce(red[:, 0], rows, X, ALU.max))
            op.tensor_tensor(rows, rows, spread(red[:, 0], NEUR), ALU.subtract).then_inc(q["l_sub"], 1)
            v.wait_ge(q["l_exp"], 1)
            ch.then(op.tensor_reduce(red[:, 0], rows, X, ALU.add))
            ch.then(op.reciprocal(red[:, 1], red[:, 0]))
            ch.then(op.tensor_tensor(rows, rows, spread(red[:, 1], NEUR), ALU.mult))
            for r in range(2 * FT):
                ch.mark(op.max(vals[:, r, :], rows[:, r, :]))
            ch.wait()
            for r in range(2 * FT):
                ch.mark(op.max_index(idx[:, r, :], vals[:, r, :], rows[:, r, :]))
            ch.mark(op.tensor_reduce(red[:, 0], vals[:, :, 0:TOPK], X, ALU.add))
            ch.wait()
            ch.mark(op.tensor_copy(idf[:], idx[:, :, 0:TOPK]))
            ch.then(op.tensor_scalar(red[:, 0], red[:, 0], 1e-8, None, ALU.add))
            ch.then(op.reciprocal(red[:, 1], red[:, 0]))
            ch.mark(op.tensor_tensor(w4[:], vals[:, :, 0:TOPK], spread(red[:, 1], TOPK), ALU.mult))
            for k in range(TOPK):
                ch.mark(op.tensor_tensor(O[k][:].rearrange("p t f e -> p (t f) e"),
                                         iota[:, 0:NEUR].unsqueeze(1).to_broadcast([128, 2 * FT, NEUR]),
                                         spread(idf[:, :, k], NEUR), ALU.is_equal))
            ch.wait()
            ch.mark(op.tensor_tensor(L[:], O[0][:], O[1][:], ALU.add))
            ch.then(op.tensor_tensor(prod[:], O[2][:], O[3][:], ALU.add))
            ch.then(op.tensor_tensor(L[:], L[:], prod[:], ALU.add))
            by_tile = L[:].rearrange("p t f e -> p t (f e)")
            ch.then(op.tensor_copy(cum[:, 0, :], by_tile[:, 0]))
            for i in range(1, FT):
                ch.then(op.tensor_tensor(cum[:, i, :], cum[:, i - 1, :], by_tile[:, i], ALU.add))
            op.memset(red[:, 0, 0:1], 0.0).then_inc(q["cums"], 1)
            v.wait_ge(q["c_ps"], 1)
            ch.then(op.tensor_scalar(cnt[:], ps[4][:, 0:2], float(SLOT - 1), None, ALU.add))
            ch.then(op.tensor_copy(cnti[:, 0], cnt[:]))
            ch.then(op.tensor_scalar(cnti[:, 1], cnti[:, 0], 7, None, ALU.arith_shift_right))
            ch.then(op.tensor_copy(nbf[:], cnti[:, 1]))
            op.tensor_copy(nbw[:], spread(nbf[:], NEUR)).then_inc(q["nb"], 1)
            v.wait_ge(q["st_ps"], 1)
            ch.mark(op.tensor_scalar(start[:], ps[5][:, 0:256], float(SLOT), None, ALU.mult))
            v.wait_ge(q["en_ps"], 1)
            ch.then(op.tensor_copy(endc[:], ps[6][:, 0:2]))
            for f in range(2):
                last = op.tensor_scalar(gt[:, f, :], iota[:], endc[:, f:f + 1], None, ALU.is_ge)
            last.then_inc(q["gts"], 1)
            for i in range(FT):
                v.wait_ge(q["r_ps"], min(i + 2, FT))
                op.tensor_tensor(cum[:, i, :], ps[i % 4][:, 0:256], start[:], ALU.add).then_inc(q["r_sb"], 1)
            v.wait_ge(q["r_sb"], FT)
            places = cum[:].rearrange("p t (f e) -> p t f e", f=2)
            for k in range(TOPK):
                ch.then(op.tensor_tensor(prod[:], O[k][:], places, ALU.mult))
                ch.then(op.tensor_reduce(posf[:, :, k], prod3, X, ALU.add))
            ch.mark(op.tensor_copy(pos[:], posf[:]))
            v.wait_ge(q["b_ps"], 1)
            ch.then(op.tensor_scalar(ef[:], ps[7][0:1, 0:2 * BLOCKS], float(NEUR - 1), None, ALU.min))
            ch.then(op.tensor_copy(eid[:], ef[:]))
        scope.close()
        phase.clear()


def routed(nc, t, keep, bank, scat, gath, w_in, w_out, slots_in, slots_out, weights, out_rows):
    HW = min(w_in, HALF) if w_in == D else w_in
    PARTS = w_in // HW
    GRP, PPG = UNR // 2, UNR // 4
    PPT = UNR // 2
    TURNS = BLOCKS // UNR
    with ExitStack() as ctx:
        def sb(name, shape, dt=F32):
            return ctx.enter_context(nc.sbuf_tensor(f"{name}_b{bank}", shape, dt))

        rows_in, pos, w4, eid, ident = (keep[n] for n in ("rows_in", "pos", "w4", "eid", "ident"))
        xb = [sb(f"xb{g}", [SLOT, GRP, w_in]) for g in range(2)]
        yb = [sb(f"yb{g}", [SLOT, GRP, w_out]) for g in range(2)]
        wb = [sb(f"wb{u}", [HW, PARTS, w_out]) for u in range(UNR)]
        xT = [sb(f"xbT{p}", [HW, 2, PARTS, SLOT]) for p in range(4)]
        got = sb("got", [128, FT, TOPK, w_out])
        psT = [ctx.enter_context(nc.psum_tensor(f"psT{bank}_{p}", [128, 512], F32)) for p in range(4)]
        psO = [ctx.enter_context(nc.psum_tensor(f"psO{bank}_{p}", [128, 512], F32)) for p in range(4)]

        phase = Phase(nc, ctx)

        def sem(n):
            return phase.sem(f"rd{bank}_{n}")

        x_ld, st = ([sem(f"{n}{g}") for g in range(2)] for n in ("x_ld", "st"))
        w_ld = [sem(f"w_ld{p}") for p in range(PPT)]
        t_ps, t_sb, y_ps, y_sb, acc = (sem(n) for n in ("t_ps", "t_sb", "y_ps", "y_sb", "acc"))
        scope = ctx.enter_context(ExitStack())
        block = scope.enter_context(nc.Block())

        @block.gpsimd
        def _(pool):
            for i in range(FT):
                for k in range(TOPK):
                    nc.gpsimd.indirect_dma_start(slots_in, bass.IndirectOffsetOnAxis(pos[:, 2 * i + bank, k:k + 1], 0),
                                                 rows_in[:, i, 0:w_in], None).then_inc(scat, 16)
            for g in range(2):
                pool.wait_ge(st[g], 16 * TURNS)
            for k in range(TOPK):
                for i in range(FT):
                    nc.gpsimd.indirect_dma_start(got[:, i, k, :], None, slots_out,
                                                 bass.IndirectOffsetOnAxis(pos[:, 2 * i + bank, k:k + 1], 0)).then_inc(gath[k], 16)

        @block.sync
        def _(sp):
            def load_x(turn, g):
                sp.dma_start(xb[g][:], slots_in[bass.ds((turn * UNR + GRP * g) * SLOT, GRP * SLOT), :].rearrange(
                    "(j p) d -> p j d", p=SLOT)).then_inc(x_ld[g], 16)

            def load_w(turn, p):
                for j in (2 * p, 2 * p + 1):
                    e = sp.value_load(eid[0:1, bass.ds(turn * UNR + (j + bank * BLOCKS), 1)], min_val=0, max_val=NEUR - 1)
                    sp.dma_start(wb[j][:], weights[bass.ds(e, 1)].rearrange("e (c p) n -> p (e c) n", p=HW)).then_inc(w_ld[p], 16)

            def load_w_first(p):
                for j in (2 * p, 2 * p + 1):
                    e = sp.value_load(eid[0:1, j + bank * BLOCKS:j + bank * BLOCKS + 1], min_val=0, max_val=NEUR - 1)
                    sp.dma_start(wb[j][:], weights[bass.ds(e, 1)].rearrange("e (c p) n -> p (e c) n", p=HW)).then_inc(w_ld[p], 16)

            for p in range(PPT):
                load_w_first(p)
            sp.wait_ge(scat, 16 * FT * TOPK)
            for g in range(2):
                sp.dma_start(xb[g][:], slots_in[GRP * g * SLOT:GRP * (g + 1) * SLOT, :].rearrange(
                    "(j p) d -> p j d", p=SLOT)).then_inc(x_ld[g], 16)
            with sp.Fori(0, TURNS - 1) as i:
                for p in range(PPT):
                    if p % PPG == PPG - 1:
                        sp.wait_ge(t_ps, i * PPT + (p + 1))
                        load_x(i + 1, p // PPG)
                    sp.wait_ge(y_ps, i * PPT + (p + 1))
                    load_w(i + 1, p)

        @block.tensor
        def _(pe):
            def turn(i, p):
                if p % PPG == 0:
                    pe.wait_ge(x_ld[p // PPG], i * 16 + 16)
                for j in range(2):
                    for c in range(PARTS):
                        last = nc.tensor.transpose(psT[p % 4][0:HW, SLOT * (PARTS * j + c):SLOT * (PARTS * j + c + 1)],
                                                   xb[p // PPG][:, 2 * (p % PPG) + j, HW * c:HW * c + HW], ident[:])
                last.then_inc(t_ps, 1)

            def product(i, p, first):
                pe.wait_ge(w_ld[p], i * 32 + 32)
                if not (first and p < 4):
                    pe.wait_ge(y_sb, i * PPT + (p - 3))
                pe.wait_ge(t_sb, i * PPT + (p + 1))
                for j in range(2):
                    for c in range(PARTS):
                        last = nc.tensor.matmul(psO[p % 4][:, w_out * j:w_out * j + w_out], xT[p % 4][:, j, c, :],
                                                wb[2 * p + j][:, c, :], start=(c == 0), stop=(c == PARTS - 1))
                last.then_inc(y_ps, 1)

            def whole(i, first=False):
                turn(i, 0)
                for p in range(PPT):
                    if p + 1 < PPT:
                        turn(i, p + 1)
                    product(i, p, first)

            whole(0, first=True)
            with pe.Fori(0, TURNS - 1) as i:
                whole(i + 1)

        @block.scalar
        def _(act):
            def store(i, g):
                act.wait_ge(y_sb, i * PPT + PPG * (g + 1))
                act.dma_start(slots_out[bass.ds((i * UNR + GRP * g) * SLOT, GRP * SLOT), :].rearrange(
                    "(j p) n -> p j n", p=SLOT), yb[g][:]).then_inc(st[g], 16)

            with act.Fori(0, TURNS) as i:
                for p in range(PPT):
                    act.wait_ge(t_ps, i * PPT + (p + 1))
                    nc.scalar.activation(xT[p % 4][:].rearrange("p j c n -> p (j c n)"), psT[p % 4][0:HW, 0:2 * PARTS * SLOT],
                                         ACT.Copy).then_inc(t_sb, 1)
                    if p >= 2 and (p - 2) % PPG == PPG - 1:
                        store(i, (p - 2) // PPG)
                store(i, 1)

        @block.vector
        def _(v):
            def whole(i, first=False):
                for p in range(PPT):
                    v.wait_ge(y_ps, i * PPT + (p + 1))
                    if p % PPG == 0 and not first:
                        v.wait_ge(st[p // PPG], i * 16)
                    b0 = 2 * (p % PPG)
                    nc.vector.tensor_copy(yb[p // PPG][:, b0:b0 + 2, :].rearrange("p j n -> p (j n)"),
                                          psO[p % 4][:, 0:2 * w_out]).then_inc(y_sb, 1)

            whole(0, first=True)
            with v.Fori(0, TURNS - 1) as i:
                whole(i + 1)
            for k in range(TOPK):
                v.wait_ge(gath[k], 16 * FT)
                for i in range(FT):
                    out, w = out_rows[:, i, :], w4[:, 2 * i + bank, k:k + 1]
                    if k == 0:
                        nc.vector.tensor_scalar(out, got[:, i, k, :], w, None, ALU.mult).then_inc(acc, 1)
                    else:
                        v.wait_ge(acc, (k - 1) * FT + i + 1)
                        nc.vector.scalar_tensor_tensor(out=out, in0=got[:, i, k, :], scalar=w, in1=out, op0=ALU.mult,
                                                       op1=ALU.add).then_inc(acc, 1)
        scope.close()
        phase.clear()


def slots(nc, t, keep, ffn_dram, y_dram, out):
    with ExitStack() as ctx:
        def sb(name, shape, dt=F32):
            return ctx.enter_context(nc.sbuf_tensor(name + "_s", shape, dt))

        h, xT, ident = keep["h"], keep["xT"], keep["ident"]
        xn, sq = (sb(n, [HALF, PAIRS, D]) for n in ("xn", "sq"))
        stats, l2 = sb("stats", [HALF, 4, PAIRS]), sb("l2", [HALF, 3, PAIRS])
        projb, eps = sb("projb", [HALF, D]), sb("eps", [HALF, 1])
        ones = sb("ones", [HALF, HALF])
        phi, phi2, scl, pn = sb("phi", [HALF, 2, SLOTS]), sb("phi2", [HALF, 2, SLOTS]), sb("scl", [HALF, 1]), sb("pn", [HALF, 2, SLOTS])
        dT, dred = sb("dT", [SLOTS, B, SEQ]), sb("dred", [SLOTS, 2, B])
        C, cred = sb("C", [HALF, PAIRS, SLOTS]), sb("cred", [HALF, 2, PAIRS])
        own = sb("own", [HALF, 2])
        Dp, Cp = (sb(n, [HALF, PAIRS, 2, SLOTS]) for n in ("Dp", "Cp"))
        CT = sb("CT", [128, PAIRS, PAIR])
        xsT = sb("xsT", [HALF, 2, SLOTS, B])
        xst = [sb(f"xst{u}", [HALF, 2, EPT, B]) for u in range(2)]
        w1 = [sb(f"w1{u}", [HALF, EPT * 2, SHID]) for u in range(2)]
        w2 = [sb(f"w2{u}", [128, EPT * HCH, D]) for u in range(2)]
        b1, b2 = sb("b1", [128, SLOTS, HCH]), sb("b2", [128, D])
        hrow, hT = sb("hrow", [128, 2, HALF * 4]), sb("hT", [128, HCH, EPT, B])
        yall = sb("yall", [128, SLOTS // EPT, D])
        ys = w2[0][:, 0:PAIRS, :]
        ps = [ctx.enter_context(nc.psum_tensor(f"pss{i}", [128, 512], F32)) for i in range(8)]
        phase = Phase(nc, ctx)
        names = ("h_in c_in set_up dve ln_sq ln_std l2_sq l2_std xn x_ps x_sb p_sq p_ps p_std phin lt_ps lt_sb ln_ps "
                 "ln_sb d_sub d_exp c_sub c_exp d_nrm dt_ps d_sb c_nrm ct_ps ct_sb xs_ps xs_sb xst h_ps h_sb ht_ps h_pre h_act y_ps y_sb "
                 "y_st ys_in ys_sb f_ps f_sb stored").split()
        q = {n: phase.sem("sl_" + n) for n in names}
        w1_ld, w2_ld = ([phase.sem(f"sl_w{n}{u}") for u in range(2)] for n in (1, 2))
        TURNS = SLOTS // EPT
        CS = 8
        scope = ctx.enter_context(ExitStack())
        block = scope.enter_context(nc.Block())

        def bank(i, rows, cols):
            return ps[i][0:rows, 0:cols]

        @block.sync
        def _(sp):
            sp.dma_start(sq[:], ffn_dram.rearrange("(r p) d -> p r d", p=PAIR)).then_inc(q["h_in"], 16)
            for dst, src in ((phi, "phi"), (own, "own"), (b1, "slot_b1")):
                sp.dma_start(dst[:], t[src]).then_inc(q["c_in"], 16)
            for bb in range(2):
                sp.dma_start(b2[SLOTS * bb:SLOTS * bb + SLOTS, :], t["slot_b2"]).then_inc(q["c_in"], 16)
            for dst, src in ((projb, "second_projb"), (scl, "phi_scale")):
                sp.dma_start(dst[:], t[src].partition_broadcast(HALF)).then_inc(q["c_in"], 16)

            def load_first(n, u):
                sp.dma_start(w1[u][:], t["slot_w1"][bass.ds(n, EPT)].rearrange("e (c p) n -> p (e c) n", p=HALF)).then_inc(w1_ld[u], 16)

            def load_second(n, u):
                sp.dma_start(w2[u][:], t["slot_w2"][bass.ds(n, EPT)].rearrange("e (c p) n -> p (e c) n", p=128)).then_inc(w2_ld[u], 16)

            def store(j):
                sp.wait_ge(q["y_sb"], j + 1)
                sp.dma_start(y_dram[bass.ds(j * EPT, EPT)].rearrange("e b d -> (e b) d"),
                             yall[:, bass.ds(j, 1), :].rearrange("p j d -> p (j d)")).then_inc(q["y_st"], 16)

            for u in range(2):
                load_first(EPT * u, u)
                load_second(EPT * u, u)
            with sp.Fori(0, TURNS // 2 - 1) as i:
                for u in range(2):
                    sp.wait_ge(q["h_ps"], i * 2 + (u + 1))
                    load_first(i * 2 * EPT + EPT * (u + 2), u)
                    store(i * 2 + u)
                    load_second(i * 2 * EPT + EPT * (u + 2), u)
            for u in range(2):
                store(TURNS - 2 + u)
            sp.wait_ge(q["y_st"], 16 * TURNS)
            for bb in range(2):
                sp.dma_start(ys[SLOTS * bb:SLOTS * bb + SLOTS, :, :],
                             y_dram.rearrange("n (r b) d -> b n r d", b=2)[bb]).then_inc(q["ys_in"], 16)
            sp.wait_ge(q["f_sb"], 8)
            sp.dma_start(out.rearrange("(r b) s d -> (b s) r d", b=2), h[:]).then_inc(q["stored"], 16)
            sp.wait_ge(q["stored"], 16)

        @block.gpsimd
        def _(pool):
            def stage(j, u):
                nc.gpsimd.tensor_copy(xst[u][:], xsT[:, :, bass.ds(j * EPT, EPT), :]).then_inc(q["xst"], 1)

            pool.wait_ge(q["xs_sb"], 8)
            stage(0, 0)
            stage(1, 1)
            with pool.Fori(0, TURNS // 2 - 1) as i:
                for u in range(2):
                    pool.wait_ge(q["h_ps"], i * 2 + (u + 1))
                    stage(i * 2 + (u + 2), u)

        @block.tensor
        def _(pe):
            pe.wait_ge(q["p_sq"], 1)
            for half in range(2):
                last = nc.tensor.matmul(bank(4, HALF, SLOTS), ones[:], phi2[:, half, :], start=(half == 0), stop=(half == 1))
            last.then_inc(q["p_ps"], 1)
            pe.wait_ge(q["xn"], 1)
            for g in range(8):
                half, r = g % 2, g // 2
                if g >= 4:
                    pe.wait_ge(q["x_sb"], g - 3)
                for j in range(4):
                    last = nc.tensor.transpose(ps[g % 4][0:HALF, HALF * j:HALF * j + HALF],
                                               xn[:, 4 * r + j, HALF * half:HALF * half + HALF], ident[0:HALF, 0:HALF])
                last.then_inc(q["x_ps"], 1)
            pe.wait_ge(q["x_sb"], 8)
            pe.wait_ge(q["phin"], 1)
            for n in range(3):
                for half in range(2):
                    last = nc.tensor.matmul(bank(5 + n, SLOTS, 512), phi[:, half, :], xT[:, half, 512 * n:512 * n + 512],
                                            start=(half == 0), stop=(half == 1))
                last.then_inc(q["lt_ps"], 1)
            for g in range(2):
                for j in range(8):
                    for half in range(2):
                        r = 8 * g + j
                        last = nc.tensor.matmul(ps[g][0:HALF, SLOTS * j:SLOTS * j + SLOTS],
                                                xT[:, half, PAIR * r:PAIR * r + PAIR], phi[:, half, :],
                                                start=(half == 0), stop=(half == 1))
                last.then_inc(q["ln_ps"], 1)
            pe.wait_ge(q["d_nrm"], 1)
            for g in range(2):
                for j in range(8):
                    r = 8 * g + j
                    last = nc.tensor.transpose(ps[2 + g][0:HALF, SLOTS * j:SLOTS * j + SLOTS],
                                               dT[:, 2 * r:2 * r + 2, :].rearrange("p b m -> p (b m)"), ident[0:SLOTS, 0:SLOTS])
                last.then_inc(q["dt_ps"], 1)
            pe.wait_ge(q["c_nrm"], 1)
            for g in range(4):
                for j in range(4):
                    last = nc.tensor.transpose(ps[4 + g][:, PAIR * j:PAIR * j + PAIR],
                                               Cp[:, 4 * g + j].rearrange("p b n -> p (b n)"), ident[0:HALF, 0:HALF])
                last.then_inc(q["ct_ps"], 1)
            pe.wait_ge(q["d_sb"], 1)
            for g in range(8):
                half, r = g % 2, g // 2
                if g >= 4:
                    pe.wait_ge(q["ct_sb"], g - 3)
                for j in range(4):
                    last = nc.tensor.matmul(ps[g][0:HALF, 128 * j:128 * j + 128],
                                            xn[:, 4 * r + j, HALF * half:HALF * half + HALF],
                                            Dp[:, 4 * r + j].rearrange("p b n -> p (b n)"), start=True, stop=True)
                last.then_inc(q["xs_ps"], 1)

            def first(j, n, u):
                pe.wait_ge(w1_ld[u], n * 16 + 16)
                pe.wait_ge(q["xst"], j + 1)
                for c in range(2):
                    for half in range(2):
                        for e in range(EPT):
                            last = nc.tensor.matmul(ps[c][B * e:B * e + B, 0:SHID // 2], xst[u][:, half, e, :],
                                                    w1[u][:, 2 * e + half, SHID // 2 * c:SHID // 2 * (c + 1)],
                                                    start=(half == 0), stop=(half == 1))
                last.then_inc(q["h_ps"], 1)

            def turned(j):
                pe.wait_ge(q["h_sb"], j + 1)
                for c in range(HCH):
                    last = nc.tensor.transpose(ps[2 + c // 3][:, 128 * (c % 3):128 * (c % 3) + 128],
                                               hrow[:, c // 3, 128 * (c % 3):128 * (c % 3) + 128], ident[:])
                last.then_inc(q["ht_ps"], 1)

            def second(j, n, u):
                pe.wait_ge(w2_ld[u], n * 16 + 16)
                pe.wait_ge(q["h_act"], j + 1)
                for c in range(HCH):
                    for e in range(EPT):
                        last = nc.tensor.matmul(ps[4][B * e:B * e + B, 0:D], hT[:, c, e, :], w2[u][:, HCH * e + c, :],
                                                start=(c == 0), stop=(c == HCH - 1))
                last.then_inc(q["y_ps"], 1)

            first(0, 0, 0)
            with pe.Fori(0, TURNS // 2 - 1) as i:
                for u in range(2):
                    turned(i * 2 + u)
                    first(i * 2 + (u + 1), i + u, 1 - u)
                    second(i * 2 + u, i, u)
            N = TURNS // 2 - 1
            turned(TURNS - 2)
            first(TURNS - 1, N, 1)
            second(TURNS - 2, N, 0)
            turned(TURNS - 1)
            second(TURNS - 1, N, 1)
            pe.wait_ge(q["ys_sb"], 1)
            for r in range(PAIRS):
                g = r // 2
                if r % 2 == 0 and g >= 4:
                    pe.wait_ge(q["f_sb"], g - 3)
                last = nc.tensor.matmul(ps[g % 4][0:HALF, D * (r % 2):D * (r % 2) + D], CT[:, r, :], ys[:, r, :],
                                        start=True, stop=True)
                if r % 2:
                    last.then_inc(q["f_ps"], 1)

        @block.scalar
        def _(act):
            act.wait_ge(q["set_up"], 1)
            act.wait_ge(q["p_ps"], 1)
            nc.scalar.activation(pn[:, 0, :], bank(4, HALF, SLOTS), ACT.Sqrt).then_inc(q["p_std"], 1)
            act.wait_ge(q["ln_sq"], 1)
            nc.scalar.activation(stats[:, 2], stats[:, 1], ACT.Sqrt, bias=eps[:], scale=1.0 / D).then_inc(q["ln_std"], 1)
            act.wait_ge(q["l2_sq"], 1)
            nc.scalar.activation(l2[:, 1], l2[:, 0], ACT.Sqrt).then_inc(q["l2_std"], 1)
            for g in range(8):
                half, r = g % 2, g // 2
                act.wait_ge(q["x_ps"], g + 1)
                nc.scalar.activation(xT[:, half, 384 * r:384 * r + 384], bank(g % 4, HALF, 384), ACT.Copy).then_inc(q["x_sb"], 1)
            flat = dT[:].rearrange("p b m -> p (b m)")
            for n in range(3):
                act.wait_ge(q["lt_ps"], n + 1)
                nc.scalar.activation(flat[:, 512 * n:512 * n + 512], bank(5 + n, SLOTS, 512), ACT.Copy).then_inc(q["lt_sb"], 1)
            for g in range(2):
                act.wait_ge(q["ln_ps"], g + 1)
                nc.scalar.activation(C[:, 8 * g:8 * g + 8, :], bank(g, HALF, 512).rearrange("p (r n) -> p r n", r=8),
                                     ACT.Copy).then_inc(q["ln_sb"], 1)
            act.wait_ge(q["d_sub"], 1)
            nc.scalar.activation(dT[:], dT[:], ACT.Exp).then_inc(q["d_exp"], 1)
            act.wait_ge(q["c_sub"], 1)
            nc.scalar.activation(C[:], C[:], ACT.Exp).then_inc(q["c_exp"], 1)
            for g in range(4):
                act.wait_ge(q["ct_ps"], g + 1)
                nc.scalar.activation(CT[:, 4 * g:4 * g + 4, :], bank(4 + g, 128, 384).rearrange("p (r m) -> p r m", r=4),
                                     ACT.Copy).then_inc(q["ct_sb"], 1)
            for g in range(8):
                half, r = g % 2, g // 2
                act.wait_ge(q["xs_ps"], g + 1)
                nc.scalar.activation(xsT[:, half].rearrange("p n b -> p b n")[:, CS * r:CS * r + CS, :],
                                     bank(g, HALF, 512).rearrange("p (b n) -> p b n", b=CS), ACT.Copy).then_inc(q["xs_sb"], 1)
            with act.Fori(0, TURNS) as j:
                act.wait_ge(q["h_pre"], j + 1)
                nc.scalar.activation(hT[:], hT[:], ACT.Gelu).then_inc(q["h_act"], 1)

        @block.vector
        def _(v):
            op = nc.vector
            ch = Steps(v, q["dve"])
            ch.mark(op.memset(ones[:], 1.0))
            op.memset(eps[:], LN_EPS).then_inc(q["set_up"], 1)
            v.wait_ge(q["c_in"], 7 * 16)
            op.tensor_tensor(phi2[:], phi[:], phi[:], ALU.mult).then_inc(q["p_sq"], 1)
            v.wait_ge(q["h_in"], 16)
            ch.then(op.tensor_tensor(h[:], h[:], sq[:], ALU.add))
            ch.then(op.tensor_tensor(h[:], h[:], projb[:].unsqueeze(1).to_broadcast([HALF, PAIRS, D]), ALU.add))
            centred(nc, ch, q["ln_sq"], q["ln_std"], h[:], xn[:], sq[:], stats)
            ch.then(op.tensor_tensor(xn[:], xn[:], spread(stats[:, 3], D), ALU.mult))
            ch.then(op.tensor_tensor(sq[:], xn[:], xn[:], ALU.mult))
            op.tensor_reduce(l2[:, 0], sq[:], X, ALU.add).then_inc(q["l2_sq"], 1)
            v.wait_ge(q["p_std"], 1)
            ch.then(op.tensor_scalar(pn[:, 0, :], pn[:, 0, :], 1e-12, None, ALU.max))
            ch.then(op.reciprocal(pn[:, 1, :], pn[:, 0, :]))
            op.scalar_tensor_tensor(out=phi[:], in0=phi[:], scalar=scl[:, 0:1],
                                    in1=pn[:, 1, :].unsqueeze(1).to_broadcast([HALF, 2, SLOTS]), op0=ALU.mult,
                                    op1=ALU.mult).then_inc(q["phin"], 1)
            v.wait_ge(q["l2_std"], 1)
            ch.then(op.tensor_scalar(l2[:, 1], l2[:, 1], 1e-12, None, ALU.max))
            ch.then(op.reciprocal(l2[:, 2], l2[:, 1]))
            op.tensor_tensor(xn[:], xn[:], spread(l2[:, 2], D), ALU.mult).then_inc(q["xn"], 1)
            v.wait_ge(q["lt_sb"], 3)
            ch.then(op.tensor_reduce(dred[:, 0], dT[:], X, ALU.max))
            op.tensor_tensor(dT[:], dT[:], spread(dred[:, 0], SEQ), ALU.subtract).then_inc(q["d_sub"], 1)
            v.wait_ge(q["ln_sb"], 2)
            ch.then(op.tensor_reduce(cred[:, 0], C[:], X, ALU.max))
            op.tensor_tensor(C[:], C[:], spread(cred[:, 0], SLOTS), ALU.subtract).then_inc(q["c_sub"], 1)
            v.wait_ge(q["d_exp"], 1)
            ch.then(op.tensor_reduce(dred[:, 0], dT[:], X, ALU.add))
            ch.then(op.reciprocal(dred[:, 1], dred[:, 0]))
            op.tensor_tensor(dT[:], dT[:], spread(dred[:, 1], SEQ), ALU.mult).then_inc(q["d_nrm"], 1)
            v.wait_ge(q["c_exp"], 1)
            ch.then(op.tensor_reduce(cred[:, 0], C[:], X, ALU.add))
            ch.then(op.reciprocal(cred[:, 1], cred[:, 0]))
            ch.then(op.tensor_tensor(C[:], C[:], spread(cred[:, 1], SLOTS), ALU.mult))
            for bb in range(2):
                last = op.tensor_scalar(Cp[:, :, bb, :], C[:], own[:, bb:bb + 1], None, ALU.mult)
                ch.mark(last)
            ch.wait()
            op.memset(cred[:, 0, 0:1], 0.0).then_inc(q["c_nrm"], 1)
            v.wait_ge(q["dt_ps"], 2)
            for g in range(2):
                for bb in range(2):
                    ch.mark(op.tensor_scalar(Dp[:, 8 * g:8 * g + 8, bb, :],
                                             bank(2 + g, HALF, 512).rearrange("p (r n) -> p r n", r=8),
                                             own[:, bb:bb + 1], None, ALU.mult))
            ch.wait()
            op.memset(dred[:, 0, 0:1], 0.0).then_inc(q["d_sb"], 1)
            def hidden(j):
                v.wait_ge(q["h_ps"], j + 1)
                for c in range(2):
                    last = op.tensor_copy(hrow[:, c, :], ps[c][:, 0:SHID // 2])
                last.then_inc(q["h_sb"], 1)

            def bias(j):
                v.wait_ge(q["ht_ps"], j + 1)
                b = b1[:, bass.ds(j * EPT, EPT), :].rearrange("p e c -> p c e")
                for c in range(2):
                    last = op.tensor_tensor(hT[:, 3 * c:3 * c + 3], ps[2 + c][:, 0:3 * 128].rearrange("p (c e b) -> p c e b", c=3, e=EPT),
                                            spread(b[:, 3 * c:3 * c + 3], B), ALU.add)
                last.then_inc(q["h_pre"], 1)

            def result(j):
                v.wait_ge(q["y_ps"], j + 1)
                op.tensor_copy(yall[:, bass.ds(j, 1), :].rearrange("p j d -> p (j d)"), ps[4][:, 0:D]).then_inc(q["y_sb"], 1)

            hidden(0)
            with v.Fori(0, TURNS - 1) as j:
                bias(j)
                hidden(j + 1)
                result(j)
            bias(TURNS - 1)
            result(TURNS - 1)
            v.wait_ge(q["ys_in"], 2 * 16)
            op.tensor_tensor(ys, ys, b2[:].unsqueeze(1).to_broadcast([128, PAIRS, D]), ALU.add).then_inc(q["ys_sb"], 1)
            for g in range(8):
                v.wait_ge(q["f_ps"], g + 1)
                hh = h[:, 2 * g:2 * g + 2, :]
                op.tensor_tensor(hh, hh, bank(g % 4, HALF, 2 * D).rearrange("p (r d) -> p r d", r=2),
                                 ALU.add).then_inc(q["f_sb"], 1)
        scope.close()
        phase.clear()


def build(nc, t):
    def dram(name, *shape):
        return nc.dram_tensor(name, shape, F32).ap()

    h_tok, m_dram, xn_dram = dram("h_tok", B, SEQ, D), dram("m_dram", 128, GH, HD, HD), dram("xn_dram", TOK, D)
    x_slots, f_slots = dram("x_slots", BLOCKS * SLOT, D), dram("f_slots", BLOCKS * SLOT, RANK)
    g_slots, r_slots = dram("g_slots", BLOCKS * SLOT, RANK), dram("r_slots", BLOCKS * SLOT, D)
    ffn_dram, y_dram = dram("ffn_dram", TOK, D), dram("y_dram", SLOTS, B, D)
    with ExitStack() as ctx:
        gathered = [ctx.enter_context(nc.semaphore(f"gathered{g}")) for g in range(2)]
        scat = [ctx.enter_context(nc.semaphore(f"scattered{bank}")) for bank in range(2)]
        gath = [[ctx.enter_context(nc.semaphore(f"routed_in{bank}_{k}")) for k in range(TOPK)] for bank in range(2)]
        embed(nc, t, h_tok, gathered)

        def hold(scope, *tensors):
            for name, shape, dt in tensors:
                keep[name] = scope.enter_context(nc.sbuf_tensor("keep_" + name, shape, dt))

        keep = {}
        hold(ctx, ("h", [HALF, PAIRS, D], F32), ("ident", [128, 128], F32), ("xT", [HALF, 2, TOK], F32))
        with ExitStack() as outer:
            hold(outer, ("oT", [HALF, 2, TOK], F32))
            with ExitStack() as scope:
                hold(scope, ("qkT", [HALF, 4, TOK], F32), ("fac", [128, 2 * GH * HD, SEQ], F32), ("v_all", [SEQ, B, D], F32),
                     ("Mbd", [HALF, 2, B, HALF], F32), ("kn4", [128, TOK], F32), ("qn4", [128, TOK], F32),
                     ("qn4c", [128, B * RCH], F32))
                qkv(nc, t, keep, h_tok)
                factor(nc, t, keep, m_dram)
                attend(nc, t, keep, m_dram, x_slots, g_slots)
            with ExitStack() as scope:
                hold(scope, ("pos", [128, 2 * FT, TOPK], I32), ("w4", [128, 2 * FT, TOPK], F32), ("eid", [1, 2 * BLOCKS], I32),
                     ("rows_in", [128, FT, D], F32))
                route(nc, t, keep, xn_dram)
                hf = scope.enter_context(nc.sbuf_tensor("hf", [128, FT, RANK], F32))
                routed(nc, t, keep, 0, scat[0], gath[0], D, RANK, x_slots, f_slots, t["f_know"], hf)
                keep["rows_in"] = hf
                ffn = scope.enter_context(nc.sbuf_tensor("ffn", [128, FT, D], F32))
                routed(nc, t, keep, 1, scat[1], gath[1], RANK, D, g_slots, r_slots, t["r_know"], ffn)
                with nc.semaphore("ffn_out") as ffn_out, nc.Block() as block:
                    @block.sync
                    def _(sp):
                        sp.dma_start(ffn_dram.rearrange("(t p) d -> p t d", p=128), ffn[:]).then_inc(ffn_out, 16)
                        sp.wait_ge(ffn_out, 16)
        slots(nc, t, keep, ffn_dram, y_dram, t["out"])


def lay_out(a):
    x = a["x"].reshape(B, 3, 8, 8, 4, 2, 8)
    w1 = a["L0_tok_W1"].reshape(5, 3, 2, 8, 2, 8, HID)
    gb = np.stack([a["L0_tok_gamma"], a["L0_tok_beta"]], -1).reshape(5, 3, 2, 8, 2, 8, 2)

    def features(w):
        w = np.concatenate([w[:3], w[3:, :, :, :, ::-1]])
        return w.transpose(4, 3, 5, 0, 1, 2, 6).reshape(128, KCH, -1)

    out = {
        "x_quads": x.transpose(5, 3, 6, 2, 4, 1, 0).reshape(128, 8, 4, 3, B),
        "W1": features(w1),
        "gb": features(gb),
        "b1": a["L0_tok_b1"].reshape(3, 128).T,
        "W2": a["L0_tok_W2"].reshape(3, 128, D).transpose(1, 0, 2),
        "b2": a["L0_tok_b2"],
        "text_ids": a["x_txt"].reshape(8, 128).T,
        "basin": a["L0_txt_basin_coords"],
        "txt_projT": a["L0_txt_proj_w"].T,
        "txt_norm": a["L0_txt_norm_w"],
    }
    qk = a["L0_attn_qkv_w"][:2 * D].reshape(2, GROUPS, GH * HD, 2, HALF)
    qkb = a["L0_attn_qkv_b"][:2 * D].reshape(2, GROUPS, GH * HD)
    out |= {
        "ident": np.eye(128, dtype=np.float32),
        "wqk": a["L0_attn_qkv_w"][:2 * D].T.reshape(2, HALF, 2 * D).transpose(1, 0, 2),
        "bqk": a["L0_attn_qkv_b"][:2 * D].reshape(4, HALF).T,
        "wqk_groups": qk.transpose(4, 3, 1, 0, 2).reshape(HALF, 2, GROUPS, HALF),
        "bqk_groups": np.repeat(qkb.transpose(1, 0, 2).reshape(GROUPS, HALF), B, axis=0),
    }
    d96, d128 = np.arange(HALF), np.arange(128)
    row, head = d128 % 64 // HEADS_2, d128 % 64 % HEADS_2
    used = d128 % 64 < SEQ
    conv = a["L0_attn_conv_w"].reshape(HEADS, 3, 2, HEADS_2)
    mix = np.zeros((128, 3, 8, HEADS), np.float32)
    for p in d128[used]:
        mix[p, :, row[p], :] = conv[:, :, p // 64, head[p]].T
    bn = [a["L0_attn_" + n] for n in ("conv_b", "bn_mean", "bn_gamma", "bn_beta", "bn_var")]
    out |= {
        "headsum": ((d96[:, None] // HD == np.arange(64) % HEADS_2) & (np.arange(64) < SEQ)).astype(np.float32),
        "rowmask": ((row[:, None] == np.arange(8)) & used[:, None]).astype(np.float32),
        "mask6": (d96[:, None] // HD == np.arange(HEADS_2)).astype(np.float32),
        "wv": a["L0_attn_qkv_w"][2 * D:].T.reshape(2, HALF, D).transpose(1, 0, 2),
        "bv": a["L0_attn_qkv_b"][2 * D:].reshape(1, D),
        "mix": mix.reshape(128, 3, HALF),
        "bncol": np.tile(np.stack(bn, -1), (8, 1)),
        "bnrow": np.tile(np.stack([a["L0_attn_bn_gamma"], a["L0_attn_bn_var"]]), (1, 8)),
        "attn_projT": a["L0_attn_proj_w"].T.reshape(2, HALF, D).transpose(1, 0, 2),
        "attn_projb": a["L0_attn_proj_b"].reshape(1, D),
        "Wf": np.concatenate([a["L0_ffn_W_fk"], a["L0_ffn_W_rk"]], 1).reshape(2, HALF, 128).transpose(1, 0, 2),
        "bf": np.concatenate([a["L0_ffn_b_fk"], a["L0_ffn_b_rk"]]).reshape(128, 1),
        "emb": np.stack([a["L0_ffn_emb_fk"], a["L0_ffn_emb_rk"]], 1),
        "upper": np.triu(np.ones((128, 128), np.float32), 1),
        "iota": np.tile(np.arange(BLOCKS, dtype=np.float32), (128, 1)),
        "own": (np.arange(HALF)[:, None] // SEQ == np.arange(2)).astype(np.float32),
        "second_projb": a["L1_attn_proj_b"],
        "phi": a["L1_ffn_phi"].reshape(2, HALF, SLOTS).transpose(1, 0, 2),
        "phi_scale": a["L1_ffn_scale"],
        "slot_w1": a["L1_ffn_w1"],
        "slot_w2": a["L1_ffn_w2"],
        "slot_b1": a["L1_ffn_b1"].reshape(SLOTS, HCH, 128).transpose(2, 0, 1),
        "slot_b2": a["L1_ffn_b2"],
        "f_know": a["L0_ffn_f_know"],
        "r_know": a["L0_ffn_r_know"],
        "scales": np.stack([a["L0_attn_scale"], a["L0_attn_riem_scale"], a["L0_attn_grass_scale"]]),
    }
    return {n: np.ascontiguousarray(v) for n, v in out.items()}


def kernel(**inputs):
    import concourse.bacc as bacc
    from concourse.bass_utils import run_bass_kernel_spmd

    nc = bacc.Bacc("TRN2", target_bir_lowering=False, num_devices=1)
    arrays = {"in_" + n: v for n, v in lay_out({n: np.asarray(v) for n, v in inputs.items()}).items()}
    t = {n[3:]: nc.dram_tensor(n, v.shape, mybir.dt.from_np(v.dtype), kind="ExternalInput").ap()
         for n, v in arrays.items()}
    t["out"] = nc.dram_tensor("out_h", (B, SEQ, D), F32, kind="ExternalOutput").ap()
    build(nc, t)
    done = run_bass_kernel_spmd(nc, [arrays], core_ids=[0])
    return done.results[0]["out_h"]
```

```python
from contextlib import ExitStack

import numpy as np

import concourse.bass as bass
from concourse import mybir

F32 = mybir.dt.float32
I32 = mybir.dt.int32
U32 = mybir.dt.uint32
ALU = mybir.AluOpType
ACT = mybir.ActivationFunctionType
X = mybir.AxisListType.X

B = 32
SEQ = 48
PATCHES, TEXT = 16, 32
TOK = B * SEQ
D = 192
HALF = 96
PAIR = 2 * SEQ
PAIRS = B // 2
HEADS, HD = 12, 16
HEADS_2 = HEADS // 2
GROUPS, GH = 4, 3
HID = 384
RING = 15
KCH = 30
LN_EPS = 1e-5
VOCAB, BASIN = 32000, 64
RCH = SEQ // 8
NEUR = 128
RANK = 128
TOPK = 4
FT = TOK // 128
SLOT = 64
BLOCKS = 224
EPT = 4
assert BLOCKS >= TOPK * TOK // SLOT + NEUR - 1
SLOTS, SHID = 64, 768
HCH = SHID // 128


class Steps:

    def __init__(self, eng, sem, base=0, turn=None, per=0):
        self.eng, self.sem, self.n, self.base, self.turn, self.per = eng, sem, 0, base, turn, per

    def value(self, n):
        return self.base + n if self.turn is None else self.turn * self.per + (self.base + n)

    def then(self, ins):
        self.mark(ins)
        self.eng.wait_ge(self.sem, self.value(self.n))

    def mark(self, ins):
        ins.then_inc(self.sem, 1)
        self.n += 1

    def wait(self):
        self.eng.wait_ge(self.sem, self.value(self.n))


def embed(nc, t, h_tok, gathered):
    with ExitStack() as ctx:
        def sb(name, shape, dt=F32):
            return ctx.enter_context(nc.sbuf_tensor(name, shape, dt))

        def pb(name, shape, dt=F32):
            return ctx.enter_context(nc.psum_tensor(name, shape, dt))

        phase = Phase(nc, ctx)
        sem = phase.sem

        quad = sb("quad", [128, 10, 4, 3, B])
        side = sb("side", [128, 8, 5, 3, B])
        sqr = sb("sqr", [128, 8, 4, 3, B])
        w1 = sb("w1", [128, KCH, HID])
        w1g = sb("w1g", [128, RING, HID])
        gb = sb("gb", [128, KCH, 2])
        gsum, gsel = sb("gsum", [128, HID]), sb("gsel", [128, 2])
        csum = sb("csum", [128, 2, 32, B])
        half1 = sb("half1", [128, 2, 128])
        qstat = sb("qstat", [128, 2, 10, 10, B])
        st = [sb(f"st{i}", [128, 2, 16, B]) for i in range(4)]
        g1c1 = sb("g1c1", [128, 3, 2])
        b1 = sb("b1", [128, 3])
        w2 = sb("w2", [128, 3, D])
        b2 = sb("b2", [128, D])
        hid = sb("hid", [128, 3, 512])
        img = sb("img", [128, 4, D])
        ident = sb("ident", [128, 128])
        eps = sb("eps", [128, 2])
        ids = sb("ids", [128, 8], I32)
        idf = sb("idf", [128, 2, 8])
        idc = sb("idc", [128, 8], I32)
        rows = sb("rows", [128, 8, BASIN])
        rowsT = sb("rowsT", [BASIN, 2, 512])
        projT = sb("projT", [BASIN, D])
        normw = sb("normw", [128, D])
        txt = sb("txt", [128, 8, D])
        txsq = sb("txsq", [128, D])
        rms = sb("rms", [128, 3, 8])
        psH = [pb(f"psH{m}", [128, 512]) for m in range(3)]
        psP = pb("psP", [128, 512])
        psC = psP[:, HID:HID + 6].rearrange("p (m s) -> p m s", m=3)
        psS = [pb(f"psS{i}", [128, 512]) for i in range(4)]

        x_in, w1_in, s_in, id_in = sem("x_in"), [sem(f"w1_in{i}") for i in range(3)], sem("s_in"), sem("id_in")
        pads, consts = sem("pads"), sem("consts")
        squared, sums_in, sums_out, sums_free = sem("squared"), sem("sums_in"), sem("sums_out"), sem("sums_free")
        dve, scaled, small, main = sem("dve"), sem("scaled"), sem("small"), sem("main")
        zeroed, parts, parts_sb = sem("zeroed"), sem("parts"), sem("parts_sb")
        var_in, std_out = sem("var_in"), sem("std_out")
        pre_act, acted, img_ps, img_sb, stored = sem("pre_act"), sem("acted"), sem("img_ps"), sem("img_sb"), sem("stored")
        clamped, txT, txT_sb, tx_ps, tx_ss, tx_std, tx_sb = (sem(n) for n in (
            "clamped", "txT", "txT_sb", "tx_ps", "tx_ss", "tx_std", "tx_sb"))
        tx_free = sem("tx_free")

        def patches(k):
            s, c, qy = k // 6, k // 2 % 3, k % 2
            if s < 3:
                y0 = 1 + qy + (0, -1, 1)[s]
                return quad[:, y0:y0 + 7:2, :, c, :]
            x0 = s - 3
            return side[:, qy:qy + 7:2, x0:x0 + 4, c, :]

        scope = ctx.enter_context(ExitStack())
        block = scope.enter_context(nc.Block())

        @block.sync
        def _(sp):
            sp.dma_start(quad[:, 1:9], t["x_quads"]).then_inc(x_in, 16)
            for i in range(3):
                sp.dma_start(w1[:, 10 * i:10 * i + 10], t["W1"][:, 10 * i:10 * i + 10]).then_inc(w1_in[i], 16)
            sp.wait_ge(tx_sb, 8)
            for q in range(4):
                sp.dma_start(h_tok[:, PATCHES:SEQ].rearrange("(i b) s d -> b s i d", b=4)[q],
                             txt[32 * q:32 * q + 32]).then_inc(stored, 16)
            sp.wait_ge(img_sb, 4)
            for gw in range(4):
                sp.dma_start(h_tok[:, 0:PATCHES].rearrange("b (gh gw) d -> gw b gh d", gw=4)[gw],
                             img[32 * gw:32 * gw + 32]).then_inc(stored, 16)
            sp.wait_ge(stored, 8 * 16)

        @block.gpsimd
        def _(pool):
            for y in (0, 9):
                nc.gpsimd.memset(quad[:, y], 0.0)
            nc.gpsimd.memset(qstat[:], 0.0).then_inc(pads, 1)
            nc.gpsimd.memset(half1[:], 1.0)
            nc.gpsimd.memset(eps[:, 0:1], LN_EPS)
            nc.gpsimd.memset(eps[:, 1:2], 1e-8)
            nc.gpsimd.memset(ident[:], 0.0).then_inc(consts, 1)
            pool.wait_ge(consts, 1)
            nc.gpsimd.affine_select(out=half1[:, 0, :], in_=half1[:, 0, :], compare_op=ALU.is_ge, fill=0.0, base=63,
                                    pattern=[[0, 128]], channel_multiplier=-1)
            nc.gpsimd.affine_select(out=half1[:, 1, :], in_=half1[:, 1, :], compare_op=ALU.is_ge, fill=0.0, base=-64,
                                    pattern=[[0, 128]], channel_multiplier=1)
            nc.gpsimd.affine_select(out=ident[:], in_=ident[:], compare_op=ALU.not_equal, fill=1.0, base=0,
                                    pattern=[[-1, 128]], channel_multiplier=1).then_inc(consts, 1)
            pool.wait_ge(clamped, 1)
            for i in range(8):
                nc.gpsimd.indirect_dma_start(rows[:, i, :], None, t["basin"],
                                             bass.IndirectOffsetOnAxis(idc[:, i:i + 1], 0)).then_inc(gathered[i // 4], 16)

        @block.scalar
        def _(act):
            act.dma_start(ids[:], t["text_ids"]).then_inc(id_in, 16)
            act.dma_start(side[0:64, :, 0:4], t["x_quads"][0:64]).then_inc(x_in, 16)
            act.dma_start(side[64:128, :, 1:5], t["x_quads"][64:128]).then_inc(x_in, 16)
            for dst, src in ((gb, "gb"), (b1, "b1"), (w2, "W2"), (projT, "txt_projT"), (gsel, "gsel")):
                act.dma_start(dst[:], t[src]).then_inc(s_in, 16)
            for dst, src in ((b2, "b2"), (normw, "txt_norm")):
                act.dma_start(dst[:], t[src].partition_broadcast(128)).then_inc(s_in, 16)
            act.wait_ge(x_in, 48)
            nc.scalar.activation(sqr[:], quad[:, 1:9], ACT.Square).then_inc(squared, 1)
            act.wait_ge(pads, 1)
            for stat in range(2):
                act.wait_ge(sums_out, stat + 1)
                for side_ in range(2):
                    for n in range(2):
                        src = psS[2 * side_ + n][:].rearrange("p (y x b) -> p y x b", y=4, x=4)
                        dst = qstat[:, stat, 1 + 4 * n:5 + 4 * n, 1 + side_:8 + side_:2, :]
                        last = nc.scalar.activation(dst, src, ACT.Copy, scale=1.0 / (5 * 768))
                last.then_inc(sums_free, 1)
            act.wait_ge(tx_ss, 1)
            nc.scalar.activation(rms[:, 1, :], rms[:, 0, :], ACT.Sqrt, bias=eps[:, 1:2],
                                 scale=1.0 / D).then_inc(tx_std, 1)
            act.wait_ge(var_in, 1)
            nc.scalar.activation(st[3][:, 1], st[3][:, 0], ACT.Sqrt, bias=eps[:, 0:1]).then_inc(std_out, 1)
            for m in range(3):
                act.wait_ge(pre_act, m + 1)
                nc.scalar.activation(hid[:, m, :], hid[:, m, :], ACT.Gelu,
                                     bias=g1c1[:, m, 1:2]).then_inc(acted, 1)

        @block.tensor
        def _(pe):
            pe.wait_ge(consts, 2)
            for stat in range(2):
                pe.wait_ge(sums_in, stat + 1)
                if stat:
                    pe.wait_ge(sums_free, stat)
                for side_ in range(2):
                    for n in range(2):
                        last = nc.tensor.matmul(psS[2 * side_ + n][:], half1[:, side_, :],
                                                csum[:, stat, 16 * n:16 * n + 16, :], start=True, stop=True)
                last.then_inc(sums_out, 1)
            pe.wait_ge(s_in, 7 * 16)
            pe.wait_ge(zeroed, 1)
            for k in range(KCH):
                if k % 10 == 0:
                    pe.wait_ge(w1_in[k // 10], 16)
                g = k % 4
                last = nc.tensor.matmul(psP[32 * g:32 * g + 2, 0:HID], gb[:, k, :], w1[:, k, :], start=(k < 4),
                                        stop=(k >= KCH - 4))
            last.then_inc(parts, 1)
            for g in range(2):
                pe.wait_ge(gathered[g], 4 * 16)
                if g == 0:
                    pe.wait_ge(sums_free, 2)
                else:
                    pe.wait_ge(txT_sb, g)
                for i in range(4):
                    last = nc.tensor.transpose(psS[0][0:BASIN, 128 * i:128 * i + 128], rows[:, 4 * g + i, :], ident[:])
                last.then_inc(txT, 1)
                for i in range(4):
                    n = 4 * g + i
                    if i == 0:
                        pe.wait_ge(txT_sb, g + 1)
                    if n >= 3:
                        pe.wait_ge(tx_free, n - 2)
                    nc.tensor.matmul(psS[1 + n % 3][:, 0:D], rowsT[:, g, 128 * i:128 * i + 128], projT[:],
                                     start=True, stop=True).then_inc(tx_ps, 1)
            pe.wait_ge(parts_sb, 1)
            for m in range(3):
                last = nc.tensor.matmul(psC[:, m, :], gsum[:, 128 * m:128 * m + 128], gsel[:], start=True, stop=True)
            last.then_inc(small, 1)
            for k in range(KCH):
                pe.wait_ge(scaled, k + 1)
                for m in range(3):
                    last = nc.tensor.matmul(psH[m][:], w1g[:, k % RING, 128 * m:128 * m + 128], patches(k),
                                            start=(k == 0), stop=(k == KCH - 1))
                last.then_inc(main, 1)
            pe.wait_ge(acted, 3)
            pe.wait_ge(tx_free, 8)
            for gh in range(4):
                for m in range(3):
                    last = nc.tensor.matmul(psS[gh][:, 0:D], hid[:, m, 128 * gh:128 * gh + 128], w2[:, m, :],
                                            start=(m == 0), stop=(m == 2))
                last.then_inc(img_ps, 1)

        @block.vector
        def _(v):
            ch = Steps(v, dve)
            nc.vector.memset(side[0:64, :, 4], 0.0)
            nc.vector.memset(side[64:128, :, 0], 0.0)
            nc.vector.memset(psP[:], 0.0).then_inc(zeroed, 1)
            v.wait_ge(id_in, 16)
            ch.then(nc.vector.tensor_copy(idf[:, 0, :], ids[:]))
            ch.then(nc.vector.tensor_scalar(idf[:, 1, :], idf[:, 0, :], 0.0, float(VOCAB), ALU.is_lt, ALU.mult))
            ch.then(nc.vector.tensor_tensor(idf[:, 0, :], idf[:, 0, :], idf[:, 1, :], ALU.add))
            nc.vector.tensor_scalar(idc[:], idf[:, 0, :], 0.0, float(VOCAB - 1), ALU.max,
                                    ALU.min).then_inc(clamped, 1)
            v.wait_ge(x_in, 48)
            nc.vector.tensor_reduce(csum[:, 0], quad[:, 1:9].rearrange("p y x c b -> p (y x) b c"), X,
                                    ALU.add).then_inc(sums_in, 1)
            v.wait_ge(squared, 1)
            nc.vector.tensor_reduce(csum[:, 1], sqr[:].rearrange("p y x c b -> p (y x) b c"), X,
                                    ALU.add).then_inc(sums_in, 1)
            v.wait_ge(s_in, 7 * 16)

            def by_gamma(k):
                v.wait_ge(w1_in[k // 10], 16)
                if k >= RING:
                    v.wait_ge(main, k - RING + 1)
                nc.vector.tensor_scalar(w1g[:, k % RING, :], w1[:, k, :], gb[:, k, 0:1], None, ALU.mult).then_inc(scaled, 1)

            for k in range(RING):
                by_gamma(k)
            v.wait_ge(parts, 1)
            nc.vector.tensor_copy(gsum[:], psP[:, 0:HID]).then_inc(parts_sb, 1)
            for g in range(2):
                v.wait_ge(txT, g + 1)
                nc.vector.tensor_copy(rowsT[:, g, :], psS[0][0:BASIN, :]).then_inc(txT_sb, 1)
                for i in range(4):
                    n = 4 * g + i
                    v.wait_ge(tx_ps, n + 1)
                    nc.vector.tensor_copy(txt[:, n, :], psS[1 + n % 3][:, 0:D]).then_inc(tx_free, 1)
                    v.wait_ge(tx_free, n + 1)
                    ch.then(nc.vector.tensor_tensor_reduce(txsq[:], txt[:, n, :], txt[:, n, :], 1.0, 0.0, ALU.mult,
                                                           ALU.add, rms[:, 0, n:n + 1]))
            nc.vector.memset(rms[:, 2, 0:1], 0.0).then_inc(tx_ss, 1)
            v.wait_ge(sums_free, 2)

            def q(stat, y, x):
                return qstat[:, stat, 1 + y:8 + y:2, 1 + x:8 + x:2, :]

            def grid(a, stat):
                return a[:, stat].rearrange("p (y x) b -> p y x b", y=4)

            def add(dst, a, b):
                for stat in range(2):
                    last = nc.vector.tensor_tensor(grid(dst, stat), a(stat), b(stat), ALU.add)
                ch.mark(last)

            def at(y, x):
                return lambda stat: q(stat, y, x)

            def of(a):
                return lambda stat: grid(a, stat)

            c0, c1, s, u = st
            add(c0, at(0, 0), at(0, 1))
            add(c1, at(1, 0), at(1, 1))
            add(s, at(-1, 0), at(-1, 1))
            add(u, at(2, 0), at(2, 1))
            ch.wait()
            add(c0, of(c0), of(c1))
            add(s, of(s), of(u))
            ch.wait()
            for dy in (0, 1):
                for dx in (-1, 2):
                    add(s, of(s), at(dy, dx))
                    ch.wait()
            ch.then(nc.vector.scalar_tensor_tensor(out=s[:], in0=c0[:], scalar=3.0, in1=s[:], op0=ALU.mult,
                                                   op1=ALU.add))
            ch.then(nc.vector.tensor_tensor(c0[:, 0], s[:, 0], s[:, 0], ALU.mult))
            nc.vector.tensor_tensor(u[:, 0], s[:, 1], c0[:, 0], ALU.subtract).then_inc(var_in, 1)
            v.wait_ge(std_out, 1)
            ch.then(nc.vector.reciprocal(c1[:, 0], u[:, 1]))
            v.wait_ge(tx_std, 1)
            ch.then(nc.vector.reciprocal(rms[:, 2, :], rms[:, 1, :]))
            for n in range(8):
                nc.vector.scalar_tensor_tensor(out=txt[:, n, :], in0=txt[:, n, :], scalar=rms[:, 2, n:n + 1],
                                               in1=normw[:], op0=ALU.mult, op1=ALU.mult).then_inc(tx_sb, 1)
            for k in range(RING, KCH):
                by_gamma(k)
            v.wait_ge(small, 1)
            ch.then(nc.vector.tensor_scalar(g1c1[:, :, 0], psC[:, :, 0], -1.0, None, ALU.mult))
            ch.then(nc.vector.tensor_tensor(g1c1[:, :, 1], psC[:, :, 1], b1[:], ALU.add))
            v.wait_ge(main, KCH)
            for m in range(3):
                ch.then(nc.vector.scalar_tensor_tensor(out=hid[:, m, :], in0=s[:, 0].rearrange("p g b -> p (g b)"),
                                                       scalar=g1c1[:, m, 0:1], in1=psH[m][:], op0=ALU.mult,
                                                       op1=ALU.add))
                nc.vector.tensor_tensor(hid[:, m, :], hid[:, m, :], c1[:, 0].rearrange("p g b -> p (g b)"),
                                        ALU.mult).then_inc(pre_act, 1)
            for gh in range(4):
                v.wait_ge(img_ps, gh + 1)
                nc.vector.tensor_tensor(img[:, gh, :], psS[gh][:, 0:D], b2[:], ALU.add).then_inc(img_sb, 1)
        scope.close()
        phase.clear()


class Phase:

    def __init__(self, nc, ctx):
        self.nc, self.ctx, self.sems = nc, ctx, []

    def sem(self, name):
        self.sems.append(self.ctx.enter_context(self.nc.semaphore(name)))
        return self.sems[-1]

    def clear(self):
        with self.nc.Block() as block:
            @block.sync
            def _(sp):
                for sem in self.sems:
                    sp.sem_clear(sem)


def spread(a, n):
    return a.unsqueeze(a.ndim).to_broadcast(list(a.shape) + [n])


def centred(nc, ch, ln_sq, ln_std, h, xc, sq, stats, n=1):
    v = nc.vector
    ch.then(v.tensor_reduce(stats[:, 0], h, X, ALU.add))
    ch.then(v.tensor_scalar(stats[:, 0], stats[:, 0], 1.0 / D, None, ALU.mult))
    ch.then(v.tensor_tensor(xc, h, spread(stats[:, 0], D), ALU.subtract))
    ch.then(v.tensor_tensor(sq, xc, xc, ALU.mult))
    v.tensor_reduce(stats[:, 1], sq, X, ALU.add).then_inc(ln_sq, 1)
    ch.eng.wait_ge(ln_std, n)
    ch.then(v.reciprocal(stats[:, 3], stats[:, 2]))


def prepare(nc, t, keep, h_tok, m_dram):
    with ExitStack() as ctx:
        def sb(name, shape, dt=F32):
            return ctx.enter_context(nc.sbuf_tensor(name, shape, dt))

        phase = Phase(nc, ctx)
        sem = phase.sem

        h, xT, qkT, fac, ident = keep["h"], keep["xT"], keep["qkT"], keep["fac"], keep["ident"]
        v_all, kn4, qn4, qn4c = (keep[n] for n in ("v_all", "kn4", "qn4", "qn4c"))
        qk2 = sb("qk2", [HALF, 4, TOK])
        xc = qk2[:, 0:2].rearrange("p a (r d) -> p (a r) d", d=D)
        xn = qk2[:, 2:4].rearrange("p a (r d) -> p (a r) d", d=D)
        stats = sb("stats", [HALF, 4, PAIRS])
        eps = sb("eps2", [HALF, 1])
        wqk, wg = sb("wqk", [HALF, 2, 4 * HALF]), sb("wg", [HALF, 2, GROUPS, HALF])
        bqk, bg = sb("bqk", [HALF, 4]), sb("bg", [128, HALF])
        stage = sb("stage", [HALF, 2, 2, 4, B])
        NM = 2 * GH
        A = fac[:].rearrange("p (m d) n -> p m d n", m=NM)
        VM, SHARED = 4, 11
        tmp = sb("tmp", [128, NM * (HD - 1) * SEQ])
        n2, nrm, sg = sb("n2", [128, NM]), sb("nrm", [128, NM]), sb("sg", [128, NM])
        w, w2 = sb("wv", [128, NM, HD]), sb("wv2", [128, NM])
        rinv = sb("rinv", [128, NM, HD])
        Xk, Y, M = (sb(n, [128, GH, HD, HD]) for n in ("Xk", "Yq", "Mm"))
        headsum, rowmask = sb("headsum", [HALF, 64]), sb("rowmask", [128, 8])
        wv_ = sb("wvT", [HALF, 2, D])
        xst = sb("xst", [HALF, 2, 2, PAIR])
        ps = [ctx.enter_context(nc.psum_tensor(f"psf{i}", [128, 512], F32)) for i in range(8)]
        h_in, w_in, c_in, dve, ln_sq, ln_std, eps_set = (sem(n) for n in (
            "h_in2", "w_in2", "c_in", "dve2", "ln_sq", "ln_std", "eps_set"))
        xn_ready, x_ps, x_sb, st_sb, f_ps, f_sb, q_ps, q_sb = (sem(n) for n in (
            "xn_ready", "x_ps", "x_sb", "st_sb", "f_ps", "f_sb", "q_ps", "q_sb"))
        qk2_sb, n_ps, n_sb, xst_sb, v_ps, v_sb = (sem(n) for n in (
            "qk2_sb", "n_ps", "n_sb", "xst_sb", "v_ps", "v_sb"))
        house, sq_sum, norm_out, m_ready, m_out = (sem(n) for n in ("house", "sq_sum", "norm_out", "m_ready", "m_out"))
        columns, prods, coeffs, spans, reflected = (sem(n) for n in ("columns", "prods", "coeffs", "spans", "reflected"))
        ROWS = 4
        STEPS = SEQ // ROWS
        scope = ctx.enter_context(ExitStack())
        block = scope.enter_context(nc.Block())

        def reflection(j, m0, m1):
            L, C, n = SEQ - j, HD - 1 - j, m1 - m0
            return (tmp[:, m0 * C * L:m1 * C * L].rearrange("p (m c l) -> p m c l", m=n, c=C),
                    A[:, m0:m1, j + 1:HD, j:SEQ],
                    A[:, m0:m1, j, j:SEQ].unsqueeze(2).to_broadcast([128, n, C, L]),
                    w[:, m0:m1, 0:C].unsqueeze(3).to_broadcast([128, n, C, L]))

        @block.gpsimd
        def _(pool):
            nc.gpsimd.memset(keep["Mbd"][:], 0.0)
            for j in range(SHARED):
                prod, rest, us, ws = reflection(j, VM, NM)
                pool.wait_ge(columns, j + 1)
                nc.gpsimd.tensor_tensor(prod, rest, us, ALU.mult).then_inc(prods, 1)
                pool.wait_ge(coeffs, j + 1)
                nc.gpsimd.tensor_tensor(prod, us, ws, ALU.mult).then_inc(spans, 1)
                pool.wait_ge(spans, j + 1)
                nc.gpsimd.tensor_tensor(rest, rest, prod, ALU.subtract).then_inc(reflected, 1)

        @block.sync
        def _(sp):
            sp.dma_start(h[:], h_tok.rearrange("(r b) s d -> (b s) r d", b=2)).then_inc(h_in, 16)
            for dst, src in ((wg, "wqk_groups"), (bg, "bqk_groups"), (ident, "ident")):
                sp.dma_start(dst[:], t[src]).then_inc(w_in, 16)
            for dst, src in ((wqk, "wqk"), (bqk, "bqk"), (headsum, "headsum"), (rowmask, "rowmask"), (wv_, "wv")):
                sp.dma_start(dst[:], t[src]).then_inc(c_in, 16)
            sp.wait_ge(m_ready, 1)
            sp.dma_start(m_dram, M[:]).then_inc(m_out, 16)
            sp.wait_ge(m_out, 16)

        @block.tensor
        def _(pe):
            pe.wait_ge(w_in, 3 * 16)
            for g in range(8):
                half, r = g % 2, g // 2
                pe.wait_ge(xn_ready, g // 4 + 1)
                if g >= 4:
                    pe.wait_ge(x_sb, g - 3)
                for j in range(4):
                    last = nc.tensor.transpose(ps[g % 4][0:HALF, HALF * j:HALF * j + HALF],
                                               xn[:, 4 * r + j, HALF * half:HALF * half + HALF], ident[0:HALF, 0:HALF])
                last.then_inc(x_ps, 1)

            def by_group(n, u):
                pe.wait_ge(st_sb, n + 1)
                if not isinstance(n, int):
                    pe.wait_ge(f_sb, n - 1)
                for j in range(ROWS):
                    for half in range(2):
                        for g in range(GROUPS):
                            last = nc.tensor.matmul(ps[6 + u][32 * g:32 * g + 32, HALF * j:HALF * j + HALF],
                                                    stage[:, u, half, j, :], wg[:, half, g, :], start=(half == 0),
                                                    stop=(half == 1))
                last.then_inc(f_ps, 1)

            for u in range(2):
                by_group(u, u)
            with pe.Fori(0, STEPS // 2 - 1) as i:
                for u in range(2):
                    by_group(i * 2 + (u + 2), u)
            pe.wait_ge(c_in, 5 * 16)
            for g in range(12):
                oh, n = g // 3, g % 3
                if g >= 4:
                    pe.wait_ge(q_sb, g - 3)
                for half in range(2):
                    last = nc.tensor.matmul(ps[g % 4][0:HALF, :], wqk[:, half, HALF * oh:HALF * oh + HALF],
                                            xT[:, half, 512 * n:512 * n + 512], start=(half == 0), stop=(half == 1))
                last.then_inc(q_ps, 1)
            pe.wait_ge(qk2_sb, 1)
            for qk in range(2):
                for n in range(3):
                    for half in range(2):
                        last = nc.tensor.matmul(ps[3 * qk + n][64 * half:64 * half + 64, :], headsum[:],
                                                qk2[:, 2 * qk + half, 512 * n:512 * n + 512], start=True, stop=True)
                    last.then_inc(n_ps, 1)
            pe.wait_ge(f_sb, STEPS)
            with pe.Fori(0, PAIRS // 2) as i:
                for u in range(2):
                    pe.wait_ge(xst_sb, i * 2 + (u + 1))
                    for bb in range(2):
                        out = ps[6 + u][0:SEQ, D * bb:D * bb + D]
                        for half in range(2):
                            last = nc.tensor.matmul(out, xst[:, u, half, SEQ * bb:SEQ * bb + SEQ], wv_[:, half, :],
                                                    start=(half == 0), stop=(half == 1))
                    last.then_inc(v_ps, 1)

        @block.scalar
        def _(act):
            act.wait_ge(eps_set, 1)
            for part in range(2):
                rows = slice(PAIRS // 2 * part, PAIRS // 2 * (part + 1))
                act.wait_ge(ln_sq, part + 1)
                nc.scalar.activation(stats[:, 2, rows], stats[:, 1, rows], ACT.Sqrt, bias=eps[:, 0:1],
                                     scale=1.0 / D).then_inc(ln_std, 1)
            for g in range(8):
                half, r = g % 2, g // 2
                act.wait_ge(x_ps, g + 1)
                nc.scalar.activation(xT[:, half, 384 * r:384 * r + 384], ps[g % 4][0:HALF, 0:384],
                                     ACT.Copy).then_inc(x_sb, 1)
            act.wait_ge(x_sb, 8)
            by_row = xT[:].rearrange("p h (b n) -> p h n b", n=SEQ)

            def staged(n, u):
                if not isinstance(n, int):
                    act.wait_ge(f_ps, n - 1)
                nc.scalar.activation(stage[:, u], by_row[:, :, bass.ds(n * ROWS, ROWS), :], ACT.Copy).then_inc(st_sb, 1)

            for u in range(2):
                staged(u, u)
            with act.Fori(0, STEPS // 2 - 1) as i:
                for u in range(2):
                    staged(i * 2 + (u + 2), u)
            act.wait_ge(c_in, 5 * 16)

            def transposed(first, last):
                for g in range(first, last):
                    oh, n = g // 3, g % 3
                    act.wait_ge(q_ps, g + 1)
                    nc.scalar.activation(qkT[:, oh, 512 * n:512 * n + 512], ps[g % 4][0:HALF, :], ACT.Identity,
                                         bias=bqk[:, oh:oh + 1]).then_inc(q_sb, 1)

            def norms(first, last):
                for n in range(first, last):
                    act.wait_ge(n_ps, n + 1)
                    dst = (qn4 if n < 3 else kn4)[:, 512 * (n % 3):512 * (n % 3) + 512]
                    nc.scalar.activation(dst, ps[n][:], ACT.Square).then_inc(n_sb, 1)

            def value_rows(first, last):
                with act.Fori(first, last) as i:
                    for u in range(2):
                        nc.scalar.activation(xst[:, u], xT[:, :, bass.ds((i * 2 + u) * PAIR, PAIR)],
                                             ACT.Copy).then_inc(xst_sb, 1)
                    for u in range(2):
                        act.wait_ge(v_ps, i * 2 + (u + 1))
                        nc.scalar.activation(v_all[:, bass.ds(i * 4 + 2 * u, 2), :],
                                             ps[6 + u][0:SEQ, 0:2 * D].rearrange("p (b d) -> p b d", b=2),
                                             ACT.Copy).then_inc(v_sb, 1)

            for j in range(HD):
                act.wait_ge(sq_sum, j + 1)
                nc.scalar.activation(nrm[:], n2[:], ACT.Sqrt).then_inc(norm_out, 1)
                if j == 0:
                    transposed(0, 8)
                elif j == 1:
                    transposed(8, 12)
                    act.wait_ge(q_sb, 12)
                    nc.scalar.activation(qk2[:], qkT[:], ACT.Square).then_inc(qk2_sb, 1)
                elif j < 4:
                    norms(3 * (j - 2), 3 * (j - 1))
                elif j < 8:
                    value_rows(j - 4, j - 3)
                elif j < 10:
                    value_rows(2 * j - 12, 2 * j - 10)

        @block.vector
        def _(v):
            ch = Steps(v, dve)
            nc.vector.memset(eps[:], LN_EPS).then_inc(eps_set, 1)
            v.wait_ge(h_in, 16)
            for part in range(2):
                rows = slice(PAIRS // 2 * part, PAIRS // 2 * (part + 1))
                centred(nc, ch, ln_sq, ln_std, h[:, rows, :], xc[:, rows, :], xn[:, rows, :], stats[:, :, rows], part + 1)
                nc.vector.tensor_tensor(xn[:, rows, :], xc[:, rows, :], spread(stats[:, 3, rows], D),
                                        ALU.mult).then_inc(xn_ready, 1)
            v.wait_ge(w_in, 3 * 16)
            with v.Fori(0, STEPS // 2) as i:
                for u in range(2):
                    v.wait_ge(f_ps, i * 2 + (u + 1))
                    nc.vector.tensor_tensor(
                        fac[:].rearrange("p m n -> p n m")[:, bass.ds((i * 2 + u) * ROWS, ROWS), :],
                        ps[6 + u][:, 0:ROWS * HALF].rearrange("p (n m) -> p n m", n=ROWS),
                        bg[:].unsqueeze(1).to_broadcast([128, ROWS, HALF]), ALU.add).then_inc(f_sb, 1)
            v.wait_ge(f_sb, STEPS)
            ch = Steps(v, house)
            op = nc.vector
            ch.then(op.memset(Xk[:], 0.0))
            for j in range(HD):
                L, C = SEQ - j, HD - 1 - j
                u = A[:, :, j, j:SEQ]
                sq = tmp[:, 0:NM * L].rearrange("p (m l) -> p m l", m=NM)
                if 0 < j <= SHARED:
                    v.wait_ge(reflected, j)
                ch.then(op.tensor_tensor(sq, u, u, ALU.mult))
                op.tensor_reduce(n2[:], sq, X, ALU.add).then_inc(sq_sum, 1)
                ch.then(op.tensor_scalar(sg[:], A[:, :, j, j], 0.0, 2.0, ALU.is_ge, ALU.mult))
                v.wait_ge(norm_out, j + 1)
                nb = sg
                ch.then(op.scalar_tensor_tensor(out=nb[:], in0=sg[:], scalar=-1.0, in1=nrm[:], op0=ALU.add,
                                                op1=ALU.mult))
                op.tensor_tensor(A[:, :, j, j], A[:, :, j, j], nb[:], ALU.add).then_inc(columns, 1)
                v.wait_ge(columns, j + 1)
                ch.mark(op.tensor_scalar(rinv[:, :, j], nb[:], -1.0, None, ALU.mult))
                if C == 0:
                    ch.wait()
                    continue
                ch.mark(op.tensor_tensor(w2[:], nb[:], A[:, :, j, j], ALU.mult))
                own = VM if j < SHARED else NM
                prod, rest, us, ws = reflection(j, 0, own)
                ch.then(op.tensor_tensor(prod, rest, us, ALU.mult))
                ch.mark(op.tensor_reduce(w[:, 0:own, 0:C], prod, X, ALU.add))
                if j < SHARED:
                    v.wait_ge(prods, j + 1)
                    ch.mark(op.tensor_reduce(w[:, VM:NM, 0:C], reflection(j, VM, NM)[0], X, ALU.add))
                ch.then(op.reciprocal(w2[:], w2[:]))
                op.tensor_tensor(w[:, :, 0:C], w[:, :, 0:C], spread(w2[:], C), ALU.mult).then_inc(coeffs, 1)
                v.wait_ge(coeffs, j + 1)
                ch.then(op.tensor_tensor(prod, us, ws, ALU.mult))
                ch.then(op.tensor_tensor(rest, rest, prod, ALU.subtract))
            ch.then(op.reciprocal(rinv[:], rinv[:]))
            for j in range(HD - 1, -1, -1):
                C = HD - 1 - j
                ch.mark(op.tensor_copy(Xk[:, :, j, j], rinv[:, GH:NM, j]))
                if C == 0:
                    ch.wait()
                    continue
                prod = tmp[:, 0:GH * C * C].rearrange("p (m c i) -> p m c i", m=GH, c=C)
                row = A[:, GH:NM, j + 1:HD, j].unsqueeze(2).to_broadcast([128, GH, C, C])
                ch.then(op.tensor_tensor(prod, Xk[:, :, j + 1:HD, j + 1:HD], row, ALU.mult))
                ch.then(op.tensor_reduce(w[:, 0:GH, 0:C], prod, X, ALU.add, negate=True))
                ch.then(op.tensor_tensor(Xk[:, :, j + 1:HD, j], w[:, 0:GH, 0:C], spread(rinv[:, GH:NM, j], C), ALU.mult))
            for j in range(HD - 1, -1, -1):
                C = HD - 1 - j
                rhs = Xk[:, :, j, :]
                if C:
                    prod = tmp[:, 0:GH * HD * C].rearrange("p (m c i) -> p m c i", m=GH, c=HD)
                    row = A[:, 0:GH, j + 1:HD, j].unsqueeze(2).to_broadcast([128, GH, HD, C])
                    ch.then(op.tensor_tensor(prod, Y[:, :, :, j + 1:HD], row, ALU.mult))
                    ch.then(op.tensor_reduce(w[:, 0:GH, :], prod, X, ALU.add))
                    ch.then(op.tensor_tensor(w[:, 0:GH, :], rhs, w[:, 0:GH, :], ALU.subtract))
                    rhs = w[:, 0:GH, :]
                ch.then(op.tensor_tensor(Y[:, :, :, j], rhs, spread(rinv[:, 0:GH, j], HD), ALU.mult))
            op.tensor_copy(M[:].rearrange("p m a c -> p m c a"), Y[:]).then_inc(m_ready, 1)
            v.wait_ge(n_sb, 6)
            v.wait_ge(c_in, 5 * 16)
            own = rowmask[:].unsqueeze(1).to_broadcast([128, TOK // 8, 8])
            by8 = qn4[:].rearrange("p (c r) -> p c r", r=8)
            ch.then(op.tensor_tensor(by8, by8, own, ALU.mult))
            ch.then(op.tensor_reduce(qn4c[:], by8, X, ALU.add))
        scope.close()
        phase.clear()


def attend(nc, t, keep, m_dram, *to_clear):
    with ExitStack() as ctx:
        def sb(name, shape, dt=F32):
            return ctx.enter_context(nc.sbuf_tensor(name, shape, dt))

        phase = Phase(nc, ctx)
        sem = phase.sem

        qkT, v_all, kn4, qn4c, Mbd, ident, oT = (keep[n] for n in ("qkT", "v_all", "kn4", "qn4c", "Mbd", "ident", "oT"))
        mask6, bv, parity = sb("mask6", [HALF, HEADS_2]), sb("bv", [HALF, 2]), sb("parity", [SEQ, 2, D])
        mix, mixr, scl, bncol = sb("mix", [128, 3, HALF]), sb("mixr", [128, 2, HALF]), sb("scl", [128, 3]), sb("bncol", [HALF, 5])
        inv, bias, eps = sb("inv", [HALF, 2]), sb("bias", [HALF, 1]), sb("eps4", [128, 2])
        CLEAR = BLOCKS * SLOT // 128 * 16
        PER = 5
        zeros = sb("zeros", [128, CLEAR])
        kst = sb("kst", [HALF, 2, PAIR])
        Mst = sb("Mst", [HALF, 2, 2, HALF])
        QX, GX = sb("QX", [HALF, 2, PAIR, HEADS_2]), sb("GX", [HALF, 2, PAIR, HEADS_2])
        S = [sb(f"S{k}", [128, 2, RCH * SEQ]) for k in range(3)]
        aq, sq, wq = (sb(n, [128, 2, RCH * SEQ]) for n in ("aq", "sq4", "wq"))
        P = sb("P", [HALF, 2, RCH, SEQ])
        mx, rs = sb("mx", [HALF, 2, RCH]), sb("rs", [HALF, 2, 2, RCH])
        pT, vst = sb("pT", [SEQ, 2, SEQ * HEADS]), sb("vst", [SEQ, 2, 2, D])
        psS = ctx.enter_context(nc.psum_tensor("psSc", [128, 2, 2, 512], F32))
        psY = ctx.enter_context(nc.psum_tensor("psY", [128, 2, 512], F32))
        psX = ctx.enter_context(nc.psum_tensor("psX", [128, 2, 512], F32))
        W = RCH * SEQ
        Yv, Tv = psY[0:HALF, :, 0:W], psX[0:SEQ, :, 0:W]
        psA = psY[0:HALF, 1, 0:D].rearrange("p (h n) -> p h n", h=2)
        psO = psX[0:HALF, :, W:W + PAIR]
        names = ("c_in4 m_in zeros cleared dve4 dve4b sk_ps gaps inv_in inv_std mix_set m_st a_ps qx kst gx s_ps s_sq s_g s_k a_sb w_sb s_r y_ps "
                 "z_sb e_sb p_sb t_ps t_sb v_st o_ps o_sb").split()
        q = {n: sem("at_" + n) for n in names}
        scope = ctx.enter_context(ExitStack())
        block = scope.enter_context(nc.Block())

        def has_before(p):
            return not isinstance(p, int) or p > 0

        def pair(a, p, axis_len=PAIR):
            return a[:, :, bass.ds(p * axis_len, axis_len)]

        @block.sync
        def _(sp):
            for dst, src in ((mask6, "mask6"), (mix, "mix"), (bncol, "bncol"), (bv, "bv"), (parity, "parity")):
                sp.dma_start(dst[:], t[src]).then_inc(q["c_in4"], 16)
            for dst, src in ((mixr, "bnrow"), (scl, "scales")):
                sp.dma_start(dst[:], t[src].partition_broadcast(128)).then_inc(q["c_in4"], 16)
            for half in range(2):
                for h in range(HEADS_2):
                    g, m = divmod(HEADS_2 * half + h, GH)
                    sp.dma_start(Mbd[HD * h:HD * h + HD, half, :, HD * h:HD * h + HD],
                                 m_dram[B * g:B * g + B, m].rearrange("b a c -> a b c")).then_inc(q["m_in"], 16)
            sp.wait_ge(q["zeros"], 1)
            for dram in to_clear:
                rows = dram.rearrange("(p r) d -> p (r d)", p=128)
                for n in range(0, rows.shape[1], CLEAR):
                    sp.dma_start(rows[:, n:n + CLEAR], zeros[:]).then_inc(q["cleared"], 16)
            sp.wait_ge(q["cleared"], 16 * sum(dram.shape[0] * dram.shape[1] // (128 * CLEAR) for dram in to_clear))

        @block.gpsimd
        def _(pool):
            def rows_by_head(p):
                if has_before(p):
                    pool.wait_ge(q["sk_ps"], p)
                nc.gpsimd.tensor_tensor(QX[:], spread(pair(qkT[:, 0:2], p), HEADS_2),
                                        mask6[:].unsqueeze(1).unsqueeze(1).to_broadcast([HALF, 2, PAIR, HEADS_2]),
                                        ALU.mult).then_inc(q["qx"], 1)

            def matrices(p):
                if has_before(p):
                    pool.wait_ge(q["a_ps"], p)
                nc.gpsimd.tensor_copy(Mst[:], Mbd[:, :, bass.ds(p * 2, 2), :]).then_inc(q["m_st"], 1)

            def keys_and_norms(p):
                if has_before(p):
                    pool.wait_ge(q["s_ps"], p)
                nc.gpsimd.tensor_copy(kst[:], pair(qkT[:, 2:4], p)).then_inc(q["kst"], 1)
                if has_before(p):
                    pool.wait_ge(q["w_sb"], p)
                nc.gpsimd.tensor_tensor(
                    aq[:].rearrange("p b (c m) -> p b c m", c=RCH),
                    kn4[:, bass.ds(p * PAIR, PAIR)].rearrange("p (b m) -> p b m", b=2).unsqueeze(2).to_broadcast([128, 2, RCH, SEQ]),
                    spread(qn4c[:, bass.ds(p * 2 * RCH, 2 * RCH)].rearrange("p (b c) -> p b c", b=2), SEQ),
                    ALU.add).then_inc(q["a_sb"], 1)

            def values_staged(p):
                if has_before(p):
                    pool.wait_ge(q["o_ps"], p)
                nc.gpsimd.tensor_tensor(vst[:], v_all[:, bass.ds(p * 2, 2), :].unsqueeze(1).to_broadcast([SEQ, 2, 2, D]),
                                        parity[:].unsqueeze(2).to_broadcast([SEQ, 2, 2, D]), ALU.mult).then_inc(q["v_st"], 1)

            def turn(i, last=False):
                keys_and_norms(i + 1)
                values_staged(i)
                if not last:
                    matrices(i + 2)
                    rows_by_head(i + 2)

            nc.gpsimd.memset(zeros[:], 0.0).then_inc(q["zeros"], 1)
            pool.wait_ge(q["c_in4"], 7 * 16)
            pool.wait_ge(q["m_in"], 12 * 16)
            matrices(0)
            rows_by_head(0)
            keys_and_norms(0)
            matrices(1)
            rows_by_head(1)
            turn(0)
            with pool.Fori(0, PAIRS - 3) as i:
                turn(i + 1)
            turn(PAIRS - 2, last=True)
            values_staged(PAIRS - 1)

        @block.tensor
        def _(pe):
            def keys(p):
                pe.wait_ge(q["m_st"], p + 1)
                for half in range(2):
                    for bb in range(2):
                        last = nc.tensor.matmul(psA[:, half, SEQ * bb:SEQ * bb + SEQ], Mst[:, half, bb, :],
                                                qkT[:, half, bass.ds((p * 2 + bb) * SEQ, SEQ)], start=True, stop=True)
                last.then_inc(q["a_ps"], 1)

            def scores(p, kind, bb):
                rows = (QX, GX)[kind]
                if kind == 0 and bb == 0:
                    if has_before(p):
                        pe.wait_ge(q["s_k"], p)
                    pe.wait_ge(q["qx"], p + 1)
                    pe.wait_ge(q["kst"], p + 1)
                if kind == 1 and bb == 0:
                    pe.wait_ge(q["gx"], p + 1)
                for c in range(RCH):
                    for half in range(2):
                        last = nc.tensor.matmul(
                            psS[64 * half:64 * half + SEQ, kind, bb, SEQ * c:SEQ * c + SEQ],
                            rows[:, half, SEQ * bb + 8 * c:SEQ * bb + 8 * c + 8, :].rearrange("p n h -> p (n h)"),
                            kst[:, half, SEQ * bb:SEQ * bb + SEQ], start=True, stop=True)
                if bb:
                    last.then_inc(q["s_ps"] if kind else q["sk_ps"], 1)

            def mixed(p, last_pair=False):
                pe.wait_ge(q["s_g"], p + 1)
                pe.wait_ge(q["s_k"], p + 1)
                if not last_pair:
                    pe.wait_ge(q["gx"], p + 2)
                for k in (0, 2, 1):
                    if k == 1:
                        pe.wait_ge(q["s_r"], p + 1)
                    for bb in range(2):
                        last = nc.tensor.matmul(Yv[:, bb, :], mix[:, k, :], S[k][:, bb, :], start=(k == 0), stop=(k == 1))
                last.then_inc(q["y_ps"], 1)

            def weights_turned(p, bb):
                if bb == 0:
                    if has_before(p):
                        pe.wait_ge(q["o_sb"], p)
                    pe.wait_ge(q["p_sb"], p + 1)
                else:
                    pe.wait_ge(q["t_sb"], p * 2 + 1)
                nc.tensor.transpose(psX[0:HALF, 0, 0:HALF], P[:, bb, 0:2, :].rearrange("p c m -> p (c m)"),
                                    ident[0:HALF, 0:HALF])
                for c in range(1, RCH):
                    last = nc.tensor.transpose(Tv[:, c // 3, HALF * (c % 3):HALF * (c % 3) + HALF], P[:, bb, c, :],
                                               ident[0:HALF, 0:HALF])
                last.then_inc(q["t_ps"], 1)

            def values(p, bb):
                if bb == 0:
                    pe.wait_ge(q["v_st"], p + 1)
                    pe.wait_ge(q["t_sb"], p * 2 + 2)
                    nc.tensor.matmul(psX[0:HALF, 0, W + D:W + D + 1], pT[:, 0, 0:HALF], vst[:, 0, 0, 0:1],
                                     start=True, stop=True)
                for half in range(2):
                    for odd in range(2):
                        for two in range(HEADS_2 // 2):
                            o = HEADS_2 * half + 2 * two + odd
                            last = nc.tensor.matmul(psO[32 * two:32 * two + 32, half, SEQ * bb:SEQ * bb + SEQ],
                                                    vst[:, odd, bb, HALF * half + 32 * two:HALF * half + 32 * two + 32],
                                                    pT[:, bb, o:SEQ * HEADS:HEADS], start=(odd == 0), stop=(odd == 1))
                if bb:
                    last.then_inc(q["o_ps"], 1)

            def turn(i):
                weights_turned(i - 1, 0)
                keys(i + 1)
                weights_turned(i - 1, 1)
                mixed(i)
                values(i - 1, 0)
                values(i - 1, 1)
                scores(i + 1, 0, 0)
                scores(i + 1, 0, 1)
                scores(i + 1, 1, 0)
                scores(i + 1, 1, 1)

            pe.wait_ge(q["gaps"], 1)
            pe.wait_ge(q["mix_set"], 1)
            keys(0)
            for kind in range(2):
                for bb in range(2):
                    scores(0, kind, bb)
            keys(1)
            scores(1, 0, 0)
            mixed(0)
            scores(1, 0, 1)
            scores(1, 1, 0)
            scores(1, 1, 1)
            turn(1)
            with pe.Fori(0, PAIRS - 3) as i:
                turn(i + 2)
            for bb in range(2):
                weights_turned(PAIRS - 2, bb)
            mixed(PAIRS - 1, last_pair=True)
            for bb in range(2):
                values(PAIRS - 2, bb)
            for bb in range(2):
                weights_turned(PAIRS - 1, bb)
            for bb in range(2):
                values(PAIRS - 1, bb)

        @block.scalar
        def _(act):
            def first_scores(p):
                act.wait_ge(q["sk_ps"], p + 1)
                nc.scalar.activation(sq[:], psS[:, 0, :, 0:W], ACT.Square, scale=float(np.sqrt(2.0))).then_inc(q["s_sq"], 1)
                nc.scalar.activation(S[0][:], psS[:, 0, :, 0:W], ACT.Copy).then_inc(q["s_k"], 1)

            def grass_scores(p):
                act.wait_ge(q["s_ps"], p + 1)
                nc.scalar.activation(S[2][:], psS[:, 1, :, 0:W], ACT.Square).then_inc(q["s_g"], 1)

            def roots(p):
                act.wait_ge(q["w_sb"], p + 1)
                nc.scalar.activation(S[1][:], wq[:], ACT.Sqrt).then_inc(q["s_r"], 1)

            def exponents(p):
                act.wait_ge(q["z_sb"], p + 1)
                nc.scalar.activation(P[:], P[:], ACT.Exp).then_inc(q["e_sb"], 1)

            def weights_out(p, bb):
                act.wait_ge(q["t_ps"], p * 2 + (bb + 1))
                nc.scalar.activation(pT[:, bb, :].rearrange("p (a n) -> p a n", a=2), Tv, ACT.Copy).then_inc(q["t_sb"], 1)

            def turn(i):
                weights_out(i - 1, 0)
                roots(i)
                weights_out(i - 1, 1)
                finish(i)

            def finish(i):
                exponents(i)
                first_scores(i + 1)
                grass_scores(i + 1)

            act.wait_ge(q["inv_in"], 1)
            act.wait_ge(q["c_in4"], 7 * 16)
            nc.scalar.activation(mixr[:, 1, :], mixr[:, 1, :], ACT.Sqrt, bias=eps[:, 0:1])
            nc.scalar.activation(inv[:, 0:1], bncol[:, 4:5], ACT.Sqrt, bias=eps[0:HALF, 0:1]).then_inc(q["inv_std"], 1)
            first_scores(0)
            grass_scores(0)
            roots(0)
            finish(0)
            with act.Fori(0, PAIRS - 2) as i:
                turn(i + 1)
            weights_out(PAIRS - 2, 0)
            roots(PAIRS - 1)
            weights_out(PAIRS - 2, 1)
            exponents(PAIRS - 1)
            for bb in range(2):
                weights_out(PAIRS - 1, bb)

        @block.vector
        def _(v):
            op = nc.vector

            def grass_rows(p):
                v.wait_ge(q["a_ps"], p + 1)
                op.tensor_tensor(GX[:], spread(psA, HEADS_2),
                                 mask6[:].unsqueeze(1).unsqueeze(1).to_broadcast([HALF, 2, PAIR, HEADS_2]),
                                 ALU.mult).then_inc(q["gx"], 1)

            def riemannian(p, ch):
                v.wait_ge(q["s_sq"], p + 1)
                v.wait_ge(q["a_sb"], p + 1)
                ch.then(op.tensor_tensor(wq[:], aq[:], sq[:], ALU.subtract))
                op.tensor_scalar(wq[:], wq[:], 0.0, 1e-8, ALU.max, ALU.add).then_inc(q["w_sb"], 1)

            def less_max(p, ch):
                v.wait_ge(q["y_ps"], p + 1)
                Y = Yv.rearrange("p b (c m) -> p b c m", c=RCH)
                ch.then(op.tensor_reduce(mx[:], Y, X, ALU.max))
                ch.then(op.tensor_scalar(mx[:], mx[:], bias[:, 0:1], None, ALU.add))
                for bb in range(2):
                    last = op.scalar_tensor_tensor(out=P[:, bb], in0=Y[:, bb], scalar=bias[:, 0:1],
                                                   in1=spread(mx[:, bb], SEQ), op0=ALU.add, op1=ALU.subtract)
                last.then_inc(q["z_sb"], 1)

            def normalised(p, ch):
                v.wait_ge(q["e_sb"], p + 1)
                ch.then(op.tensor_reduce(rs[:, 0], P[:], X, ALU.add))
                ch.then(op.reciprocal(rs[:, 1], rs[:, 0]))
                flat = P[:].rearrange("p b c m -> p (b c) m")
                op.tensor_tensor(flat, flat, spread(rs[:, 1].rearrange("p b c -> p (b c)"), SEQ), ALU.mult).then_inc(q["p_sb"], 1)

            def outputs(p):
                v.wait_ge(q["o_ps"], p + 1)
                for half in range(2):
                    last = op.tensor_scalar(oT[:, half, bass.ds(p * PAIR, PAIR)], psO[:, half], bv[:, half:half + 1], None,
                                            ALU.add)
                last.then_inc(q["o_sb"], 1)

            def turn(i, ch):
                grass_rows(i + 1)
                less_max(i, ch)
                if has_before(i):
                    outputs(i - 1)
                normalised(i, ch)
                riemannian(i + 1, ch)
                assert ch.n == PER

            op.memset(psS[:], 0.0).then_inc(q["gaps"], 1)
            op.memset(eps[:], LN_EPS).then_inc(q["inv_in"], 1)
            ch = Steps(v, q["dve4"])
            v.wait_ge(q["c_in4"], 7 * 16)
            v.wait_ge(q["inv_std"], 1)
            ch.mark(op.reciprocal(mixr[:, 1, :], mixr[:, 1, :]))
            ch.then(op.reciprocal(inv[:, 1:2], inv[:, 0:1]))
            ch.mark(op.tensor_tensor(mixr[:, 0, :], mixr[:, 0, :], mixr[:, 1, :], ALU.mult))
            ch.mark(op.tensor_tensor(inv[:, 1:2], inv[:, 1:2], bncol[:, 2:3], ALU.mult))
            ch.mark(op.tensor_scalar(scl[:, 1:2], scl[:, 1:2], -1.0, None, ALU.mult))
            ch.then(op.tensor_tensor(bias[:], bncol[:, 0:1], bncol[:, 1:2], ALU.subtract))
            ch.then(op.scalar_tensor_tensor(out=bias[:], in0=bias[:], scalar=inv[:, 1:2], in1=bncol[:, 3:4],
                                            op0=ALU.mult, op1=ALU.add))
            for k in range(3):
                last = op.scalar_tensor_tensor(out=mix[:, k, :], in0=mix[:, k, :], scalar=scl[:, k:k + 1],
                                               in1=mixr[:, 0, :], op0=ALU.mult, op1=ALU.mult)
            last.then_inc(q["mix_set"], 1)
            ch = Steps(v, q["dve4b"])
            grass_rows(0)
            riemannian(0, ch)
            turn(0, Steps(v, q["dve4b"], base=1))
            turn(1, Steps(v, q["dve4b"], base=1 + PER))
            with v.Fori(0, PAIRS - 3) as i:
                turn(i + 2, Steps(v, q["dve4b"], base=1 + 2 * PER, turn=i, per=PER))
            ch = Steps(v, q["dve4b"], base=1 + PER * (PAIRS - 1))
            less_max(PAIRS - 1, ch)
            outputs(PAIRS - 2)
            normalised(PAIRS - 1, ch)
            outputs(PAIRS - 1)
        scope.close()
        phase.clear()


def scatter(nc, rows, pos, i, bank, slots_in, scat):
    for k in range(TOPK):
        nc.gpsimd.indirect_dma_start(slots_in, bass.IndirectOffsetOnAxis(pos[:, 2 * i + bank, k:k + 1], 0),
                                     rows, None).then_inc(scat, 16)


def route(nc, t, keep, xn_dram, h_dram, x_slots, scat):
    with ExitStack() as ctx:
        def sb(name, shape, dt=F32):
            return ctx.enter_context(nc.sbuf_tensor(name, shape, dt))

        h, xT, oT, ident = keep["h"], keep["xT"], keep["oT"], keep["ident"]
        pos, w4, eid, xr = keep["pos"], keep["w4"], keep["eid"], keep["rows_in"]
        xc, sq, stats = sb("xc5", [HALF, PAIRS, D]), sb("sq5", [HALF, PAIRS, D]), sb("stats5", [HALF, 4, PAIRS])
        projT, projb = sb("projT5", [HALF, 2, D]), sb("projb5", [HALF, D])
        ones = sb("ones5", [128, 128])
        eps = sb("eps5", [128, 1])
        Wf, bf = sb("Wf", [HALF, 2, 128]), sb("bf", [128, 1])
        emb, emb2, est = sb("emb", [128, 2, 64]), sb("emb2", [128, 2, 64]), sb("est", [128, 3, 2])
        embT, fT = sb("embT", [128, 128]), sb("fT", [128, TOK])
        upper, iota = sb("upper", [128, 128]), sb("iota", [128, BLOCKS])
        L, prod = sb("L", [128, FT, 2, NEUR]), sb("prod5", [128, FT, 2, NEUR])
        O = [sb(f"O{k}", [128, FT, 2, NEUR]) for k in range(TOPK)]
        cum = sb("cum", [128, FT, 2 * NEUR])
        red, vals, idx, idf = (sb("red", [128, 2, 2 * FT]), sb("vals", [128, 2 * FT, 8]),
                               sb("idx", [128, 2 * FT, 8], U32), sb("idf5", [128, 2 * FT, TOPK]))
        posf = sb("posf", [128, 2 * FT, TOPK])
        cnt, cnti, nbf = sb("cnt", [128, 2]), sb("cnti", [128, 2, 2], I32), sb("nbf", [128, 2])
        nbw, start, endc = sb("nbw", [128, 2, NEUR]), sb("start", [128, 2 * NEUR]), sb("endc", [128, 2])
        gt, ef = sb("gt", [128, 2, BLOCKS]), sb("ef", [1, 2 * BLOCKS])
        ps = [ctx.enter_context(nc.psum_tensor(f"psr{i}", [128, 512], F32)) for i in range(8)]
        names = ("c_in dve set_up o_ps h_sb ln_sq ln_std xn xn_out h_out xr_in x_ps x_sb e_sq e_std e_n e_ps e_sb f_ps f_sb "
                 "l_ps l_sb l_sub l_exp hot hot_sum placed pos_set cums r_ps r_sb c_ps nb st_ps en_ps gts b_ps").split()
        phase = Phase(nc, ctx)
        q = {n: phase.sem("rt_" + n) for n in names}
        LBANK = [0, 3, 1, 5, 2, 6]
        scope = ctx.enter_context(ExitStack())
        block = scope.enter_context(nc.Block())

        @block.sync
        def _(sp):
            sp.dma_start(projb[:], t["attn_projb"].partition_broadcast(HALF)).then_inc(q["c_in"], 16)
            for dst, src in ((projT, "attn_projT"), (Wf, "Wf"), (bf, "bf"), (emb, "emb"),
                             (upper, "upper"), (iota, "iota")):
                sp.dma_start(dst[:], t[src]).then_inc(q["c_in"], 16)
            sp.wait_ge(q["h_sb"], 8)
            sp.dma_start(h_dram.rearrange("(r p) d -> p r d", p=PAIR), h[:]).then_inc(q["h_out"], 16)
            sp.wait_ge(q["xn"], 2)
            sp.dma_start(xn_dram.rearrange("(r p) d -> p r d", p=PAIR), sq[:]).then_inc(q["xn_out"], 16)
            sp.wait_ge(q["xn_out"], 16)
            sp.dma_start(xr[:], xn_dram.rearrange("(t p) d -> p t d", p=128)).then_inc(q["xr_in"], 16)
            sp.wait_ge(q["xr_in"], 16)
            sp.wait_ge(q["h_out"], 16)

        @block.tensor
        def _(pe):
            pe.wait_ge(q["c_in"], 7 * 16)
            pe.wait_ge(q["set_up"], 1)
            for g in range(8):
                if g >= 4:
                    pe.wait_ge(q["h_sb"], g - 3)
                for j in range(2):
                    out = ps[g % 4][0:HALF, D * j:D * j + D]
                    for half in range(2):
                        last = nc.tensor.matmul(out, oT[:, half, PAIR * (2 * g + j):PAIR * (2 * g + j + 1)],
                                                projT[:, half, :], start=(half == 0), stop=(half == 1))
                last.then_inc(q["o_ps"], 1)
            pe.wait_ge(q["e_n"], 1)
            nc.tensor.transpose(ps[4][:, 0:128], emb2[:].rearrange("p f d -> p (f d)"), ident[:]).then_inc(q["e_ps"], 1)
            for g in range(8):
                half, r = g % 2, g // 2
                pe.wait_ge(q["xn"], g // 4 + 1)
                if g < 4:
                    pe.wait_ge(q["h_sb"], 5 + g)
                else:
                    pe.wait_ge(q["x_sb"], g - 3)
                for j in range(4):
                    last = nc.tensor.transpose(ps[g % 4][0:HALF, HALF * j:HALF * j + HALF],
                                               sq[:, 4 * r + j, HALF * half:HALF * half + HALF], ident[0:HALF, 0:HALF])
                last.then_inc(q["x_ps"], 1)
            pe.wait_ge(q["x_sb"], 8)
            for n in range(3):
                for half in range(2):
                    last = nc.tensor.matmul(ps[5 + n][:], Wf[:, half, :], xT[:, half, 512 * n:512 * n + 512],
                                            start=(half == 0), stop=(half == 1))
                last.then_inc(q["f_ps"], 1)
            pe.wait_ge(q["e_sb"], 1)
            pe.wait_ge(q["f_sb"], 3)
            for g in range(6):
                n, f = g // 2, g % 2
                for j in range(4):
                    last = nc.tensor.matmul(ps[LBANK[g]][:, 128 * j:128 * j + 128],
                                            fT[64 * f:64 * f + 64, 128 * (4 * n + j):128 * (4 * n + j + 1)],
                                            embT[64 * f:64 * f + 64, :], start=True, stop=True)
                last.then_inc(q["l_ps"], 1)
            pe.wait_ge(q["cums"], 1)
            nc.tensor.matmul(ps[4][:, 0:1], cum[:, FT - 1, 0:NEUR], ones[:, 0:1], start=True, stop=True)
            nc.tensor.matmul(ps[4][:, 1:2], cum[:, FT - 1, NEUR:], ones[:, 0:1], start=True, stop=True).then_inc(q["c_ps"], 1)
            def earlier(i):
                if i < 4:
                    pe.wait_ge(q["l_sb"], 6)
                else:
                    pe.wait_ge(q["r_sb"], i - 3)
                last = nc.tensor.matmul(ps[i % 4][:, 0:256], upper[:], L[:, i].rearrange("p f e -> p (f e)"), start=True,
                                        stop=(i == 0))
                if i:
                    last = nc.tensor.matmul(ps[i % 4][:, 0:256], ones[:], cum[:, i - 1, :], start=False, stop=True)
                last.then_inc(q["r_ps"], 1)

            for i in range(4):
                earlier(i)
            pe.wait_ge(q["nb"], 1)
            for f in range(2):
                last = nc.tensor.matmul(ps[5][:, 128 * f:128 * f + 128], nbw[:, f, :], upper[:], start=True, stop=True)
            last.then_inc(q["st_ps"], 1)
            nc.tensor.matmul(ps[6][:, 0:2], upper[:], nbf[:], start=True, stop=False)
            nc.tensor.matmul(ps[6][:, 0:2], ident[:], nbf[:], start=False, stop=True).then_inc(q["en_ps"], 1)
            for i in range(4, FT):
                earlier(i)
            pe.wait_ge(q["gts"], 1)
            nc.tensor.matmul(ps[7][0:1, 0:2 * BLOCKS], ones[:, 0:1], gt[:].rearrange("p f j -> p (f j)"), start=True,
                             stop=True).then_inc(q["b_ps"], 1)

        @block.scalar
        def _(act):
            act.wait_ge(q["set_up"], 1)
            act.wait_ge(q["e_sq"], 1)
            nc.scalar.activation(est[:, 1], est[:, 0], ACT.Sqrt).then_inc(q["e_std"], 1)
            for part in range(2):
                rows = slice(PAIRS // 2 * part, PAIRS // 2 * (part + 1))
                act.wait_ge(q["ln_sq"], part + 1)
                nc.scalar.activation(stats[:, 2, rows], stats[:, 1, rows], ACT.Sqrt, bias=eps[0:HALF],
                                     scale=1.0 / D).then_inc(q["ln_std"], 1)
            act.wait_ge(q["e_ps"], 1)
            nc.scalar.activation(embT[:], ps[4][:, 0:128], ACT.Copy).then_inc(q["e_sb"], 1)
            for g in range(8):
                half, r = g % 2, g // 2
                act.wait_ge(q["x_ps"], g + 1)
                nc.scalar.activation(xT[:, half, 384 * r:384 * r + 384], ps[g % 4][0:HALF, 0:384],
                                     ACT.Copy).then_inc(q["x_sb"], 1)
            for n in range(3):
                act.wait_ge(q["f_ps"], n + 1)
                nc.scalar.activation(fT[:, 512 * n:512 * n + 512], ps[5 + n][:], ACT.Identity,
                                     bias=bf[:]).then_inc(q["f_sb"], 1)
            for g in range(6):
                act.wait_ge(q["l_ps"], g + 1)
                nc.scalar.activation(L[:, 4 * (g // 2):4 * (g // 2) + 4, g % 2, :],
                                     ps[LBANK[g]][:].rearrange("p (t e) -> p t e", t=4), ACT.Copy).then_inc(q["l_sb"], 1)
            act.wait_ge(q["l_sub"], 1)
            nc.scalar.activation(L[:], L[:], ACT.Exp).then_inc(q["l_exp"], 1)

        places = cum[:].rearrange("p t (f e) -> p t f e", f=2)

        @block.gpsimd
        def _(pool):
            pool.wait_ge(q["hot"], 2)
            nc.gpsimd.tensor_tensor(prod[:], O[0][:], O[1][:], ALU.add).then_inc(q["hot_sum"], 1)
            pool.wait_ge(q["r_sb"], FT)
            nc.gpsimd.tensor_tensor(O[3][:, :, 0], O[3][:, :, 0], places[:, :, 0], ALU.mult).then_inc(q["placed"], 1)
            pool.wait_ge(q["xr_in"], 16)
            pool.wait_ge(q["pos_set"], 1)
            for i in range(FT):
                scatter(nc, xr[:, i, :], pos, i, 0, x_slots, scat)

        @block.vector
        def _(v):
            op = nc.vector
            ch = Steps(v, q["dve"])
            ch.then(op.memset(ones[:], 1.0))
            op.memset(eps[:], LN_EPS).then_inc(q["set_up"], 1)
            v.wait_ge(q["c_in"], 7 * 16)
            ch.then(op.tensor_tensor(emb2[:], emb[:], emb[:], ALU.mult))
            op.tensor_reduce(est[:, 0], emb2[:], X, ALU.add).then_inc(q["e_sq"], 1)
            v.wait_ge(q["e_std"], 1)
            ch.then(op.tensor_scalar(est[:, 1], est[:, 1], 1e-8, None, ALU.add))
            ch.then(op.reciprocal(est[:, 2], est[:, 1]))
            op.tensor_tensor(emb2[:], emb[:], spread(est[:, 2], 64), ALU.mult).then_inc(q["e_n"], 1)
            ch.then(op.tensor_tensor(h[:], h[:], projb[:].unsqueeze(1).to_broadcast([HALF, PAIRS, D]), ALU.add))
            for part in range(2):
                for g in range(4 * part, 4 * part + 4):
                    v.wait_ge(q["o_ps"], g + 1)
                    hh = h[:, 2 * g:2 * g + 2, :]
                    op.tensor_tensor(hh, hh, ps[g % 4][0:HALF, 0:2 * D].rearrange("p (r d) -> p r d", r=2),
                                     ALU.add).then_inc(q["h_sb"], 1)
                v.wait_ge(q["h_sb"], 4 * part + 4)
                rows = slice(PAIRS // 2 * part, PAIRS // 2 * (part + 1))
                centred(nc, ch, q["ln_sq"], q["ln_std"], h[:, rows, :], xc[:, rows, :], sq[:, rows, :], stats[:, :, rows], part + 1)
                op.tensor_tensor(sq[:, rows, :], xc[:, rows, :], spread(stats[:, 3, rows], D), ALU.mult).then_inc(q["xn"], 1)
            v.wait_ge(q["l_sb"], 6)
            rows = L[:].rearrange("p t f e -> p (t f) e")
            ch.then(op.tensor_reduce(red[:, 0], rows, X, ALU.max))
            op.tensor_tensor(rows, rows, spread(red[:, 0], NEUR), ALU.subtract).then_inc(q["l_sub"], 1)
            v.wait_ge(q["l_exp"], 1)
            ch.mark(op.tensor_reduce(red[:, 0], rows, X, ALU.add))
            for r in range(2 * FT):
                ch.mark(op.max(vals[:, r, :], rows[:, r, :]))
            ch.wait()
            for r in range(2 * FT):
                ch.mark(op.max_index(idx[:, r, :], vals[:, r, :], rows[:, r, :]))
            ch.then(op.reciprocal(red[:, 1], red[:, 0]))
            ch.then(op.tensor_tensor(vals[:, :, 0:TOPK], vals[:, :, 0:TOPK], spread(red[:, 1], TOPK), ALU.mult))
            ch.mark(op.tensor_reduce(red[:, 0], vals[:, :, 0:TOPK], X, ALU.add))
            ch.wait()
            ch.mark(op.tensor_copy(idf[:], idx[:, :, 0:TOPK]))
            ch.then(op.tensor_scalar(red[:, 0], red[:, 0], 1e-8, None, ALU.add))
            ch.then(op.reciprocal(red[:, 1], red[:, 0]))
            ch.mark(op.tensor_tensor(w4[:], vals[:, :, 0:TOPK], spread(red[:, 1], TOPK), ALU.mult))
            for k in range(TOPK):
                op.tensor_tensor(O[k][:].rearrange("p t f e -> p (t f) e"),
                                 iota[:, 0:NEUR].unsqueeze(1).to_broadcast([128, 2 * FT, NEUR]),
                                 spread(idf[:, :, k], NEUR), ALU.is_equal).then_inc(q["hot"], 1)
            v.wait_ge(q["hot"], TOPK)
            ch.then(op.tensor_tensor(L[:], O[2][:], O[3][:], ALU.add))
            v.wait_ge(q["hot_sum"], 1)
            ch.then(op.tensor_tensor(L[:], L[:], prod[:], ALU.add))
            by_tile = L[:].rearrange("p t f e -> p t (f e)")
            ch.then(op.tensor_copy(cum[:, 0, :], by_tile[:, 0]))
            for i in range(1, FT):
                ch.then(op.tensor_tensor(cum[:, i, :], cum[:, i - 1, :], by_tile[:, i], ALU.add))
            op.memset(red[:, 0, 0:1], 0.0).then_inc(q["cums"], 1)
            v.wait_ge(q["c_ps"], 1)
            ch.then(op.tensor_scalar(cnt[:], ps[4][:, 0:2], float(SLOT - 1), None, ALU.add))
            ch.then(op.tensor_copy(cnti[:, 0], cnt[:]))
            ch.then(op.tensor_scalar(cnti[:, 1], cnti[:, 0], SLOT.bit_length() - 1, None, ALU.arith_shift_right))
            ch.then(op.tensor_copy(nbf[:], cnti[:, 1]))
            op.tensor_copy(nbw[:], spread(nbf[:], NEUR)).then_inc(q["nb"], 1)
            v.wait_ge(q["st_ps"], 1)
            ch.mark(op.tensor_scalar(start[:], ps[5][:, 0:256], float(SLOT), None, ALU.mult))
            v.wait_ge(q["en_ps"], 1)
            ch.then(op.tensor_copy(endc[:], ps[6][:, 0:2]))
            for f in range(2):
                last = op.tensor_scalar(gt[:, f, :], iota[:], endc[:, f:f + 1], None, ALU.is_ge)
            last.then_inc(q["gts"], 1)
            for i in range(FT):
                v.wait_ge(q["r_ps"], min(i + 2, FT))
                op.tensor_tensor(cum[:, i, :], ps[i % 4][:, 0:256], start[:], ALU.add).then_inc(q["r_sb"], 1)
            v.wait_ge(q["r_sb"], FT)
            for f in range(2):
                to, from_ = (a[:].rearrange("p (t f) k -> p t f k", f=2)[:, :, f] for a in (pos, posf))
                for k in range(TOPK):
                    if f == 0 and k == TOPK - 1:
                        v.wait_ge(q["placed"], 1)
                        ch.then(op.tensor_reduce(from_[:, :, k], O[k][:, :, 0], X, ALU.add))
                    else:
                        ch.then(op.tensor_tensor(prod[:, :, f], O[k][:, :, f], places[:, :, f], ALU.mult))
                        ch.then(op.tensor_reduce(from_[:, :, k], prod[:, :, f], X, ALU.add))
                op.tensor_copy(to, from_).then_inc(q["pos_set"], 1)
            v.wait_ge(q["b_ps"], 1)
            ch.then(op.tensor_scalar(ef[:], ps[7][0:1, 0:2 * BLOCKS], float(NEUR - 1), None, ALU.min))
            ch.then(op.tensor_copy(eid[:], ef[:]))
        scope.close()
        phase.clear()


def routed_bank(nc, phase, ctx, keep, psT, psO, banks_free, bank, scat, gath, w_in, w_out, slots_in, slots_out, weights,
                out_rows, following=None, tail=None):
    HW = min(w_in, HALF) if w_in == D else w_in
    PARTS = w_in // HW
    TILE, BPT, GRP, PPG = 128, 128 // SLOT, 4, 2
    PPT = 2 * PPG
    BPP = 2 * BPT
    GATHERS, TPG = 4, FT // 4
    TURNS = BLOCKS // (PPT * BPP)
    assert BLOCKS % (PPT * BPP) == 0
    def sb(name, shape, dt=F32):
        return ctx.enter_context(nc.sbuf_tensor(f"{name}_b{bank}", shape, dt))

    pos, w4, eid, ident = (keep[n] for n in ("pos", "w4", "eid", "ident"))
    xb = [sb(f"xb{g}", [TILE, GRP, w_in]) for g in range(2)]
    yb = [sb(f"yb{g}", [TILE, GRP, w_out]) for g in range(2)]
    wb = [sb(f"wb{u}", [HW, PARTS, w_out]) for u in range(PPT * BPP)]
    xT = [sb(f"xbT{p}", [HW, 2, PARTS, TILE]) for p in range(PPT)]
    got = sb("got", [128, FT, TOPK, w_out])
    if tail:
        h_in, h_out, xn_out, bias = tail
        biasr, eps = sb("biasr", [128, D]), sb("eps", [128, 1])
        xnt, sq = sb("xnt", [128, FT, D]), sb("sq", [128, TPG, D])
        stats, l2 = sb("stats", [128, 4, FT]), sb("l2", [128, 3, FT])

    def sem(n):
        return phase.sem(f"rd{bank}_{n}")

    h_ld, h_set, dve, ln_sq, ln_std, unit, u_ps, u_sb, rows_out = (sem(n) for n in (
        "h_ld", "h_set", "dve", "ln_sq", "ln_std", "unit", "u_ps", "u_sb", "rows_out"))
    x_ld, st = ([sem(f"{n}{g}") for g in range(2)] for n in ("x_ld", "st"))
    w_ld = [sem(f"w_ld{p}") for p in range(PPT)]
    t_ps, t_sb, y_ps, y_sb, acc = (sem(n) for n in ("t_ps", "t_sb", "y_ps", "y_sb", "acc"))

    def gpsimd(pool):
        for g in range(2):
            pool.wait_ge(st[g], 16 * TURNS)
        for i in range(FT):
            for k in range(TOPK):
                nc.gpsimd.indirect_dma_start(got[:, i, k, :], None, slots_out,
                                             bass.IndirectOffsetOnAxis(pos[:, 2 * i + bank, k:k + 1], 0)).then_inc(gath[i // TPG], 16)
        if following:
            for i in range(FT):
                if i % TPG == 0:
                    pool.wait_ge(acc, TPG * TOPK * (i // TPG + 1))
                scatter(nc, out_rows[:, i, :], pos, i, 1, *following)

    def load_w(eng, turn, p, part):
        cut = p * BPP + BPP // 2
        for u in range(*((cut, (p + 1) * BPP) if part else (p * BPP, cut))):
            e = eng.value_load(eid[0:1, bass.ds(turn * (PPT * BPP) + (u + bank * BLOCKS), 1)])
            eng.dma_start(wb[u][:], weights[bass.ds(e, 1)].rearrange("e (c p) n -> p (e c) n", p=HW)).then_inc(w_ld[p], 16)

    def sync(sp):
        def load_x(turn, g):
            sp.dma_start(xb[g][:], slots_in[bass.ds((turn * 2 + g) * (GRP * TILE), GRP * TILE), :].rearrange(
                "(j p) d -> p j d", p=TILE)).then_inc(x_ld[g], 16)

        if tail:
            sp.dma_start(biasr[:], bias.partition_broadcast(128)).then_inc(h_ld, 16)
            sp.dma_start(out_rows[:], h_in.rearrange("(t p) d -> p t d", p=128)).then_inc(h_ld, 16)
        if banks_free is None:
            sp.wait_ge(scat, 16 * FT * TOPK)
            load_x(0, 0)
            load_x(0, 1)
        for p in range(PPT):
            load_w(sp, 0, p, 0)
        if banks_free:
            sp.wait_ge(scat, 16 * FT * TOPK)
            load_x(0, 0)
            load_x(0, 1)
        with sp.Fori(0, TURNS - 1) as i:
            for p in range(PPT):
                if p % PPG == PPG - 1:
                    sp.wait_ge(t_ps, i * PPT + (p + 1))
                    load_x(i + 1, p // PPG)
                sp.wait_ge(y_ps, i * PPT + (p + 1))
                load_w(sp, i + 1, p, 0)
        if tail:
            sp.wait_ge(unit, GATHERS)
            for rows, dst in ((xnt, xn_out), (out_rows, h_out)):
                sp.dma_start(dst.rearrange("(t p) d -> p t d", p=128), rows[:]).then_inc(rows_out, 16)
            sp.wait_ge(rows_out, 2 * 16)

    def tensor(pe):
        def turned(i, p):
            if p % PPG == 0:
                pe.wait_ge(x_ld[p // PPG], i * 16 + 16)
            for j in range(2):
                for c in range(PARTS):
                    last = nc.tensor.transpose(psT[p][0:HW, TILE * (PARTS * j + c):TILE * (PARTS * j + c + 1)],
                                               xb[p // PPG][:, 2 * (p % PPG) + j, HW * c:HW * c + HW], ident[:])
            last.then_inc(t_ps, 1)

        def product(i, p, first):
            pe.wait_ge(w_ld[p], i * (16 * BPP) + 16 * BPP)
            if not first:
                pe.wait_ge(y_sb, i * PPT + (p - 3))
            pe.wait_ge(t_sb, i * PPT + (p + 1))
            for j in range(2):
                for c in range(PARTS):
                    for s in range(BPT):
                        rows = slice(SLOT * s, SLOT * s + SLOT)
                        last = nc.tensor.matmul(psO[p][rows, w_out * j:w_out * j + w_out], xT[p][:, j, c, rows],
                                                wb[p * BPP + BPT * j + s][:, c, :], start=(c == 0), stop=(c == PARTS - 1))
            last.then_inc(y_ps, 1)

        def turn(i, first=False, last=False):
            for p in range(PPT):
                if p + 1 < PPT:
                    turned(i, p + 1)
                elif not last:
                    turned(i + 1, 0)
                product(i, p, first)

        if banks_free:
            pe.wait_ge(*banks_free)
        turned(0, 0)
        turn(0, first=True)
        with pe.Fori(0, TURNS - 2) as i:
            turn(i + 1)
        turn(TURNS - 1, last=True)
        if tail:
            pe.wait_ge(y_sb, TURNS * PPT)
            for g in range(GATHERS):
                pe.wait_ge(unit, g + 1)
                for half in range(2):
                    for i in range(TPG):
                        last = nc.tensor.transpose((psT, psO)[half][g][0:HALF, TILE * i:TILE * i + TILE],
                                                   xnt[:, TPG * g + i, HALF * half:HALF * half + HALF], ident[:])
                last.then_inc(u_ps, 1)

    def scalar(act):
        def store(i, g):
            act.wait_ge(y_sb, i * PPT + PPG * (g + 1))
            act.dma_start(slots_out[bass.ds((i * 2 + g) * (GRP * TILE), GRP * TILE), :].rearrange(
                "(j p) n -> p j n", p=TILE), yb[g][:]).then_inc(st[g], 16)

        def turn(i, first=False, last=False):
            for p in range(PPT):
                act.wait_ge(t_ps, i * PPT + (p + 1))
                nc.scalar.activation(xT[p][:].rearrange("p j c n -> p (j c n)"), psT[p][0:HW, 0:2 * PARTS * TILE],
                                     ACT.Copy).then_inc(t_sb, 1)
                if p >= 2 and not last:
                    act.wait_ge(y_ps, i * PPT + (p - 1))
                    load_w(act, i + 1, p - 2, 1)
                if p < 2 and not first:
                    act.wait_ge(y_ps, i * PPT + (p - 1))
                    load_w(act, i, p + 2, 1)
                if p == PPT - 1:
                    store(i, 0)
                if p == 1 and not first:
                    store(i - 1, 1)

        for p in range(PPT):
            load_w(act, 0, p, 1)
        turn(0, first=True)
        with act.Fori(0, TURNS - 2) as i:
            turn(i + 1)
        turn(TURNS - 1, last=True)
        store(TURNS - 1, 1)
        if tail:
            def unit_rows_out(g):
                act.wait_ge(u_ps, g + 1)
                for half in range(2):
                    nc.scalar.activation(keep["xT"][:, half, TPG * TILE * g:TPG * TILE * (g + 1)],
                                         (psT, psO)[half][g][0:HALF, 0:TPG * TILE], ACT.Copy).then_inc(u_sb, 1)

            act.wait_ge(h_set, 1)
            for g in range(GATHERS):
                tiles = slice(TPG * g, TPG * (g + 1))
                act.wait_ge(ln_sq, g + 1)
                nc.scalar.activation(l2[:, 1, tiles], stats[:, 1, tiles], ACT.Sqrt)
                nc.scalar.activation(stats[:, 2, tiles], stats[:, 1, tiles], ACT.Sqrt, bias=eps[:],
                                     scale=1.0 / D).then_inc(ln_std, 1)
                if g:
                    unit_rows_out(g - 1)
            unit_rows_out(GATHERS - 1)

    def vector(v):
        def turn(i, first=False):
            for p in range(PPT):
                v.wait_ge(y_ps, i * PPT + (p + 1))
                if p % PPG == 0 and not first:
                    v.wait_ge(st[p // PPG], i * 16)
                b0 = 2 * (p % PPG)
                nc.vector.tensor_copy(yb[p // PPG][:, b0:b0 + 2, :].rearrange("p j n -> p (j n)"),
                                      psO[p][:, 0:2 * w_out]).then_inc(y_sb, 1)

        if tail:
            nc.vector.memset(eps[:], LN_EPS)
            v.wait_ge(h_ld, 2 * 16)
            nc.vector.tensor_tensor(out_rows[:], out_rows[:], biasr[:].unsqueeze(1).to_broadcast([128, FT, D]),
                                    ALU.add).then_inc(h_set, 1)
        turn(0, first=True)
        with v.Fori(0, TURNS - 1) as i:
            turn(i + 1)
        if tail:
            v.wait_ge(h_set, 1)
            ch = Steps(v, dve)
        n = 0
        for g in range(GATHERS):
            tiles = slice(TPG * g, TPG * (g + 1))
            v.wait_ge(gath[g], 16 * TPG * TOPK)
            for k in range(TOPK):
                for i in range(TPG * g, TPG * (g + 1)):
                    out, w = out_rows[:, i, :], w4[:, 2 * i + bank, k:k + 1]
                    if k == 0 and not tail:
                        nc.vector.tensor_scalar(out, got[:, i, k, :], w, None, ALU.mult).then_inc(acc, 1)
                    else:
                        if k:
                            v.wait_ge(acc, n - TPG + 1)
                        nc.vector.scalar_tensor_tensor(out=out, in0=got[:, i, k, :], scalar=w, in1=out, op0=ALU.mult,
                                                       op1=ALU.add).then_inc(acc, 1)
                    n += 1
            if tail:
                v.wait_ge(acc, n)
                x = xnt[:, tiles, :]
                centred(nc, ch, ln_sq, ln_std, out_rows[:, tiles, :], x, sq[:], stats[:, :, tiles], g + 1)
                ch.then(nc.vector.tensor_tensor(l2[:, 1, tiles], l2[:, 1, tiles], stats[:, 3, tiles], ALU.mult))
                ch.then(nc.vector.tensor_scalar(l2[:, 1, tiles], l2[:, 1, tiles], 1e-12, None, ALU.max))
                ch.then(nc.vector.reciprocal(l2[:, 2, tiles], l2[:, 1, tiles]))
                ch.then(nc.vector.tensor_tensor(l2[:, 2, tiles], l2[:, 2, tiles], stats[:, 3, tiles], ALU.mult))
                nc.vector.tensor_tensor(x, x, spread(l2[:, 2, tiles], D), ALU.mult).then_inc(unit, 1)
    return {"gpsimd": gpsimd, "sync": sync, "tensor": tensor, "scalar": scalar, "vector": vector}, (y_sb, TURNS * PPT)


def routed(nc, t, keep, scat, gath, x_slots, f_slots, g_slots, r_slots, h_in, h_out, xn_out, hf, h3):
    with ExitStack() as ctx:
        psT, psO = ([ctx.enter_context(nc.psum_tensor(f"{n}{p}", [128, 512], F32)) for p in range(4)]
                    for n in ("psT", "psO"))
        phase = Phase(nc, ctx)
        feature, read = routed_bank(nc, phase, ctx, keep, psT, psO, None, 0, scat[0], gath[0], D, RANK, x_slots, f_slots,
                                    t["f_know"], hf, following=(g_slots, scat[1]))
        restore, _ = routed_bank(nc, phase, ctx, keep, psT, psO, read, 1, scat[1], gath[1], RANK, D, g_slots, r_slots,
                                 t["r_know"], h3, tail=(h_in, h_out, xn_out, t["second_projb"]))
        scope = ctx.enter_context(ExitStack())
        block = scope.enter_context(nc.Block())

        @block.gpsimd
        def _(pool):
            feature["gpsimd"](pool)
            restore["gpsimd"](pool)

        @block.sync
        def _(sp):
            feature["sync"](sp)
            restore["sync"](sp)

        @block.tensor
        def _(pe):
            feature["tensor"](pe)
            restore["tensor"](pe)

        @block.scalar
        def _(act):
            feature["scalar"](act)
            restore["scalar"](act)

        @block.vector
        def _(v):
            feature["vector"](v)
            restore["vector"](v)

        scope.close()
        phase.clear()


def slots(nc, t, keep, h_dram, xn_dram, y_dram, out):
    with ExitStack() as ctx:
        def sb(name, shape, dt=F32):
            return ctx.enter_context(nc.sbuf_tensor(name + "_s", shape, dt))

        h, xT, ident = keep["h"], keep["xT"], keep["ident"]
        xn = sb("xn", [HALF, PAIRS, D])
        ones = sb("ones", [HALF, HALF])
        phi, phi2, scl, pn = sb("phi", [HALF, 2, SLOTS]), sb("phi2", [HALF, 2, SLOTS]), sb("scl", [HALF, 1]), sb("pn", [HALF, 2, SLOTS])
        dT, dred = sb("dT", [SLOTS, B, SEQ]), sb("dred", [SLOTS, 2, B])
        C, cred = sb("C", [HALF, PAIRS, SLOTS]), sb("cred", [HALF, 2, PAIRS])
        own = sb("own", [HALF, 2])
        Dp, Cp = (sb(n, [HALF, PAIRS, 2, SLOTS]) for n in ("Dp", "Cp"))
        CT = sb("CT", [128, PAIRS, PAIR])
        xsT = sb("xsT", [HALF, 2, SLOTS, B])
        xst = [sb(f"xst{u}", [HALF, 2, EPT, B]) for u in range(2)]
        w1 = [sb(f"w1{u}", [HALF, EPT * 2, SHID]) for u in range(2)]
        w2 = [sb(f"w2{u}", [128, EPT * HCH, D]) for u in range(2)]
        b1, b2 = sb("b1", [128, SLOTS, HCH]), sb("b2", [128, D])
        hrow, hT = sb("hrow", [128, 2, HALF * 4]), sb("hT", [128, HCH, EPT, B])
        yall = sb("yall", [128, SLOTS // EPT, D])
        ys = w2[0][:, 0:PAIRS, :]
        ps = [ctx.enter_context(nc.psum_tensor(f"pss{i}", [128, 512], F32)) for i in range(8)]
        phase = Phase(nc, ctx)
        names = ("h_in phi_in c_in xn_in set_up dve p_sq p_ps p_std phin lt_ps lt_sb ln_ps "
                 "ln_sb d_sub d_exp c_sub c_exp d_nrm dt_ps d_sb c_nrm ct_ps ct_sb xs_ps xs_sb xst h_ps h_sb ht_ps h_pre h_act y_ps y_sb "
                 "y_st ys_in ys_sb f_ps f_sb stored").split()
        q = {n: phase.sem("sl_" + n) for n in names}
        w1_ld, w2_ld = ([phase.sem(f"sl_w{n}{u}") for u in range(2)] for n in (1, 2))
        TURNS = SLOTS // EPT
        CS = 8
        scope = ctx.enter_context(ExitStack())
        block = scope.enter_context(nc.Block())

        def bank(i, rows, cols):
            return ps[i][0:rows, 0:cols]

        @block.sync
        def _(sp):
            sp.dma_start(phi[:], t["phi"]).then_inc(q["phi_in"], 16)
            sp.dma_start(scl[:], t["phi_scale"].partition_broadcast(HALF)).then_inc(q["phi_in"], 16)
            for dst, src in ((own, "own"), (b1, "slot_b1")):
                sp.dma_start(dst[:], t[src]).then_inc(q["c_in"], 16)
            for bb in range(2):
                sp.dma_start(b2[SLOTS * bb:SLOTS * bb + SLOTS, :], t["slot_b2"]).then_inc(q["c_in"], 16)

            sp.dma_start(xn[:], xn_dram.rearrange("(r p) d -> p r d", p=PAIR)).then_inc(q["xn_in"], 16)
            sp.dma_start(h[:], h_dram.rearrange("(r p) d -> p r d", p=PAIR)).then_inc(q["h_in"], 16)

            def load_first(n, u):
                sp.dma_start(w1[u][:], t["slot_w1"][bass.ds(n, EPT)].rearrange("e (c p) n -> p (e c) n", p=HALF)).then_inc(w1_ld[u], 16)

            def load_second(n, u):
                sp.dma_start(w2[u][:], t["slot_w2"][bass.ds(n, EPT)].rearrange("e (c p) n -> p (e c) n", p=128)).then_inc(w2_ld[u], 16)

            def store(j):
                sp.wait_ge(q["y_sb"], j + 1)
                sp.dma_start(y_dram[bass.ds(j * EPT, EPT)].rearrange("e b d -> (e b) d"),
                             yall[:, bass.ds(j, 1), :].rearrange("p j d -> p (j d)")).then_inc(q["y_st"], 16)

            for u in range(2):
                load_first(EPT * u, u)
                load_second(EPT * u, u)
            sp.wait_ge(q["h_ps"], 1)
            load_first(2 * EPT, 0)
            with sp.Fori(0, TURNS // 2 - 2) as i:
                for u in range(2):
                    sp.wait_ge(q["h_ps"], i * 2 + (u + 2))
                    load_first(i * 2 * EPT + EPT * (u + 3), 1 - u)
                    store(i * 2 + u)
                    load_second(i * 2 * EPT + EPT * (u + 2), u)
            sp.wait_ge(q["h_ps"], TURNS - 2)
            load_first((TURNS - 1) * EPT, 1)
            for u in range(2):
                store(TURNS - 4 + u)
                load_second((TURNS - 2 + u) * EPT, u)
            for u in range(2):
                store(TURNS - 2 + u)
            sp.wait_ge(q["y_st"], 16 * TURNS)
            for bb in range(2):
                sp.dma_start(ys[SLOTS * bb:SLOTS * bb + SLOTS, :, :],
                             y_dram.rearrange("n (r b) d -> b n r d", b=2)[bb]).then_inc(q["ys_in"], 16)
            for part in range(2):
                rows = slice(PAIRS // 2 * part, PAIRS // 2 * (part + 1))
                sp.wait_ge(q["f_sb"], 4 * part + 4)
                sp.dma_start(out.rearrange("(r b) s d -> (b s) r d", b=2)[:, rows], h[:, rows, :]).then_inc(q["stored"], 16)
            sp.wait_ge(q["stored"], 2 * 16)

        @block.gpsimd
        def _(pool):
            def stage(j, u):
                nc.gpsimd.tensor_copy(xst[u][:], xsT[:, :, bass.ds(j * EPT, EPT), :]).then_inc(q["xst"], 1)

            pool.wait_ge(q["xs_sb"], 8)
            stage(0, 0)
            stage(1, 1)
            with pool.Fori(0, TURNS // 2 - 1) as i:
                for u in range(2):
                    pool.wait_ge(q["h_ps"], i * 2 + (u + 1))
                    stage(i * 2 + (u + 2), u)

        @block.tensor
        def _(pe):
            pe.wait_ge(q["p_sq"], 1)
            for half in range(2):
                last = nc.tensor.matmul(bank(4, HALF, SLOTS), ones[:], phi2[:, half, :], start=(half == 0), stop=(half == 1))
            last.then_inc(q["p_ps"], 1)
            pe.wait_ge(q["phin"], 1)
            for n in range(3):
                for half in range(2):
                    last = nc.tensor.matmul(bank(5 + n, SLOTS, 512), phi[:, half, :], xT[:, half, 512 * n:512 * n + 512],
                                            start=(half == 0), stop=(half == 1))
                last.then_inc(q["lt_ps"], 1)
            for g in range(2):
                for j in range(8):
                    for half in range(2):
                        r = 8 * g + j
                        last = nc.tensor.matmul(ps[g][0:HALF, SLOTS * j:SLOTS * j + SLOTS],
                                                xT[:, half, PAIR * r:PAIR * r + PAIR], phi[:, half, :],
                                                start=(half == 0), stop=(half == 1))
                last.then_inc(q["ln_ps"], 1)
            pe.wait_ge(q["d_nrm"], 1)
            for g in range(2):
                for j in range(8):
                    r = 8 * g + j
                    last = nc.tensor.transpose(ps[2 + g][0:HALF, SLOTS * j:SLOTS * j + SLOTS],
                                               dT[:, 2 * r:2 * r + 2, :].rearrange("p b m -> p (b m)"), ident[0:SLOTS, 0:SLOTS])
                last.then_inc(q["dt_ps"], 1)
            pe.wait_ge(q["d_sb"], 1)
            pe.wait_ge(q["xn_in"], 16)
            pe.wait_ge(q["ln_sb"], 2)
            for g in range(8):
                half, r = g % 2, g // 2
                for j in range(4):
                    last = nc.tensor.matmul(ps[g][0:HALF, 128 * j:128 * j + 128],
                                            xn[:, 4 * r + j, HALF * half:HALF * half + HALF],
                                            Dp[:, 4 * r + j].rearrange("p b n -> p (b n)"), start=True, stop=True)
                last.then_inc(q["xs_ps"], 1)

            def first(j, n, u):
                pe.wait_ge(w1_ld[u], n * 16 + 16)
                pe.wait_ge(q["xst"], j + 1)
                for c in range(2):
                    for half in range(2):
                        for e in range(EPT):
                            last = nc.tensor.matmul(ps[c][B * e:B * e + B, 0:SHID // 2], xst[u][:, half, e, :],
                                                    w1[u][:, 2 * e + half, SHID // 2 * c:SHID // 2 * (c + 1)],
                                                    start=(half == 0), stop=(half == 1))
                last.then_inc(q["h_ps"], 1)

            def turned(j):
                pe.wait_ge(q["h_sb"], j + 1)
                for c in range(HCH):
                    last = nc.tensor.transpose(ps[2 + c // 3][:, 128 * (c % 3):128 * (c % 3) + 128],
                                               hrow[:, c // 3, 128 * (c % 3):128 * (c % 3) + 128], ident[:])
                last.then_inc(q["ht_ps"], 1)

            def second(j, n, u):
                pe.wait_ge(w2_ld[u], n * 16 + 16)
                pe.wait_ge(q["h_act"], j + 1)
                for c in range(HCH):
                    for e in range(EPT):
                        last = nc.tensor.matmul(ps[4][B * e:B * e + B, 0:D], hT[:, c, e, :], w2[u][:, HCH * e + c, :],
                                                start=(c == 0), stop=(c == HCH - 1))
                last.then_inc(q["y_ps"], 1)

            first(0, 0, 0)
            with pe.Fori(0, TURNS // 2 - 1) as i:
                for u in range(2):
                    turned(i * 2 + u)
                    first(i * 2 + (u + 1), i + u, 1 - u)
                    second(i * 2 + u, i, u)
            N = TURNS // 2 - 1
            turned(TURNS - 2)
            first(TURNS - 1, N, 1)
            second(TURNS - 2, N, 0)
            turned(TURNS - 1)
            second(TURNS - 1, N, 1)
            pe.wait_ge(q["c_nrm"], 1)
            pe.wait_ge(q["y_sb"], TURNS)
            for g in range(4):
                for j in range(4):
                    last = nc.tensor.transpose(ps[4 + g][:, PAIR * j:PAIR * j + PAIR],
                                               Cp[:, 4 * g + j].rearrange("p b n -> p (b n)"), ident[0:HALF, 0:HALF])
                last.then_inc(q["ct_ps"], 1)
            pe.wait_ge(q["ct_sb"], 4)
            for r in range(PAIRS):
                g = r // 2
                if r % 4 == 0:
                    pe.wait_ge(q["ys_sb"], r // 4 + 1)
                if r % 2 == 0 and g >= 4:
                    pe.wait_ge(q["f_sb"], g - 3)
                last = nc.tensor.matmul(ps[g % 4][0:HALF, D * (r % 2):D * (r % 2) + D], CT[:, r, :], ys[:, r, :],
                                        start=True, stop=True)
                if r % 2:
                    last.then_inc(q["f_ps"], 1)

        @block.scalar
        def _(act):
            act.wait_ge(q["set_up"], 1)
            act.wait_ge(q["p_ps"], 1)
            nc.scalar.activation(pn[:, 0, :], bank(4, HALF, SLOTS), ACT.Sqrt).then_inc(q["p_std"], 1)
            flat = dT[:].rearrange("p b m -> p (b m)")
            for n in range(3):
                act.wait_ge(q["lt_ps"], n + 1)
                nc.scalar.activation(flat[:, 512 * n:512 * n + 512], bank(5 + n, SLOTS, 512), ACT.Copy).then_inc(q["lt_sb"], 1)
            for g in range(2):
                act.wait_ge(q["ln_ps"], g + 1)
                nc.scalar.activation(C[:, 8 * g:8 * g + 8, :], bank(g, HALF, 512).rearrange("p (r n) -> p r n", r=8),
                                     ACT.Copy).then_inc(q["ln_sb"], 1)
            act.wait_ge(q["d_sub"], 1)
            nc.scalar.activation(dT[:], dT[:], ACT.Exp).then_inc(q["d_exp"], 1)
            act.wait_ge(q["c_sub"], 1)
            nc.scalar.activation(C[:], C[:], ACT.Exp).then_inc(q["c_exp"], 1)
            for g in range(8):
                half, r = g % 2, g // 2
                act.wait_ge(q["xs_ps"], g + 1)
                nc.scalar.activation(xsT[:, half].rearrange("p n b -> p b n")[:, CS * r:CS * r + CS, :],
                                     bank(g, HALF, 512).rearrange("p (b n) -> p b n", b=CS), ACT.Copy).then_inc(q["xs_sb"], 1)
            with act.Fori(0, TURNS) as j:
                act.wait_ge(q["h_pre"], j + 1)
                nc.scalar.activation(hT[:], hT[:], ACT.Gelu).then_inc(q["h_act"], 1)
            for g in range(4):
                act.wait_ge(q["ct_ps"], g + 1)
                nc.scalar.activation(CT[:, 4 * g:4 * g + 4, :], bank(4 + g, 128, 384).rearrange("p (r m) -> p r m", r=4),
                                     ACT.Copy).then_inc(q["ct_sb"], 1)

        @block.vector
        def _(v):
            op = nc.vector
            ch = Steps(v, q["dve"])
            ch.mark(op.memset(ones[:], 1.0))
            ch.wait()
            op.memset(cred[:, 0, 0:1], 0.0).then_inc(q["set_up"], 1)
            v.wait_ge(q["phi_in"], 2 * 16)
            op.tensor_tensor(phi2[:], phi[:], phi[:], ALU.mult).then_inc(q["p_sq"], 1)
            v.wait_ge(q["p_std"], 1)
            ch.then(op.tensor_scalar(pn[:, 0, :], pn[:, 0, :], 1e-12, None, ALU.max))
            ch.then(op.reciprocal(pn[:, 1, :], pn[:, 0, :]))
            op.scalar_tensor_tensor(out=phi[:], in0=phi[:], scalar=scl[:, 0:1],
                                    in1=pn[:, 1, :].unsqueeze(1).to_broadcast([HALF, 2, SLOTS]), op0=ALU.mult,
                                    op1=ALU.mult).then_inc(q["phin"], 1)
            v.wait_ge(q["c_in"], 4 * 16)
            v.wait_ge(q["lt_sb"], 3)
            ch.then(op.tensor_reduce(dred[:, 0], dT[:], X, ALU.max))
            op.tensor_tensor(dT[:], dT[:], spread(dred[:, 0], SEQ), ALU.subtract).then_inc(q["d_sub"], 1)
            v.wait_ge(q["ln_sb"], 2)
            ch.then(op.tensor_reduce(cred[:, 0], C[:], X, ALU.max))
            op.tensor_tensor(C[:], C[:], spread(cred[:, 0], SLOTS), ALU.subtract).then_inc(q["c_sub"], 1)
            v.wait_ge(q["d_exp"], 1)
            ch.then(op.tensor_reduce(dred[:, 0], dT[:], X, ALU.add))
            ch.then(op.reciprocal(dred[:, 1], dred[:, 0]))
            op.tensor_tensor(dT[:], dT[:], spread(dred[:, 1], SEQ), ALU.mult).then_inc(q["d_nrm"], 1)
            v.wait_ge(q["dt_ps"], 2)
            for g in range(2):
                for bb in range(2):
                    ch.mark(op.tensor_scalar(Dp[:, 8 * g:8 * g + 8, bb, :],
                                             bank(2 + g, HALF, 512).rearrange("p (r n) -> p r n", r=8),
                                             own[:, bb:bb + 1], None, ALU.mult))
            ch.wait()
            op.memset(dred[:, 0, 0:1], 0.0).then_inc(q["d_sb"], 1)
            v.wait_ge(q["c_exp"], 1)
            ch.then(op.tensor_reduce(cred[:, 0], C[:], X, ALU.add))
            ch.then(op.reciprocal(cred[:, 1], cred[:, 0]))
            ch.then(op.tensor_tensor(C[:], C[:], spread(cred[:, 1], SLOTS), ALU.mult))
            for bb in range(2):
                last = op.tensor_scalar(Cp[:, :, bb, :], C[:], own[:, bb:bb + 1], None, ALU.mult)
                ch.mark(last)
            ch.wait()
            op.memset(cred[:, 0, 0:1], 0.0).then_inc(q["c_nrm"], 1)
            def hidden(j):
                v.wait_ge(q["h_ps"], j + 1)
                for c in range(2):
                    last = op.tensor_copy(hrow[:, c, :], ps[c][:, 0:SHID // 2])
                last.then_inc(q["h_sb"], 1)

            def bias(j):
                v.wait_ge(q["ht_ps"], j + 1)
                b = b1[:, bass.ds(j * EPT, EPT), :].rearrange("p e c -> p c e")
                for c in range(2):
                    last = op.tensor_tensor(hT[:, 3 * c:3 * c + 3], ps[2 + c][:, 0:3 * 128].rearrange("p (c e b) -> p c e b", c=3, e=EPT),
                                            spread(b[:, 3 * c:3 * c + 3], B), ALU.add)
                last.then_inc(q["h_pre"], 1)

            def result(j):
                v.wait_ge(q["y_ps"], j + 1)
                op.tensor_copy(yall[:, bass.ds(j, 1), :].rearrange("p j d -> p (j d)"), ps[4][:, 0:D]).then_inc(q["y_sb"], 1)

            hidden(0)
            with v.Fori(0, TURNS - 1) as j:
                bias(j)
                hidden(j + 1)
                result(j)
            bias(TURNS - 1)
            result(TURNS - 1)
            v.wait_ge(q["ys_in"], 2 * 16)
            for g in range(4):
                part = ys[:, 4 * g:4 * g + 4, :]
                op.tensor_tensor(part, part, b2[:].unsqueeze(1).to_broadcast([128, 4, D]), ALU.add).then_inc(q["ys_sb"], 1)
            v.wait_ge(q["h_in"], 16)
            for g in range(8):
                v.wait_ge(q["f_ps"], g + 1)
                hh = h[:, 2 * g:2 * g + 2, :]
                op.tensor_tensor(hh, hh, bank(g % 4, HALF, 2 * D).rearrange("p (r d) -> p r d", r=2),
                                 ALU.add).then_inc(q["f_sb"], 1)
        scope.close()
        phase.clear()


def build(nc, t):
    def dram(name, *shape):
        return nc.dram_tensor(name, shape, F32).ap()

    h_tok, m_dram, xn_dram = dram("h_tok", B, SEQ, D), dram("m_dram", 128, GH, HD, HD), dram("xn_dram", TOK, D)
    x_slots, f_slots = dram("x_slots", BLOCKS * SLOT, D), dram("f_slots", BLOCKS * SLOT, RANK)
    g_slots, r_slots = dram("g_slots", BLOCKS * SLOT, RANK), dram("r_slots", BLOCKS * SLOT, D)
    h_tok2, h_tok3, unit_dram = (dram(n, TOK, D) for n in ("h_tok2", "h_tok3", "unit_dram"))
    y_dram = dram("y_dram", SLOTS, B, D)
    with ExitStack() as ctx:
        gathered = [ctx.enter_context(nc.semaphore(f"gathered{g}")) for g in range(2)]
        scat = [ctx.enter_context(nc.semaphore(f"scattered{bank}")) for bank in range(2)]
        gath = [[ctx.enter_context(nc.semaphore(f"routed_in{bank}_{g}")) for g in range(4)] for bank in range(2)]
        embed(nc, t, h_tok, gathered)

        def hold(scope, *tensors):
            for name, shape, dt in tensors:
                keep[name] = scope.enter_context(nc.sbuf_tensor("keep_" + name, shape, dt))

        keep = {}
        hold(ctx, ("h", [HALF, PAIRS, D], F32), ("ident", [128, 128], F32), ("xT", [HALF, 2, TOK], F32))
        with ExitStack() as outer:
            hold(outer, ("oT", [HALF, 2, TOK], F32))
            with ExitStack() as scope:
                hold(scope, ("qkT", [HALF, 4, TOK], F32), ("fac", [128, 2 * GH * HD, SEQ], F32), ("v_all", [SEQ, B, D], F32),
                     ("Mbd", [HALF, 2, B, HALF], F32), ("kn4", [128, TOK], F32), ("qn4", [128, TOK], F32),
                     ("qn4c", [128, B * RCH], F32))
                prepare(nc, t, keep, h_tok, m_dram)
                attend(nc, t, keep, m_dram, x_slots, g_slots)
            with ExitStack() as scope:
                hold(scope, ("pos", [128, 2 * FT, TOPK], I32), ("w4", [128, 2 * FT, TOPK], F32), ("eid", [1, 2 * BLOCKS], I32),
                     ("rows_in", [128, FT, D], F32))
                route(nc, t, keep, xn_dram, h_tok2, x_slots, scat[0])
                hf = scope.enter_context(nc.sbuf_tensor("hf", [128, FT, RANK], F32))
                h3 = scope.enter_context(nc.sbuf_tensor("h3", [128, FT, D], F32))
                routed(nc, t, keep, scat, gath, x_slots, f_slots, g_slots, r_slots, h_tok2, h_tok3, unit_dram, hf, h3)
        slots(nc, t, keep, h_tok3, unit_dram, y_dram, t["out"])


def lay_out(a):
    x = a["x"].reshape(B, 3, 8, 8, 4, 2, 8)
    w1 = a["L0_tok_W1"].reshape(5, 3, 2, 8, 2, 8, HID)
    gb = np.stack([a["L0_tok_gamma"], a["L0_tok_beta"]], -1).reshape(5, 3, 2, 8, 2, 8, 2)

    def features(w):
        w = np.concatenate([w[:3], w[3:, :, :, :, ::-1]])
        return w.transpose(4, 3, 5, 0, 1, 2, 6).reshape(128, KCH, -1)

    out = {
        "x_quads": x.transpose(5, 3, 6, 2, 4, 1, 0).reshape(128, 8, 4, 3, B),
        "W1": features(w1),
        "gb": features(gb),
        "gsel": (np.arange(128)[:, None] % 32 == np.arange(2)).astype(np.float32),
        "b1": a["L0_tok_b1"].reshape(3, 128).T,
        "W2": a["L0_tok_W2"].reshape(3, 128, D).transpose(1, 0, 2),
        "b2": a["L0_tok_b2"],
        "text_ids": a["x_txt"].reshape(8, 128).T,
        "basin": a["L0_txt_basin_coords"],
        "txt_projT": a["L0_txt_proj_w"].T,
        "txt_norm": a["L0_txt_norm_w"],
    }
    qk = a["L0_attn_qkv_w"][:2 * D].reshape(2, GROUPS, GH * HD, 2, HALF)
    qkb = a["L0_attn_qkv_b"][:2 * D].reshape(2, GROUPS, GH * HD)
    out |= {
        "ident": np.eye(128, dtype=np.float32),
        "wqk": a["L0_attn_qkv_w"][:2 * D].T.reshape(2, HALF, 2 * D).transpose(1, 0, 2),
        "bqk": a["L0_attn_qkv_b"][:2 * D].reshape(4, HALF).T,
        "wqk_groups": qk.transpose(4, 3, 1, 0, 2).reshape(HALF, 2, GROUPS, HALF),
        "bqk_groups": np.repeat(qkb.transpose(1, 0, 2).reshape(GROUPS, HALF), B, axis=0),
    }
    d96, d128 = np.arange(HALF), np.arange(128)
    row, head = d128 % 64 // HEADS_2, d128 % 64 % HEADS_2
    used = d128 % 64 < SEQ
    conv = a["L0_attn_conv_w"].reshape(HEADS, 3, 2, HEADS_2)
    mix = np.zeros((128, 3, 8, HEADS), np.float32)
    for p in d128[used]:
        mix[p, :, row[p], :] = conv[:, :, p // 64, head[p]].T
    bn = [a["L0_attn_" + n] for n in ("conv_b", "bn_mean", "bn_gamma", "bn_beta", "bn_var")]
    out |= {
        "headsum": ((d96[:, None] // HD == np.arange(64) % HEADS_2) & (np.arange(64) < SEQ)).astype(np.float32),
        "rowmask": ((row[:, None] == np.arange(8)) & used[:, None]).astype(np.float32),
        "mask6": (d96[:, None] // HD == np.arange(HEADS_2)).astype(np.float32),
        "wv": a["L0_attn_qkv_w"][2 * D:].T.reshape(2, HALF, D).transpose(1, 0, 2),
        "bv": a["L0_attn_qkv_b"][2 * D:].reshape(2, HALF).T,
        "parity": np.tile(np.arange(D) // HD % 2 == np.arange(2)[:, None], (SEQ, 1, 1)).astype(np.float32),
        "mix": mix.reshape(128, 3, HALF),
        "bncol": np.tile(np.stack(bn, -1), (8, 1)),
        "bnrow": np.tile(np.stack([a["L0_attn_bn_gamma"], a["L0_attn_bn_var"]]), (1, 8)),
        "attn_projT": a["L0_attn_proj_w"].T.reshape(2, HALF, D).transpose(1, 0, 2),
        "attn_projb": a["L0_attn_proj_b"],
        "Wf": np.concatenate([a["L0_ffn_W_fk"], a["L0_ffn_W_rk"]], 1).reshape(2, HALF, 128).transpose(1, 0, 2),
        "bf": np.concatenate([a["L0_ffn_b_fk"], a["L0_ffn_b_rk"]]).reshape(128, 1),
        "emb": np.stack([a["L0_ffn_emb_fk"], a["L0_ffn_emb_rk"]], 1),
        "upper": np.triu(np.ones((128, 128), np.float32), 1),
        "iota": np.tile(np.arange(BLOCKS, dtype=np.float32), (128, 1)),
        "own": (np.arange(HALF)[:, None] // SEQ == np.arange(2)).astype(np.float32),
        "second_projb": a["L1_attn_proj_b"],
        "phi": a["L1_ffn_phi"].reshape(2, HALF, SLOTS).transpose(1, 0, 2),
        "phi_scale": a["L1_ffn_scale"],
        "slot_w1": a["L1_ffn_w1"],
        "slot_w2": a["L1_ffn_w2"],
        "slot_b1": a["L1_ffn_b1"].reshape(SLOTS, HCH, 128).transpose(2, 0, 1),
        "slot_b2": a["L1_ffn_b2"],
        "f_know": a["L0_ffn_f_know"],
        "r_know": a["L0_ffn_r_know"],
        "scales": np.stack([a["L0_attn_scale"], a["L0_attn_riem_scale"], a["L0_attn_grass_scale"]]),
    }
    return {n: np.ascontiguousarray(v) for n, v in out.items()}


def kernel(**inputs):
    import concourse.bacc as bacc
    from concourse.bass_utils import run_bass_kernel_spmd

    nc = bacc.Bacc("TRN2", target_bir_lowering=False, num_devices=1)
    arrays = {"in_" + n: v for n, v in lay_out({n: np.asarray(v) for n, v in inputs.items()}).items()}
    t = {n[3:]: nc.dram_tensor(n, v.shape, mybir.dt.from_np(v.dtype), kind="ExternalInput").ap()
         for n, v in arrays.items()}
    t["out"] = nc.dram_tensor("out_h", (B, SEQ, D), F32, kind="ExternalOutput").ap()
    build(nc, t)
    done = run_bass_kernel_spmd(nc, [arrays], core_ids=[0])
    return done.results[0]["out_h"]
```
